# Optimizing a Trainium2 kernel written in Bass

```python
import numpy as np
import jax
import jax.numpy as jnp

def _softmax(x, axis=-1):
    return jax.nn.softmax(x, axis=axis)

def _gelu(x):
    return jax.nn.gelu(x, approximate=True)

def _silu(x):
    return jax.nn.silu(x)

def _sigmoid(x):
    return jax.nn.sigmoid(x)

def _layernorm(x, axis=-1, eps=1e-05):
    m = jnp.mean(x, axis=axis, keepdims=True)
    v = jnp.var(x, axis=axis, keepdims=True)
    return (x - m) / jnp.sqrt(v + eps)

def _scatter_add(tgt, idx, src, axis=0):
    return tgt.at[idx].add(src)

def _segment_sum(src, seg, n):
    return jax.ops.segment_sum(src, seg, n)
kernel_name = 'mk_decoder_preln_d2_seqx_r4_9f9ef9'

def setup_inputs(seed: int=0):
    np.random.seed(seed)
    _w = jnp.asarray

    def _rec_inputs():
        import jax
        import jax.numpy as jnp
        _rk = jax.random.key(seed)
        x = -0.0002928 + 1 * jax.random.normal(jax.random.fold_in(_rk, 1), (16, 128, 256), jnp.float32)
        _lenS = 128 - jax.random.randint(jax.random.fold_in(_rk, 7), (16,), 0, max(1, 128 // 4) + 1, jnp.int32)
        _lenS2 = 128 - jax.random.randint(jax.random.fold_in(_rk, 8), (16,), 0, max(1, 128 // 4) + 1, jnp.int32)
        _ctx_768P = jax.random.normal(jax.random.fold_in(_rk, 11), (16, 16, 192), jnp.float32)
        _ctx_768c = jax.random.dirichlet(jax.random.fold_in(_rk, 511), 0.3 * jnp.ones((16,), jnp.float32), (16, 128))
        _ctx_768t = jnp.einsum('bsk,bkd->bsd', _ctx_768c, _ctx_768P)
        _ctx_768t = _ctx_768t * jax.lax.rsqrt(jnp.mean(jnp.square(_ctx_768t)) + 1e-12) * 0.953939
        ctx_768 = 2.09791e-05 + 1.00001 * (_ctx_768t + 0.3 * jax.random.normal(jax.random.fold_in(_rk, 611), (16, 128, 192), jnp.float32))
        _validS = jnp.arange(128)[None, :] < _lenS[:, None]
        _validS2 = jnp.arange(128)[None, :] < _lenS2[:, None]
        _causal = jnp.tril(jnp.ones((128, 128), dtype=bool))
        mask_BxS2_bk0 = jnp.logical_not(jnp.broadcast_to(_validS2[:, :], (16, 128)))
        return (x, ctx_768, mask_BxS2_bk0)
    x, ctx_768, mask_BxS2_bk0 = _rec_inputs()

    def _L0_attn_setup():
        import jax, jax.numpy as jnp
        import numpy as np
        EPS = 1e-05

        def layer_norm(x, gamma, beta):
            mu = jnp.mean(x, axis=-1, keepdims=True)
            var = jnp.var(x, axis=-1, keepdims=True)
            return (x - mu) * jax.lax.rsqrt(var + EPS) * gamma + beta
        key = jax.random.key(seed)
        ks = jax.random.split(key, 8)
        T, B, E, H, K = (512, 2, 256, 16, 64)
        x = jax.random.normal(ks[0], (T, B, E), dtype=jnp.float32)
        attn_mask = jnp.where(jnp.tril(jnp.ones((T, T), dtype=bool)), 0.0, -1000000000.0).astype(jnp.float32)

        def xavier(k, shape, gain):
            fan_out, fan_in = shape
            std = gain * np.sqrt(2.0 / (fan_in + fan_out))
            return jax.random.normal(k, shape, dtype=jnp.float32) * std
        Wq = xavier(ks[1], (H * K, E), 1.0)
        Wk = xavier(ks[2], (K, E), 1.0)
        Wv = xavier(ks[3], (E, E), 1.0)
        return {'x': x, 'attn_mask': attn_mask, 'Wq': Wq, 'bq': jnp.zeros((H * K,), jnp.float32), 'Wk': Wk, 'bk': jnp.zeros((K,), jnp.float32), 'Wv': Wv, 'bv': jnp.zeros((E,), jnp.float32), 'k_gamma': jnp.ones((K,), jnp.float32), 'k_beta': jnp.zeros((K,), jnp.float32), 'v_gamma': jnp.ones((E,), jnp.float32), 'v_beta': jnp.zeros((E,), jnp.float32)}
    _L0_attn_all = _L0_attn_setup()
    _L0_attn_in = {k: v for k, v in _L0_attn_all.items() if k in ('attn_mask', 'Wq', 'bq', 'Wk', 'bk', 'Wv', 'bv', 'k_gamma', 'k_beta', 'v_gamma', 'v_beta')}
    del _L0_attn_all

    def _L0_xattn_setup():
        import jax, jax.numpy as jnp
        import numpy as np
        N_HEADS = 16
        D_EMBED = 256
        N_CROSS = 192
        D_HEAD = D_EMBED // N_HEADS
        key = jax.random.key(seed)
        ks = jax.random.split(key, 10)
        B, S = (2, 512)
        x = jax.random.normal(ks[0], (B, S, D_EMBED), dtype=jnp.float32)
        context = jax.random.normal(ks[1], (B, S, N_CROSS), dtype=jnp.float32)
        sq = 1.0 / np.sqrt(D_EMBED)
        sc = 1.0 / np.sqrt(N_CROSS)
        Wq = jax.random.normal(ks[2], (D_EMBED, D_EMBED), dtype=jnp.float32) * sq
        bq = jnp.zeros((D_EMBED,), dtype=jnp.float32)
        Wk = jax.random.normal(ks[3], (N_CROSS, D_EMBED), dtype=jnp.float32) * sc
        bk = jnp.zeros((D_EMBED,), dtype=jnp.float32)
        Wv = jax.random.normal(ks[4], (N_CROSS, D_EMBED), dtype=jnp.float32) * sc
        bv = jnp.zeros((D_EMBED,), dtype=jnp.float32)
        Wo = jax.random.normal(ks[5], (D_EMBED, D_EMBED), dtype=jnp.float32) * sq
        bo = jnp.zeros((D_EMBED,), dtype=jnp.float32)
        return {'x': x, 'context': context, 'Wq': Wq, 'bq': bq, 'Wk': Wk, 'bk': bk, 'Wv': Wv, 'bv': bv, 'Wo': Wo, 'bo': bo}
    _L0_xattn_all = _L0_xattn_setup()
    _L0_xattn_in = {k: v for k, v in _L0_xattn_all.items() if k in ('Wq', 'bq', 'Wk', 'bk', 'Wv', 'bv', 'Wo', 'bo')}
    del _L0_xattn_all

    def _L0_ffn_setup():
        import jax, jax.numpy as jnp
        import numpy as np
        B, S, D, H, E = (4, 512, 256, 1024, 8)
        key = jax.random.key(seed)
        ks = jax.random.split(key, 8)
        s_d = 1.0 / np.sqrt(D)
        s_h = 1.0 / np.sqrt(H)
        return {'x': jax.random.normal(ks[0], (B, S, D), dtype=jnp.float32), 'gate_w': jax.random.uniform(ks[1], (E, D), jnp.float32, -s_d, s_d), 'gate_b': jax.random.uniform(ks[2], (E,), jnp.float32, -s_d, s_d), 'w1': jax.random.uniform(ks[3], (E, H, D), jnp.float32, -s_d, s_d), 'b1': jax.random.uniform(ks[4], (E, H), jnp.float32, -s_d, s_d), 'w2': jax.random.uniform(ks[5], (E, D, H), jnp.float32, -s_h, s_h), 'b2': jax.random.uniform(ks[6], (E, D), jnp.float32, -s_h, s_h)}
    _L0_ffn_all = _L0_ffn_setup()
    _L0_ffn_in = {k: v for k, v in _L0_ffn_all.items() if k in ('gate_w', 'gate_b', 'w1', 'b1', 'w2', 'b2')}
    del _L0_ffn_all

    def _L1_attn_setup():
        import jax, jax.numpy as jnp
        import numpy as np
        B, N, D = (2, 512, 256)
        H = 16
        DH = D // H
        WINDOW = 64
        SCALE = 1.0 / np.sqrt(DH).astype(np.float32)

        def _causal_window_mask(n: int) -> jnp.ndarray:
            pos = jnp.arange(n)
            diff = pos[:, None] - pos[None, :]
            return (diff >= 0) & (diff < WINDOW)
        key = jax.random.key(seed)
        k1, k2, k3 = jax.random.split(key, 3)
        lim_qkv = np.sqrt(6.0 / (D + 3 * D)).astype(np.float32)
        lim_out = np.sqrt(6.0 / (D + D)).astype(np.float32)
        x = jax.random.normal(k1, (B, N, D), dtype=jnp.float32)
        Wqkv = jax.random.uniform(k2, (3 * D, D), dtype=jnp.float32, minval=-lim_qkv, maxval=lim_qkv)
        bqkv = jnp.zeros((3 * D,), dtype=jnp.float32)
        Wout = jax.random.uniform(k3, (D, D), dtype=jnp.float32, minval=-lim_out, maxval=lim_out)
        bout = jnp.zeros((D,), dtype=jnp.float32)
        return {'x': x, 'Wqkv': Wqkv, 'bqkv': bqkv, 'Wout': Wout, 'bout': bout}
    _L1_attn_all = _L1_attn_setup()
    _L1_attn_in = {k: v for k, v in _L1_attn_all.items() if k in ('Wqkv', 'bqkv', 'Wout', 'bout')}
    del _L1_attn_all

    def _L1_xattn_setup():
        import jax, jax.numpy as jnp
        import numpy as np
        DIM_IN, DIM_LAT, DIM_HEAD = (192, 256, 64)
        INNER = max(DIM_LAT, DIM_IN)
        HEADS = INNER // DIM_HEAD
        SCALE = DIM_HEAD ** (-0.5)
        RMS_EPS = 1e-08
        LN_EPS = 1e-05

        def layernorm(x, g, b):
            mu = jnp.mean(x, axis=-1, keepdims=True)
            var = jnp.mean((x - mu) ** 2, axis=-1, keepdims=True)
            return (x - mu) * jax.lax.rsqrt(var + LN_EPS) * g + b

        def rmsnorm(x, gamma):
            norm = jnp.sqrt(jnp.sum(x * x, axis=-1, keepdims=True)) * x.shape[-1] ** (-0.5)
            return x / jnp.maximum(norm, RMS_EPS) * gamma
        key = jax.random.key(seed)
        ks = jax.random.split(key, 12)
        b, n, m = (4, 1024, 128)
        x = jax.random.normal(ks[0], (b, n, DIM_IN), jnp.float32)
        latents = jax.random.normal(ks[1], (b, m, DIM_LAT), jnp.float32)
        mask = jax.random.randint(ks[2], (b, n), 0, 2).astype(bool)
        s = lambda k, sh, fan: jax.random.normal(k, sh, jnp.float32) * fan ** (-0.5)
        return {'x': x, 'latents': latents, 'mask': mask, 'ln_x_g': jnp.ones((DIM_IN,), jnp.float32), 'ln_x_b': jnp.zeros((DIM_IN,), jnp.float32), 'ln_l_g': jnp.ones((DIM_LAT,), jnp.float32), 'ln_l_b': jnp.zeros((DIM_LAT,), jnp.float32), 'qn_g': jnp.ones((DIM_HEAD,), jnp.float32), 'kn_g': jnp.ones((DIM_HEAD,), jnp.float32), 'Wq': s(ks[3], (INNER, DIM_LAT), DIM_LAT), 'Wkv': s(ks[4], (2 * INNER, DIM_IN), DIM_IN), 'Wlkv': s(ks[5], (2 * INNER, DIM_LAT), DIM_LAT), 'Wo': s(ks[6], (DIM_LAT, INNER), INNER), 'bo': jnp.zeros((DIM_LAT,), jnp.float32)}
    _L1_xattn_all = _L1_xattn_setup()
    _L1_xattn_in = {k: v for k, v in _L1_xattn_all.items() if k in ('ln_x_g', 'ln_x_b', 'ln_l_g', 'ln_l_b', 'qn_g', 'kn_g', 'Wq', 'Wkv', 'Wlkv', 'Wo', 'bo')}
    del _L1_xattn_all

    def _L1_ffn_setup():
        import jax, jax.numpy as jnp
        import numpy as np
        B, S, D, H, E = (64, 256, 256, 64, 8)
        EPS = 1e-05
        key = jax.random.key(seed)
        ks = jax.random.split(key, 8)
        x = jax.random.normal(ks[0], (B, S, D), jnp.float32)
        return {'x': x, 'ln_g': jnp.ones((D,), jnp.float32), 'ln_b': jnp.zeros((D,), jnp.float32), 'bn_g': jnp.ones((D,), jnp.float32), 'bn_b': jnp.zeros((D,), jnp.float32), 'bn_mean': jax.random.normal(ks[1], (D,), jnp.float32) * 0.01, 'bn_var': jnp.ones((D,), jnp.float32), 'Wr': jax.random.normal(ks[2], (D, E), jnp.float32) * 0.02, 'br': jnp.zeros((E,), jnp.float32), 'W_down': jax.random.normal(ks[3], (E, D, H), jnp.float32) * 0.02, 'b_down': jnp.zeros((E, H), jnp.float32), 'W_up': jax.random.normal(ks[4], (E, H, D), jnp.float32) * 0.02, 'b_up': jnp.zeros((E, D), jnp.float32)}
    _L1_ffn_all = _L1_ffn_setup()
    _L1_ffn_in = {k: v for k, v in _L1_ffn_all.items() if k in ('ln_g', 'ln_b', 'bn_g', 'bn_b', 'bn_mean', 'bn_var', 'Wr', 'br', 'W_down', 'b_down', 'W_up', 'b_up')}
    del _L1_ffn_all
    return {'x': x, 'ctx_768': ctx_768, 'mask_BxS2_bk0': mask_BxS2_bk0, 'L0_attn_attn_mask': _L0_attn_in['attn_mask'], 'L0_attn_Wq': _L0_attn_in['Wq'], 'L0_attn_bq': _L0_attn_in['bq'], 'L0_attn_Wk': _L0_attn_in['Wk'], 'L0_attn_bk': _L0_attn_in['bk'], 'L0_attn_Wv': _L0_attn_in['Wv'], 'L0_attn_bv': _L0_attn_in['bv'], 'L0_attn_k_gamma': _L0_attn_in['k_gamma'], 'L0_attn_k_beta': _L0_attn_in['k_beta'], 'L0_attn_v_gamma': _L0_attn_in['v_gamma'], 'L0_attn_v_beta': _L0_attn_in['v_beta'], 'L0_xattn_Wq': _L0_xattn_in['Wq'], 'L0_xattn_bq': _L0_xattn_in['bq'], 'L0_xattn_Wk': _L0_xattn_in['Wk'], 'L0_xattn_bk': _L0_xattn_in['bk'], 'L0_xattn_Wv': _L0_xattn_in['Wv'], 'L0_xattn_bv': _L0_xattn_in['bv'], 'L0_xattn_Wo': _L0_xattn_in['Wo'], 'L0_xattn_bo': _L0_xattn_in['bo'], 'L0_ffn_gate_w': _L0_ffn_in['gate_w'], 'L0_ffn_gate_b': _L0_ffn_in['gate_b'], 'L0_ffn_w1': _L0_ffn_in['w1'], 'L0_ffn_b1': _L0_ffn_in['b1'], 'L0_ffn_w2': _L0_ffn_in['w2'], 'L0_ffn_b2': _L0_ffn_in['b2'], 'L1_attn_Wqkv': _L1_attn_in['Wqkv'], 'L1_attn_bqkv': _L1_attn_in['bqkv'], 'L1_attn_Wout': _L1_attn_in['Wout'], 'L1_attn_bout': _L1_attn_in['bout'], 'L1_xattn_ln_x_g': _L1_xattn_in['ln_x_g'], 'L1_xattn_ln_x_b': _L1_xattn_in['ln_x_b'], 'L1_xattn_ln_l_g': _L1_xattn_in['ln_l_g'], 'L1_xattn_ln_l_b': _L1_xattn_in['ln_l_b'], 'L1_xattn_qn_g': _L1_xattn_in['qn_g'], 'L1_xattn_kn_g': _L1_xattn_in['kn_g'], 'L1_xattn_Wq': _L1_xattn_in['Wq'], 'L1_xattn_Wkv': _L1_xattn_in['Wkv'], 'L1_xattn_Wlkv': _L1_xattn_in['Wlkv'], 'L1_xattn_Wo': _L1_xattn_in['Wo'], 'L1_xattn_bo': _L1_xattn_in['bo'], 'L1_ffn_ln_g': _L1_ffn_in['ln_g'], 'L1_ffn_ln_b': _L1_ffn_in['ln_b'], 'L1_ffn_bn_g': _L1_ffn_in['bn_g'], 'L1_ffn_bn_b': _L1_ffn_in['bn_b'], 'L1_ffn_bn_mean': _L1_ffn_in['bn_mean'], 'L1_ffn_bn_var': _L1_ffn_in['bn_var'], 'L1_ffn_Wr': _L1_ffn_in['Wr'], 'L1_ffn_br': _L1_ffn_in['br'], 'L1_ffn_W_down': _L1_ffn_in['W_down'], 'L1_ffn_b_down': _L1_ffn_in['b_down'], 'L1_ffn_W_up': _L1_ffn_in['W_up'], 'L1_ffn_b_up': _L1_ffn_in['b_up']}

def reference(x, ctx_768, mask_BxS2_bk0, L0_attn_attn_mask, L0_attn_Wq, L0_attn_bq, L0_attn_Wk, L0_attn_bk, L0_attn_Wv, L0_attn_bv, L0_attn_k_gamma, L0_attn_k_beta, L0_attn_v_gamma, L0_attn_v_beta, L0_xattn_Wq, L0_xattn_bq, L0_xattn_Wk, L0_xattn_bk, L0_xattn_Wv, L0_xattn_bv, L0_xattn_Wo, L0_xattn_bo, L0_ffn_gate_w, L0_ffn_gate_b, L0_ffn_w1, L0_ffn_b1, L0_ffn_w2, L0_ffn_b2, L1_attn_Wqkv, L1_attn_bqkv, L1_attn_Wout, L1_attn_bout, L1_xattn_ln_x_g, L1_xattn_ln_x_b, L1_xattn_ln_l_g, L1_xattn_ln_l_b, L1_xattn_qn_g, L1_xattn_kn_g, L1_xattn_Wq, L1_xattn_Wkv, L1_xattn_Wlkv, L1_xattn_Wo, L1_xattn_bo, L1_ffn_ln_g, L1_ffn_ln_b, L1_ffn_bn_g, L1_ffn_bn_b, L1_ffn_bn_mean, L1_ffn_bn_var, L1_ffn_Wr, L1_ffn_br, L1_ffn_W_down, L1_ffn_b_down, L1_ffn_W_up, L1_ffn_b_up):
    import jax
    import jax.numpy as jnp

    def _L0_attn_ref(x, attn_mask, Wq, bq, Wk, bk, Wv, bv, k_gamma, k_beta, v_gamma, v_beta):
        import jax, jax.numpy as jnp
        import numpy as np
        EPS = 1e-05

        def layer_norm(x, gamma, beta):
            mu = jnp.mean(x, axis=-1, keepdims=True)
            var = jnp.var(x, axis=-1, keepdims=True)
            return (x - mu) * jax.lax.rsqrt(var + EPS) * gamma + beta
        T, B, E = x.shape
        K = Wk.shape[0]
        H = Wq.shape[0] // K
        q = (x @ Wq.T + bq).reshape(T, B, H, K)
        k = layer_norm(x @ Wk.T + bk, k_gamma, k_beta)
        v = layer_norm(x @ Wv.T + bv, v_gamma, v_beta)
        outer = jnp.einsum('tbk,tbd->tbkd', k, v)
        s = jnp.cumsum(outer, axis=0)
        scaling = jax.lax.rsqrt(jnp.arange(1, T + 1, dtype=x.dtype))
        s = s * scaling[:, None, None, None]
        qn = jnp.mean(jax.nn.softmax(q, axis=-1), axis=2)
        attn = jnp.einsum('tbk,tbkd->tbd', qn, s)
        return attn

    def _L0_xattn_ref(x, context, Wq, bq, Wk, bk, Wv, bv, Wo, bo):
        import jax, jax.numpy as jnp
        import numpy as np
        N_HEADS = 16
        D_EMBED = 256
        N_CROSS = 192
        D_HEAD = D_EMBED // N_HEADS
        B, S, _ = x.shape

        def split_heads(t):
            return t.reshape(B, S, N_HEADS, D_HEAD).transpose(0, 2, 1, 3)
        q = split_heads(x @ Wq + bq)
        k = split_heads(context @ Wk + bk)
        v = split_heads(context @ Wv + bv)
        scale = 1.0 / np.sqrt(D_HEAD)
        scores = jnp.einsum('bhqd,bhkd->bhqk', q, k) * scale
        attn = jax.nn.softmax(scores, axis=-1)
        out = jnp.einsum('bhqk,bhkd->bhqd', attn, v)
        out = out.transpose(0, 2, 1, 3).reshape(B, S, D_EMBED)
        return out @ Wo + bo

    def _L0_ffn_ref(x, gate_w, gate_b, w1, b1, w2, b2):
        import jax, jax.numpy as jnp
        import numpy as np
        B, S, D, H, E = (4, 512, 256, 1024, 8)
        b, s, d = x.shape
        xf = x.reshape(-1, d)
        logits = xf @ gate_w.T + gate_b
        top1 = jnp.argmax(logits, axis=-1)
        out = jnp.zeros_like(xf)
        n_experts = w1.shape[0]
        for e in range(n_experts):
            h = jax.nn.relu(xf @ w1[e].T + b1[e])
            y = h @ w2[e].T + b2[e]
            out = out + jnp.where((top1 == e)[:, None], y, jnp.zeros((), y.dtype))
        return out.reshape(b, s, d)

    def _L1_attn_ref(x, Wqkv, bqkv, Wout, bout):
        import jax, jax.numpy as jnp
        import numpy as np
        B, N, D = (2, 512, 256)
        H = 16
        DH = D // H
        WINDOW = 64
        SCALE = 1.0 / np.sqrt(DH).astype(np.float32)

        def _causal_window_mask(n: int) -> jnp.ndarray:
            pos = jnp.arange(n)
            diff = pos[:, None] - pos[None, :]
            return (diff >= 0) & (diff < WINDOW)
        b, n, d = x.shape
        qkv = x @ Wqkv.T + bqkv
        qkv = qkv.reshape(b, n, 3, H, DH)
        qkv = jnp.transpose(qkv, (2, 0, 3, 1, 4))
        q, k, v = (qkv[0], qkv[1], qkv[2])
        scores = jnp.einsum('bhqd,bhkd->bhqk', q, k) * SCALE
        mask = _causal_window_mask(n)
        neg_inf = jnp.asarray(-jnp.inf, dtype=scores.dtype)
        scores = jnp.where(mask[None, None], scores, neg_inf)
        attn = jax.nn.softmax(scores, axis=-1)
        out = jnp.einsum('bhqk,bhkd->bhqd', attn, v)
        out = jnp.transpose(out, (0, 2, 1, 3)).reshape(b, n, d)
        return out @ Wout.T + bout

    def _L1_xattn_ref(x, latents, mask, ln_x_g, ln_x_b, ln_l_g, ln_l_b, qn_g, kn_g, Wq, Wkv, Wlkv, Wo, bo):
        import jax, jax.numpy as jnp
        import numpy as np
        DIM_IN, DIM_LAT, DIM_HEAD = (192, 256, 64)
        INNER = max(DIM_LAT, DIM_IN)
        HEADS = INNER // DIM_HEAD
        SCALE = DIM_HEAD ** (-0.5)
        RMS_EPS = 1e-08
        LN_EPS = 1e-05

        def layernorm(x, g, b):
            mu = jnp.mean(x, axis=-1, keepdims=True)
            var = jnp.mean((x - mu) ** 2, axis=-1, keepdims=True)
            return (x - mu) * jax.lax.rsqrt(var + LN_EPS) * g + b

        def rmsnorm(x, gamma):
            norm = jnp.sqrt(jnp.sum(x * x, axis=-1, keepdims=True)) * x.shape[-1] ** (-0.5)
            return x / jnp.maximum(norm, RMS_EPS) * gamma
        b, n, _ = x.shape
        m = latents.shape[1]
        xn = layernorm(x, ln_x_g, ln_x_b)
        ln = layernorm(latents, ln_l_g, ln_l_b)
        q = ln @ Wq.T
        kv = jnp.concatenate([xn @ Wkv.T, ln @ Wlkv.T], axis=1)
        k, v = (kv[..., :INNER], kv[..., INNER:])
        split_heads = lambda t: t.reshape(t.shape[0], t.shape[1], HEADS, DIM_HEAD).transpose(0, 2, 1, 3)
        q, k, v = (split_heads(q), split_heads(k), split_heads(v))
        qn = rmsnorm(q, qn_g) * SCALE
        kn = rmsnorm(k, kn_g)
        attn = jnp.einsum('bhid,bhjd->bhij', qn, kn)
        full_mask = jnp.pad(mask, ((0, 0), (0, m)), constant_values=True)
        attn = jnp.where(full_mask[:, None, None, :], attn, -jnp.finfo(attn.dtype).max)
        attn = jax.nn.softmax(attn, axis=-1)
        out = jnp.einsum('bhij,bhjd->bhid', attn, v)
        out = out.transpose(0, 2, 1, 3).reshape(b, m, INNER)
        return out @ Wo.T + bo

    def _L1_ffn_ref(x, ln_g, ln_b, bn_g, bn_b, bn_mean, bn_var, Wr, br, W_down, b_down, W_up, b_up):
        import jax, jax.numpy as jnp
        import numpy as np
        B, S, D, H, E = (64, 256, 256, 64, 8)
        EPS = 1e-05
        mu = jnp.mean(x, axis=-1, keepdims=True)
        var = jnp.var(x, axis=-1, keepdims=True)
        z = (x - mu) * jax.lax.rsqrt(var + EPS) * ln_g + ln_b
        z_sent = jnp.mean(z, axis=1)
        z_bn = (z_sent - bn_mean) * jax.lax.rsqrt(bn_var + EPS) * bn_g + bn_b
        probs = jax.nn.softmax(z_bn @ Wr + br, axis=-1)
        idx = jnp.argmax(probs, axis=-1)
        gate = jnp.take_along_axis(probs, idx[:, None], axis=1)[:, 0]
        h = jax.nn.relu(jnp.einsum('bsd,bdh->bsh', z, W_down[idx]) + b_down[idx][:, None, :])
        y = jnp.einsum('bsh,bhd->bsd', h, W_up[idx]) + b_up[idx][:, None, :]
        return y * gate[:, None, None]
    x = x + _L0_attn_ref(_layernorm(x, axis=-1), L0_attn_attn_mask, L0_attn_Wq, L0_attn_bq, L0_attn_Wk, L0_attn_bk, L0_attn_Wv, L0_attn_bv, L0_attn_k_gamma, L0_attn_k_beta, L0_attn_v_gamma, L0_attn_v_beta)
    x = x + _L0_xattn_ref(_layernorm(x, axis=-1), ctx_768, L0_xattn_Wq, L0_xattn_bq, L0_xattn_Wk, L0_xattn_bk, L0_xattn_Wv, L0_xattn_bv, L0_xattn_Wo, L0_xattn_bo)
    x = x + _L0_ffn_ref(_layernorm(x, axis=-1), L0_ffn_gate_w, L0_ffn_gate_b, L0_ffn_w1, L0_ffn_b1, L0_ffn_w2, L0_ffn_b2)
    x = x + _L1_attn_ref(_layernorm(x, axis=-1), L1_attn_Wqkv, L1_attn_bqkv, L1_attn_Wout, L1_attn_bout)
    x = x + _L1_xattn_ref(ctx_768, _layernorm(x, axis=-1), mask_BxS2_bk0, L1_xattn_ln_x_g, L1_xattn_ln_x_b, L1_xattn_ln_l_g, L1_xattn_ln_l_b, L1_xattn_qn_g, L1_xattn_kn_g, L1_xattn_Wq, L1_xattn_Wkv, L1_xattn_Wlkv, L1_xattn_Wo, L1_xattn_bo)
    x = x + _L1_ffn_ref(_layernorm(x, axis=-1), L1_ffn_ln_g, L1_ffn_ln_b, L1_ffn_bn_g, L1_ffn_bn_b, L1_ffn_bn_mean, L1_ffn_bn_var, L1_ffn_Wr, L1_ffn_br, L1_ffn_W_down, L1_ffn_b_down, L1_ffn_W_up, L1_ffn_b_up)
    return x

_drawn_inputs = setup_inputs


def setup_inputs(seed=0):
    import zlib

    import numpy as np

    out = dict(_drawn_inputs(seed))
    spreads = {'L0_attn_bq': (0.0, 0.473),
     'L0_attn_bk': (0.0, 0.7),
     'L0_attn_bv': (0.0, 0.419),
     'L0_attn_k_gamma': (1.0, 0.2),
     'L0_attn_k_beta': (0.0, 0.1),
     'L0_attn_v_gamma': (1.0, 0.6),
     'L0_attn_v_beta': (0.0, 0.474),
     'L0_xattn_bq': (0.0, 0.1),
     'L0_xattn_bk': (0.0, 0.8),
     'L0_xattn_bv': (0.0, 0.1),
     'L0_xattn_bo': (0.0, 0.1),
     'L1_attn_bqkv': (0.0, 0.1),
     'L1_attn_bout': (0.0, 0.1),
     'L1_xattn_ln_x_g': (1.0, 0.6),
     'L1_xattn_ln_x_b': (0.0, 0.552),
     'L1_xattn_ln_l_g': (1.0, 0.2),
     'L1_xattn_ln_l_b': (0.0, 0.1),
     'L1_xattn_qn_g': (1.0, 0.6),
     'L1_xattn_kn_g': (1.0, 0.6),
     'L1_xattn_bo': (0.0, 0.1),
     'L1_ffn_ln_g': (1.0, 0.6),
     'L1_ffn_ln_b': (0.0, 0.8),
     'L1_ffn_bn_g': (1.0, 0.6),
     'L1_ffn_bn_b': (0.0, 0.8),
     'L1_ffn_bn_var': (1.0, 0.6),
     'L1_ffn_br': (0.0, 0.772),
     'L1_ffn_b_down': (0.0, 0.8),
     'L1_ffn_b_up': (0.0, 0.636)}
    factors = {'L0_ffn_b1': 4.782,
     'L0_ffn_b2': 3.608,
     'L1_ffn_bn_mean': 8.0,
     'L1_ffn_Wr': 4.921,
     'L1_ffn_W_down': 8.0,
     'L1_ffn_W_up': 8.0}
    for name, (base, spread) in spreads.items():
        noise = np.random.default_rng([zlib.crc32(name.encode()), seed]).standard_normal(out[name].shape)
        drawn = base * np.exp(spread * noise) if base else spread * noise
        out[name] = jnp.asarray(drawn.astype(out[name].dtype))
    for name, factor in factors.items():
        out[name] = (out[name] * factor).astype(out[name].dtype)
    return out
```

```python
from contextlib import ExitStack, contextmanager

import concourse.bass as bass
import numpy as np
from concourse import mybir

ALU = mybir.AluOpType
ACT = mybir.ActivationFunctionType
F32 = mybir.dt.float32
BF16 = mybir.dt.bfloat16
I32 = mybir.dt.int32
U8 = mybir.dt.uint8
AX = mybir.AxisListType

P = 128
B = 16
S = 128
D = 256
C = 192
N = B * S // P
KD = D // P
EPS = 1e-5
FAR = -1e30

QH, QK = 16, 64
H, HD = 16, 16
XH, XD = 4, 64
E, F = 8, 1024
F1 = 64
ROUTED = N + E - 1
WINDOW = 64

BIAS_ROWS = [("q0", QH * QK), ("k0", QK), ("v0", D), ("xq", D), ("xk", D), ("xv", D), ("xo", D), ("gate", E),
             ("aq", D), ("ak", D), ("av", D), ("ao", D), ("po", D), ("route", E)]
BIAS_AT, _n = {}, 0
for _name, _width in BIAS_ROWS:
    BIAS_AT[_name] = (_n, _width)
    _n += _width
BIAS_G = -(-_n // P)
BIAS_N = BIAS_G * P
EXPERT_BIAS = F + D + F1 + D

COLS = {}
for _name, _width in [("kg", 1), ("kb", 1), ("xg", 2), ("xb", 2), ("lg", 2), ("lb", 2), ("qn", 1), ("kn", 1),
                      ("fg", 2), ("fb", 2), ("bng", 2), ("bnb", 2), ("bnm", 2), ("bnv", 2)]:
    COLS[_name] = (sum(w for _, w in COLS.values()), _width)
COLS_N = sum(w for _, w in COLS.values())

CONSTS = {}
for _name, _width in [("ident", P), ("gram", P), ("parity", 2), ("steps", N), ("before", E * E), ("backward", E),
                      ("tiles", ROUTED + 1), ("power", 2), ("root", 3 * XH)]:
    CONSTS[_name] = (sum(w for _, w in CONSTS.values()), _width)
CONSTS_N = sum(w for _, w in CONSTS.values())
CONSTS16 = {}
for _name, _width in [("ident", P), ("upper", P), ("ones", P), ("window", P), ("select", E * P)]:
    CONSTS16[_name] = (sum(w for _, w in CONSTS16.values()), _width)
CONSTS16_N = sum(w for _, w in CONSTS16.values())


def constants():
    c = np.zeros((P, CONSTS_N), np.float32)

    def put(name, a):
        at, width = CONSTS[name]
        c[:, at:at + width] = a

    row, col = np.arange(P)[:, None], np.arange(P)[None, :]
    put("ident", np.eye(P))
    same = (row // B == col // B) & (row % B <= col % B)
    put("gram", same / np.sqrt(col % B + 1.0) / QH)
    head = np.arange(P) // HD % 2
    put("parity", np.stack([head == 0, head == 1], 1) * (HD ** -0.5))
    put("steps", np.arange(N)[None, :] * P)
    put("before", (np.arange(E)[None, :] < np.arange(E)[:, None]).reshape(1, -1))
    put("backward", E - np.arange(E)[None, :])
    put("power", -0.5)
    put("root", 0.5)
    put("tiles", np.arange(ROUTED + 1)[None, :])
    c16 = np.zeros((P, CONSTS16_N), np.float32)

    def put16(name, a):
        at, width = CONSTS16[name]
        c16[:, at:at + width] = a

    put16("ident", np.eye(P))
    put16("upper", row < col)
    put16("ones", 1.0)
    put16("window", np.where((row >= col) & (row - col < WINDOW), 0.0, FAR))
    select = (row[:, :, None] < 3 * E) & (row[:, :, None] % E == np.arange(E)[None, :, None])
    put16("select", np.broadcast_to(select, (P, E, P)).reshape(P, -1))
    return c, c16


class Step:

    def __init__(self, pair, slot, tiles):
        self.pair, self.parity, self.tiles = pair, slot, tiles
        self.step = 2 * pair + slot

    def has(self, k):
        return not isinstance(self.pair, int) or 0 <= self.step - k < self.tiles

    def n(self, k):
        return self.step - k

    def slot(self, k):
        return (self.parity - k) % 2

    def use(self, k):
        return self.pair + (self.parity - k) // 2


def pipeline(eng, tiles, lag, work):
    first = -(-(lag + 2) // 2)
    for s in range(2 * first):
        work(Step(s // 2, s % 2, tiles))
    with eng.Fori(first, tiles // 2) as pair:
        for slot in range(2):
            work(Step(pair, slot, tiles))
    for s in range(tiles // 2 * 2, tiles + lag):
        work(Step(s // 2, s % 2, tiles))


@contextmanager
def semaphores(nc, prefix):
    taken = []

    def sem(name):
        taken.append(nc.alloc_semaphore(name=prefix + name))
        return taken[-1]

    yield sem
    nc.clear_and_free_semaphores(taken)
    nc.all_engine_barrier()


def after(eng, sem, count):
    if not isinstance(count, int) or count > 0:
        eng.wait_ge(sem, count)


def hold(eng, sem, count):
    after(eng, sem, count)
    eng.nop(nofuse=True)


def inverse_root(k, pool, out, var, computed, count):
    n = out.shape[1]
    k.nc.gpsimd.tensor_scalar(out, var, EPS, 1.0, ALU.add, ALU.mult).then_inc(computed, 1)
    pool.wait_ge(computed, 2 * count + 1)
    k.nc.gpsimd.tensor_tensor(out, out, k.const("power")[:, 0:n], ALU.pow).then_inc(computed, 1)


def row(t, n):
    return t[:, bass.ds(n, 1), :].rearrange("p a d -> p (a d)")


def halves(t):
    return t.rearrange("p (a b) -> p a b", b=P)


class Core:
    pass


def decoder(nc, x_seq, ctx_tok, mask, w, cols, bias, expert_bias, consts, consts16, out):
    k = Core()
    k.nc, k.w, k.ctx_tok, k.mask, k.out = nc, w, ctx_tok, mask, out
    k.x1_dram = nc.dram_tensor("x1_by_sequence", (B * S, D), F32).ap()
    k.slots_in = nc.dram_tensor("tokens_by_expert", (ROUTED * P, D), F32).ap()
    k.slots_out = nc.dram_tensor("experts_output", (ROUTED * P, D), F32).ap()
    k.bias_dram = nc.dram_tensor("bias_parts", (3, BIAS_N), BF16).ap()
    with ExitStack() as ctx:
        def sb(name, shape, dt=F32):
            return ctx.enter_context(nc.sbuf_tensor(name, shape, dt))

        k.sb_c, k.sb_c16 = sb("constants", [P, CONSTS_N]), sb("constants16", [P, CONSTS16_N], BF16)
        k.cols = sb("cols", [P, COLS_N])
        k.bias = sb("bias_rows", [3, BIAS_N], BF16)
        k.expert_bias = sb("expert_bias", [P, EXPERT_BIAS], BF16)
        k.x = sb("x", [P, N, D])
        k.slot_i = sb("slot_of_token", [P, N], I32)
        k.tile_expert = sb("expert_of_tile", [P, ROUTED + 1], I32)
        k.loaded = {n: ctx.enter_context(nc.semaphore(n + "_loaded")) for n in (
            "consts", "small", "bias", "x", "w0", "wx0", "ffn", "wa1", "fill")}

        def const(name, table=CONSTS, t=k.sb_c):
            at, width = table[name]
            return t[:, at:at + width]

        k.const = const
        k.const16 = lambda name: const(name, CONSTS16, k.sb_c16)
        k.col = lambda name, i=0, rows=P: k.cols[0:rows, COLS[name][0] + i:COLS[name][0] + i + 1]
        k.bias_row = lambda name, a=0, n=None: k.bias[0:3, BIAS_AT[name][0] + a:BIAS_AT[name][0] + (
            BIAS_AT[name][1] if n is None else a + n)]
        k.ones3 = k.const16("ones")[0:3, :]

        with ExitStack() as first:
            k.w1 = first.enter_context(nc.sbuf_tensor("w1", [P, E, KD, F], F32))
            k.w2 = first.enter_context(nc.sbuf_tensor("w2", [P, E, F // P, D], F32))
            linear_attention(k, x_seq, cols, bias, expert_bias, consts, consts16)
            softmax_attention(k, 0)
            route(k)
            experts(k)
        k.wq1, k.wo1 = sb("wqkv1", [P, KD, 3 * D]), sb("wout1", [P, KD, D])
        softmax_attention(k, 1)
        perceiver(k)
        sentence_experts(k)


def linear_attention(k, x_seq, cols, bias, expert_bias, consts, consts16):
    nc, w = k.nc, k.w
    with ExitStack() as ctx:
        def sb(name, shape, dt=F32):
            return ctx.enter_context(nc.sbuf_tensor("l_" + name, shape, dt))

        sem = ctx.enter_context(semaphores(nc, "l_"))

        def ps(name, cols=512):
            return ctx.enter_context(nc.psum_tensor("l_" + name, [P, cols], F32))

        wq, wkv = sb("wq", [P, KD, QH * QK]), sb("wkv", [P, KD, QK + D])
        v_gain, v_shift = sb("v_gain", [P, D]), sb("v_shift", [P, D])
        bias_f, bias_r = sb("bias_f", [P, BIAS_G]), sb("bias_r", [P, BIAS_G])
        bias_p = sb("bias_p", [P, 3, BIAS_G], BF16)
        eb_f = sb("eb_f", [E, EXPERT_BIAS])
        eb_p = sb("eb_p", [E, EXPERT_BIAS], BF16)
        stats, mv, rstd = sb("stats", [P, 6]), sb("mv", [P, 2]), sb("rstd", [P, 1])
        xn = sb("xn", [P, 2, D])
        xn_t = sb("xn_t", [P, 2, D])
        qmax, qsum = sb("qmax", [P, QH]), sb("qsum", [P, QH])
        qexp = sb("qexp", [P, QH * QK])
        qprob = sb("qprob", [P, QH * QK])
        qk = sb("qk", [P, 2, 2 * QK])
        kvstats, kvmv, kvr = sb("kvstats", [P, 12]), sb("kvmv", [P, 4]), sb("kvr", [P, 2])
        v = sb("v", [P, 2, D])
        qk_t = sb("qk_t", [QK, 2, P])
        gram = sb("gram", [P, P])
        x1 = sb("x1", [P, 2, D])

        p_xt, p_kv, p_qkt, p_out = ps("p_xt"), ps("p_kv"), ps("p_qkt"), ps("p_out")
        p_q = [ps("p_q0", 1024), ps("p_q1", 1024)]

        mv_ready, rstd_steps, kvmv_ready, kvr_steps = (
            sem("mv_ready"), sem("rstd_steps"), sem("kvmv_ready"), sem("kvr_steps"))
        ln, xn_ready, xt_ready, xt_copied = sem("ln"), sem("xn_ready"), sem("xt_ready"), sem("xt_copied")
        q_ready, kv_ready = sem("q_ready"), sem("kv_ready")
        max_ready, sub_ready, exp_ready = sem("max_ready"), sem("sub_ready"), sem("exp_ready")
        sum_ready, rsum_ready, prob_ready, qmean_ready = (
            sem("sum_ready"), sem("rsum_ready"), sem("prob_ready"), sem("qmean_ready"))
        kv_ln, kn_ready, vn_ready, vgain_ready, v_ready = (
            sem("kv_ln"), sem("kn_ready"), sem("vn_ready"), sem("vgain_ready"), sem("v_ready"))
        qkt_ready, qkt_copied = sem("qkt_ready"), sem("qkt_copied")
        gram_ready, gram_masked, att_ready, x1_ready = (
            sem("gram_ready"), sem("gram_masked"), sem("att_ready"), sem("x1_ready"))
        stored = [sem("stored0"), sem("stored1")]
        b_hi, b_res, b_mid, b_res2, b_parts = sem("b_hi"), sem("b_res"), sem("b_mid"), sem("b_res2"), sem("b_parts")
        b_stored, eb_zero, eb_moved, v_rows = sem("b_stored"), sem("eb_zero"), sem("eb_moved"), sem("v_rows")
        eb_steps, zero_set = sem("eb_steps"), sem("zero_set")
        zero = sb("zero", [P, D])
        block = ctx.enter_context(nc.Block())

        @block.sync
        def _(sp):
            sp.dma_start(k.sb_c[:], consts).then_inc(k.loaded["consts"], 16)
            sp.dma_start(bias_f[:], bias).then_inc(k.loaded["small"], 16)
            for a in range(0, N, 4):
                sp.dma_start(k.x[:, a:a + 4, :], x_seq.rearrange("(n p) d -> p n d", p=P)[:, a:a + 4, :]).then_inc(
                    k.loaded["x"], 16)
            sp.dma_start(wkv[:], w["kv0"].rearrange("(c p) n -> p c n", p=P)).then_inc(k.loaded["w0"], 16)
            sp.wait_ge(b_parts, 1)
            for part in range(3):
                sp.dma_start(k.bias_dram[part].rearrange("(p g) -> p g", p=P), bias_p[:, part, :]).then_inc(b_stored, 16)
            sp.wait_ge(b_stored, 48)
            sp.dma_start(k.bias[:], k.bias_dram).then_inc(k.loaded["bias"], 16)
            for e in range(E):
                sp.dma_start(k.w1[:, e], w["w1"][e].rearrange("(c p) n -> p c n", p=P)).then_inc(k.loaded["ffn"], 16)
                sp.dma_start(k.w2[:, e], w["w2"][e].rearrange("(c p) n -> p c n", p=P)).then_inc(k.loaded["ffn"], 16)
            sp.wait_ge(zero_set, 1)
            for i in range(ROUTED):
                sp.dma_start(k.slots_in[i * P:(i + 1) * P, :], zero[:]).then_inc(k.loaded["fill"], 16)
            with sp.Fori(0, N // 2) as pair:
                for slot in range(2):
                    n = 2 * pair + slot
                    sp.wait_ge(x1_ready, n + 1)
                    sp.dma_start(k.x1_dram[bass.ds(n * P, P), :], x1[:, slot, :]).then_inc(stored[slot], 16)
            sp.wait_ge(stored[0], 16 * (N // 2))
            sp.wait_ge(stored[1], 16 * (N // 2))

        @block.gpsimd
        def _(pool):
            nc.gpsimd.memset(zero[:], 0.0).then_inc(zero_set, 1)
            nc.gpsimd.memset(k.expert_bias[:], 0.0).then_inc(eb_zero, 1)
            pool.wait_ge(v_rows, 32)
            pool.wait_ge(k.loaded["consts"], 48)

            def work(st):
                if st.has(0):
                    n = st.n(0)
                    hold(pool, mv_ready, n + 1)
                    inverse_root(k, pool, rstd[:], mv[:, 1:2], rstd_steps, n)
                if st.has(2):
                    n, s = st.n(2), st.slot(2)
                    hold(pool, kvmv_ready, n + 1)
                    inverse_root(k, pool, kvr[:], kvmv[:].rearrange("p (a b) -> p a b", b=2)[:, :, 1], kvr_steps, n)
                    pool.wait_ge(rsum_ready, n + 1)
                    after(pool, qmean_ready, n)
                    nc.gpsimd.tensor_tensor(
                        qprob[:].rearrange("p (h k) -> p h k", k=QK), qexp[:].rearrange("p (h k) -> p h k", k=QK),
                        qsum[:].unsqueeze(2).to_broadcast([P, QH, QK]), ALU.mult).then_inc(prob_ready, 1)
                    pool.wait_ge(vn_ready, n + 1)
                    nc.gpsimd.tensor_tensor(v[:, s, :], v[:, s, :], v_gain[:], ALU.mult).then_inc(vgain_ready, 1)
                    pool.wait_ge(vgain_ready, n + 1)
                    nc.gpsimd.tensor_tensor(v[:, s, :], v[:, s, :], v_shift[:], ALU.add).then_inc(v_ready, 1)

            pipeline(pool, N, 3, work)

        @block.scalar
        def _(act):
            act.dma_start(k.sb_c16[:], consts16).then_inc(k.loaded["consts"], 16)
            act.dma_start(k.cols[:], cols).then_inc(k.loaded["consts"], 16)
            act.dma_start(eb_f[:], expert_bias).then_inc(k.loaded["small"], 16)
            act.dma_start(wq[:], w["q0"].rearrange("(c p) n -> p c n", p=P)).then_inc(k.loaded["w0"], 16)
            act.dma_start(v_gain[:], w["v_gamma"].partition_broadcast(P)).then_inc(v_rows, 16)
            act.dma_start(v_shift[:], w["v_beta"].partition_broadcast(P)).then_inc(v_rows, 16)
            act.wait_ge(eb_zero, 1)
            for part in range(3):
                act.wait_ge(eb_steps, 2 * part + 1)
                act.dma_start(k.expert_bias[part * E:(part + 1) * E, :], eb_p[:]).then_inc(eb_moved, 16)
                act.wait_ge(eb_moved, 16 * (part + 1))
            act.wait_ge(k.loaded["consts"], 48)

            def work(st):
                if st.has(1):
                    n = st.n(1)
                    act.wait_ge(xt_ready, n + 1)
                    after(act, kv_ready, n - 1)
                    nc.scalar.copy(xn_t[:, st.slot(1), :], p_xt[:, 0:D]).then_inc(xt_copied, 1)
                if st.has(2):
                    n = st.n(2)
                    act.wait_ge(sub_ready, n + 1)
                    nc.scalar.activation(qexp[:], qexp[:], ACT.Exp).then_inc(exp_ready, 1)
                if st.has(3):
                    n = st.n(3)
                    act.wait_ge(qkt_ready, n + 1)
                    after(act, gram_ready, n)
                    nc.scalar.copy(qk_t[:, 0, :], p_qkt[0:QK, 0:P])
                    nc.scalar.activation(qk_t[:, 1, :], p_qkt[0:QK, P:2 * P], ACT.Identity, bias=k.col("kb", rows=QK),
                                         scale=k.col("kg", rows=QK)).then_inc(qkt_copied, 1)

            pipeline(act, N, 3, work)

        @block.vector
        def _(dve):
            dve.wait_ge(k.loaded["small"], 32)
            nc.vector.tensor_copy(bias_p[:, 0, :], bias_f[:]).then_inc(b_hi, 1)
            dve.wait_ge(b_hi, 1)
            nc.vector.tensor_tensor(bias_r[:], bias_f[:], bias_p[:, 0, :], ALU.subtract).then_inc(b_res, 1)
            dve.wait_ge(b_res, 1)
            nc.vector.tensor_copy(bias_p[:, 1, :], bias_r[:]).then_inc(b_mid, 1)
            dve.wait_ge(b_mid, 1)
            nc.vector.tensor_tensor(bias_r[:], bias_r[:], bias_p[:, 1, :], ALU.subtract).then_inc(b_res2, 1)
            dve.wait_ge(b_res2, 1)
            nc.vector.tensor_copy(bias_p[:, 2, :], bias_r[:]).then_inc(b_parts, 1)
            for part in range(3):
                after(dve, eb_steps, 2 * part)
                after(dve, eb_moved, 16 * part)
                nc.vector.tensor_copy(eb_p[:], eb_f[:]).then_inc(eb_steps, 1)
                if part < 2:
                    dve.wait_ge(eb_steps, 2 * part + 1)
                    nc.vector.tensor_tensor(eb_f[:], eb_f[:], eb_p[:], ALU.subtract).then_inc(eb_steps, 1)
            dve.wait_ge(k.loaded["consts"], 48)
            dve.wait_ge(k.loaded["x"], 16 * (N // 4))

            def work(st):
                if st.has(0):
                    n, s = st.n(0), st.slot(0)
                    nc.vector.bn_stats(stats[:], row(k.x, n)).then_inc(ln, 1)
                    after(dve, xn_ready, n)
                    hold(dve, ln, n + 1)
                    nc.vector.bn_aggr(mv[:], stats[:]).then_inc(mv_ready, 1)
                if st.has(2):
                    n, s = st.n(2), st.slot(2)
                    q3 = p_q[s][:].rearrange("p (h k) -> p h k", k=QK)
                    e3 = qexp[:].rearrange("p (h k) -> p h k", k=QK)
                    dve.wait_ge(q_ready, n + 1)
                    nc.vector.tensor_reduce(qmax[:], q3, AX.X, ALU.max).then_inc(max_ready, 1)
                    dve.wait_ge(max_ready, n + 1)
                    after(dve, prob_ready, n)
                    nc.vector.tensor_tensor(e3, q3, qmax[:].unsqueeze(2).to_broadcast([P, QH, QK]),
                                            ALU.subtract).then_inc(sub_ready, 1)
                if st.has(3):
                    n = st.n(3)
                    dve.wait_ge(gram_ready, n + 1)
                    after(dve, att_ready, n)
                    nc.vector.tensor_tensor(gram[:], p_out[:, D:D + P], k.const("gram"), ALU.mult).then_inc(
                        gram_masked, 1)
                if st.has(2):
                    n, s = st.n(2), st.slot(2)
                    dve.wait_ge(kv_ready, n + 1)
                    nc.vector.bn_stats(kvstats[:, 0:6], p_kv[:, 0:QK])
                    nc.vector.bn_stats(kvstats[:, 6:12], p_kv[:, QK:QK + D]).then_inc(kv_ln, 1)
                    hold(dve, kv_ln, n + 1)
                    nc.vector.bn_aggr(kvmv[:, 0:2], kvstats[:, 0:6])
                    nc.vector.bn_aggr(kvmv[:, 2:4], kvstats[:, 6:12]).then_inc(kvmv_ready, 1)
                    dve.wait_ge(exp_ready, n + 1)
                    nc.vector.tensor_reduce(qsum[:], e3, AX.X, ALU.add).then_inc(sum_ready, 1)
                    dve.wait_ge(sum_ready, n + 1)
                    nc.vector.reciprocal(qsum[:], qsum[:]).then_inc(rsum_ready, 1)
                    dve.wait_ge(kvr_steps, 2 * n + 2)
                    after(dve, qkt_ready, n - 1)
                    nc.vector.tensor_scalar(qk[:, s, QK:2 * QK], p_kv[:, 0:QK], kvmv[:, 0:1], kvr[:, 0:1],
                                            ALU.subtract, ALU.mult).then_inc(kn_ready, 1)
                    after(dve, att_ready, n - 1)
                    nc.vector.tensor_scalar(v[:, s, :], p_kv[:, QK:QK + D], kvmv[:, 2:3], kvr[:, 1:2], ALU.subtract,
                                            ALU.mult).then_inc(vn_ready, 1)
                if st.has(3):
                    n, s = st.n(3), st.slot(3)
                    dve.wait_ge(att_ready, n + 1)
                    after(dve, stored[s], 16 * st.use(3))
                    nc.vector.tensor_tensor(x1[:, s, :], p_out[:, 0:D], row(k.x, n), ALU.add).then_inc(x1_ready, 1)
                if st.has(2):
                    n, s = st.n(2), st.slot(2)
                    dve.wait_ge(prob_ready, n + 1)
                    nc.vector.tensor_reduce(qk[:, s, 0:QK], qprob[:].rearrange("p (h k) -> p k h", k=QK), AX.X,
                                            ALU.add).then_inc(qmean_ready, 1)
                if st.has(0):
                    n, s = st.n(0), st.slot(0)
                    dve.wait_ge(rstd_steps, 2 * n + 2)
                    after(dve, xt_ready, n - 1)
                    nc.vector.tensor_scalar(xn[:, s, :], row(k.x, n), mv[:, 0:1], rstd[:, 0:1], ALU.subtract,
                                            ALU.mult).then_inc(xn_ready, 1)

            pipeline(dve, N, 3, work)

        @block.tensor
        def _(pe):
            pe.wait_ge(k.loaded["consts"], 48)
            pe.wait_ge(k.loaded["w0"], 32)
            pe.wait_ge(k.loaded["bias"], 16)

            def work(st):
                if st.has(1):
                    n, s = st.n(1), st.slot(1)
                    pe.wait_ge(xn_ready, n + 1)
                    after(pe, xt_copied, n)
                    for c in range(KD):
                        t = nc.tensor.transpose(p_xt[:, c * P:(c + 1) * P], xn[:, s, c * P:(c + 1) * P],
                                                k.const("ident"))
                    t.then_inc(xt_ready, 1)
                if st.has(3):
                    n, s = st.n(3), st.slot(3)
                    pe.wait_ge(qmean_ready, n + 1)
                    after(pe, qkt_copied, n)
                    hold(pe, kn_ready, n + 1)
                    for c in range(2):
                        t = nc.tensor.transpose(p_qkt[0:QK, c * P:(c + 1) * P], qk[:, s, c * QK:(c + 1) * QK],
                                                k.const("ident"))
                    t.then_inc(qkt_ready, 1)
                if st.has(1):
                    n, s = st.n(1), st.slot(1)
                    xt = halves(xn_t[:, s, :])
                    pe.wait_ge(xt_copied, n + 1)
                    after(pe, sub_ready, n - 1)
                    for c in range(2):
                        o = p_q[s][:, c * 512:(c + 1) * 512]
                        nc.tensor.matmul(o, k.ones3, k.bias_row("q0", c * 512, 512), start=True, stop=False)
                        for i in range(KD):
                            t = nc.tensor.matmul(o, xt[:, i, :], wq[:, i, c * 512:(c + 1) * 512], start=False,
                                                 stop=i == KD - 1)
                    t.then_inc(q_ready, 1)
                if st.has(3):
                    n, s = st.n(3), st.slot(3)
                    pe.wait_ge(qkt_copied, n + 1)
                    after(pe, x1_ready, n)
                    nc.tensor.matmul(p_out[:, D:D + P], qk_t[:, 1, :], qk_t[:, 0, :], start=True,
                                     stop=True).then_inc(gram_ready, 1)
                if st.has(1):
                    n, s = st.n(1), st.slot(1)
                    after(pe, vn_ready, n)
                    o = p_kv[:, 0:QK + D]
                    nc.tensor.matmul(o, k.ones3, k.bias[0:3, BIAS_AT["k0"][0]:BIAS_AT["k0"][0] + QK + D], start=True,
                                     stop=False)
                    for i in range(KD):
                        t = nc.tensor.matmul(o, xt[:, i, :], wkv[:, i, :], start=False, stop=i == KD - 1)
                    t.then_inc(kv_ready, 1)
                if st.has(3):
                    n, s = st.n(3), st.slot(3)
                    pe.wait_ge(gram_masked, n + 1)
                    pe.wait_ge(v_ready, n + 1)
                    nc.tensor.matmul(p_out[:, 0:D], gram[:], v[:, s, :], start=True, stop=True).then_inc(att_ready, 1)

            pipeline(pe, N, 3, work)


def softmax_attention(k, layer):
    nc, w = k.nc, k.w
    cross = layer == 0
    with ExitStack() as ctx:
        def sb(name, shape, dt=F32):
            return ctx.enter_context(nc.sbuf_tensor(f"a{layer}_" + name, shape, dt))

        sem = ctx.enter_context(semaphores(nc, f"a{layer}_"))

        def ps(name):
            return ctx.enter_context(nc.psum_tensor(f"a{layer}_" + name, [P, 512], F32))

        STRIPS = 4
        KC = 4 if cross else 2
        if cross:
            wq, wk, wv, wo = (sb("w" + c, [P, KD, D]) for c in "qkvo")
            token = sb("token", [P, 2, C])
        else:
            wq, wk, wv, wo = k.wq1[:, :, 0:D], k.wq1[:, :, D:2 * D], k.wq1[:, :, 2 * D:3 * D], k.wo1
            moe = sb("moe", [P, 2, D])
        stats, mv, rstd = sb("stats", [P, 6]), sb("mv", [P, 2]), sb("rstd", [P, 1])
        xn = sb("xn", [P, 2, D])
        in_t = sb("in_t", [P, KC, P])
        q_t = sb("q_t", [P, 2, 2, 2, P])
        k_t = sb("k_t", [P, 2, 2, P])
        v1 = sb("v1", [P, 2, H, HD + 1])
        smax = sb("smax", [P, 4, STRIPS])
        prob = sb("prob", [P, STRIPS, 512])
        prob_t = sb("prob_t", [P, STRIPS, 512])
        rsum = sb("rsum", [P, H])
        att = sb("att", [P, D])
        att_t = sb("att_t", [P, KD, P])

        p_s = [ps(f"p_s{i}") for i in range(STRIPS)]
        p_in, p_qk, p_vo, p_pv = ps("p_in"), ps("p_qk"), ps("p_vo"), ps("p_pv")

        w_loaded, x_loaded = sem("w_loaded"), sem("x_loaded")
        token_loaded = [sem("token0"), sem("token1")]
        mv_ready, rstd_steps = sem("mv_ready"), sem("rstd_steps")
        one_set, x_summed, ln, xn_ready = sem("one_set"), sem("x_summed"), sem("ln"), sem("xn_ready")
        in_ready, in_copied, qk_ready, q_copied, k_copied = (
            sem("in_ready"), sem("in_copied"), sem("qk_ready"), sem("q_copied"), sem("k_copied"))
        v_ready, v_copied = sem("v_ready"), sem("v_copied")
        s_ready, max_ready, sub_ready, exp_ready = sem("s_ready"), sem("max_ready"), sem("sub_ready"), sem("exp_ready")
        pt_ready, pt_copied, pv_ready = sem("pt_ready"), sem("pt_copied"), sem("pv_ready")
        rsum_ready, att_ready, att_t_ready, att_t_copied = (
            sem("rsum_ready"), sem("att_ready"), sem("att_t_ready"), sem("att_t_copied"))
        o_ready, x_ready = sem("o_ready"), sem("x_ready")
        block = ctx.enter_context(nc.Block())

        @block.sync
        def _(sp):
            if not cross:
                sp.dma_start(k.wq1[:], w["qkv1"].rearrange("(c p) n -> p c n", p=P)).then_inc(k.loaded["wa1"], 16)
                sp.dma_start(k.wo1[:], w["out1"].rearrange("(c p) n -> p c n", p=P)).then_inc(k.loaded["wa1"], 16)
                return
            for a in range(0, N, 4):
                sp.dma_start(k.x[:, a:a + 4, :], k.x1_dram.rearrange("(s n) d -> s n d", n=N)[:, a:a + 4, :]).then_inc(
                    x_loaded, 16)
            for t, name in ((wq, "xq"), (wo, "xo")):
                sp.dma_start(t[:], w[name].rearrange("(c p) n -> p c n", p=P)).then_inc(w_loaded, 16)
            for t, name in ((wk, "xk"), (wv, "xv")):
                sp.dma_start(t[:, 0, :], w[name][0:P, :]).then_inc(w_loaded, 16)
                sp.dma_start(t[0:C - P, 1, :], w[name][P:C, :]).then_inc(w_loaded, 16)
            for slot in range(2):
                sp.dma_start(token[:, slot, :], k.ctx_tok[slot]).then_inc(token_loaded[slot], 16)
            with sp.Fori(1, N // 2) as pair:
                for slot in range(2):
                    sp.wait_ge(in_ready, 2 * pair + slot - 1)
                    sp.dma_start(token[:, slot, :], k.ctx_tok[bass.ds(2 * pair + slot, 1)].rearrange(
                        "a s c -> (a s) c")).then_inc(token_loaded[slot], 16)

        @block.gpsimd
        def _(pool):
            nc.gpsimd.memset(v1[:], 1.0).then_inc(one_set, 1)

            def gather(n, slot):
                nc.gpsimd.indirect_dma_start(
                    out=moe[:, slot, :], out_offset=None, in_=k.slots_out,
                    in_offset=bass.IndirectOffsetOnAxis(ap=k.slot_i[:, n:n + 1], axis=0)).then_inc(
                    token_loaded[slot], 16)

            if not cross:
                gather(0, 0)
            for n in range(N):
                if not cross and n + 1 < N:
                    after(pool, x_summed, n)
                    gather(n + 1, (n + 1) % 2)
                hold(pool, mv_ready, n + 1)
                inverse_root(k, pool, rstd[:], mv[:, 1:2], rstd_steps, n)

        @block.scalar
        def _(act):
            act.wait_ge(one_set, 1)

            def work(st):
                if st.has(3):
                    n = st.n(3)
                    act.wait_ge(att_t_ready, n + 1)
                    after(act, o_ready, n)
                    nc.scalar.copy(att_t[:], halves(p_vo[:, 0:D])).then_inc(att_t_copied, 1)
                if st.has(1):
                    n = st.n(1)
                    act.wait_ge(in_ready, n + 1)
                    after(act, v_ready, n)
                    if cross:
                        nc.scalar.copy(in_t[:, 0:3, :], halves(p_in[:, 0:3 * P]))
                        nc.scalar.copy(in_t[0:C - P, 3, :], p_in[0:C - P, 3 * P:]).then_inc(in_copied, 1)
                    else:
                        nc.scalar.copy(in_t[:], halves(p_in[:, 0:D])).then_inc(in_copied, 1)
                if st.has(2):
                    n = st.n(2)
                    for i in range(STRIPS):
                        act.wait_ge(sub_ready, STRIPS * n + i + 1)
                        nc.scalar.activation(prob[:, i, :], prob[:, i, :], ACT.Exp).then_inc(exp_ready, 1)
                if st.has(1):
                    n, s = st.n(1), st.slot(1)
                    act.wait_ge(q_copied, n + 1)
                    after(act, s_ready, STRIPS * (n - 1))
                    nc.scalar.copy(k_t[:, s], halves(p_qk[:, D:2 * D])).then_inc(k_copied, 1)
                    act.wait_ge(v_ready, n + 1)
                    after(act, pv_ready, n - 1)
                    nc.scalar.copy(v1[:, s, :, 0:HD], p_vo[:, 0:D].rearrange("p (h c) -> p h c", c=HD)).then_inc(
                        v_copied, 1)
                if st.has(2):
                    n = st.n(2)
                    after(act, pv_ready, n)
                    for i in range(STRIPS):
                        act.wait_ge(pt_ready, STRIPS * n + i + 1)
                        nc.scalar.copy(prob_t[:, i, :], p_s[i][:]).then_inc(pt_copied, 1)

            pipeline(act, N, 3, work)

        @block.vector
        def _(dve):
            if cross:
                dve.wait_ge(x_loaded, 16 * (N // 4))

            def work(st):
                if st.has(2):
                    n = st.n(2)
                    for i in range(STRIPS):
                        sc = halves(p_s[i][:])
                        dve.wait_ge(s_ready, STRIPS * n + i + 1)
                        nc.vector.tensor_reduce(smax[:, :, i], sc, AX.X, ALU.max).then_inc(max_ready, 1)
                        dve.wait_ge(max_ready, STRIPS * n + i + 1)
                        after(dve, pt_ready, STRIPS * (n - 1) + i + 1)
                        nc.vector.tensor_tensor(halves(prob[:, i, :]), sc, smax[:, :, i].unsqueeze(2).to_broadcast(
                            [P, 4, P]), ALU.subtract).then_inc(sub_ready, 1)
                if st.has(3):
                    n = st.n(3)
                    dve.wait_ge(o_ready, n + 1)
                    nc.vector.tensor_tensor(row(k.x, n), p_vo[:, D:2 * D], row(k.x, n), ALU.add).then_inc(x_ready, 1)
                if st.has(1):
                    n, s = st.n(1), st.slot(1)
                    dve.wait_ge(qk_ready, n + 1)
                    after(dve, s_ready, STRIPS * (n - 1))
                    for parity in range(2):
                        t = nc.vector.tensor_scalar(q_t[:, s, parity], halves(p_qk[:, 0:D]),
                                                    k.const("parity")[:, parity:parity + 1], None, ALU.mult)
                    t.then_inc(q_copied, 1)
                if st.has(0):
                    n, s = st.n(0), st.slot(0)
                    if not cross:
                        dve.wait_ge(token_loaded[s], 16 * (st.use(0) + 1))
                        nc.vector.tensor_tensor(row(k.x, n), moe[:, s, :], row(k.x, n), ALU.add).then_inc(x_summed, 1)
                        hold(dve, x_summed, n + 1)
                    nc.vector.bn_stats(stats[:], row(k.x, n)).then_inc(ln, 1)
                    after(dve, xn_ready, n)
                    hold(dve, ln, n + 1)
                    nc.vector.bn_aggr(mv[:], stats[:]).then_inc(mv_ready, 1)
                if st.has(2):
                    n = st.n(2)
                    pv = p_pv[:, 0:H * (HD + 1)].rearrange("p (h c) -> p h c", c=HD + 1)
                    dve.wait_ge(pv_ready, n + 1)
                    nc.vector.reciprocal(rsum[:], pv[:, :, HD]).then_inc(rsum_ready, 1)
                    dve.wait_ge(rsum_ready, n + 1)
                    after(dve, att_t_ready, n)
                    nc.vector.tensor_tensor(att[:].rearrange("p (h c) -> p h c", c=HD), pv[:, :, 0:HD],
                                            rsum[:].unsqueeze(2).to_broadcast([P, H, HD]), ALU.mult).then_inc(
                        att_ready, 1)
                if st.has(0):
                    n, s = st.n(0), st.slot(0)
                    dve.wait_ge(rstd_steps, 2 * n + 2)
                    after(dve, in_ready, n - 1)
                    nc.vector.tensor_scalar(xn[:, s, :], row(k.x, n), mv[:, 0:1], rstd[:, 0:1], ALU.subtract,
                                            ALU.mult).then_inc(xn_ready, 1)

            pipeline(dve, N, 3, work)

        @block.tensor
        def _(pe):
            if cross:
                pe.wait_ge(w_loaded, 16 * 6)
            else:
                pe.wait_ge(k.loaded["wa1"], 32)
            names = ("xq", "xk", "xv", "xo") if cross else ("aq", "ak", "av", "ao")
            kv_chunks = [(2, P), (3, C - P)] if cross else [(0, P), (1, P)]

            def work(st):
                if st.has(2):
                    n, s = st.n(2), st.slot(2)
                    pe.wait_ge(q_copied, n + 1)
                    pe.wait_ge(k_copied, n + 1)
                    after(pe, pt_copied, STRIPS * n)
                    if not cross:
                        for i in range(STRIPS):
                            nc.tensor.matmul(halves(p_s[i][:]), k.const16("ident"), k.const16("window").unsqueeze(
                                1).to_broadcast([P, 4, P]), start=True, stop=False, skip_group_check=True)
                    for j in range(4):
                        half, parity = j // 2, j % 2
                        for i in range(STRIPS):
                            rows = slice(32 * i, 32 * i + 32)
                            t = nc.tensor.matmul(p_s[i][:, j * P:(j + 1) * P], q_t[rows, s, parity, half, :],
                                                 k_t[rows, s, half, :], start=cross, stop=True,
                                                 skip_group_check=not cross)
                            if j == 3:
                                t.then_inc(s_ready, 1)
                if st.has(3):
                    n = st.n(3)
                    pe.wait_ge(att_ready, n + 1)
                    after(pe, v_copied, n + 2 if st.has(1) else N)
                    for c in range(KD):
                        t = nc.tensor.transpose(p_vo[:, c * P:(c + 1) * P], att[:, c * P:(c + 1) * P],
                                                k.const("ident"))
                    t.then_inc(att_t_ready, 1)
                if st.has(1):
                    n, s = st.n(1), st.slot(1)
                    pe.wait_ge(xn_ready, n + 1)
                    after(pe, in_copied, n)
                    for c in range(KD):
                        t = nc.tensor.transpose(p_in[:, c * P:(c + 1) * P], xn[:, s, c * P:(c + 1) * P],
                                                k.const("ident"))
                    if cross:
                        pe.wait_ge(token_loaded[s], 16 * (st.use(1) + 1))
                        nc.tensor.transpose(p_in[:, 2 * P:3 * P], token[:, s, 0:P], k.const("ident"))
                        t = nc.tensor.transpose(p_in[0:C - P, 3 * P:4 * P], token[:, s, P:C], k.const("ident"))
                    t.then_inc(in_ready, 1)
                if st.has(3):
                    n = st.n(3)
                    pe.wait_ge(att_t_copied, n + 1)
                    o = p_vo[:, D:2 * D]
                    nc.tensor.matmul(o, k.ones3, k.bias_row(names[3]), start=True, stop=False)
                    for i in range(KD):
                        t = nc.tensor.matmul(o, att_t[:, i, :], wo[:, i, :], start=False, stop=i == KD - 1)
                    t.then_inc(o_ready, 1)
                if st.has(1):
                    n, s = st.n(1), st.slot(1)
                    pe.wait_ge(in_copied, n + 1)
                    after(pe, q_copied, n)
                    after(pe, k_copied, n)
                    for name, wt, at, chunks in ((names[0], wq, 0, [(0, P), (1, P)]), (names[1], wk, D, kv_chunks)):
                        for c in range(KD):
                            o = p_qk[:, at + c * P:at + (c + 1) * P]
                            nc.tensor.matmul(o, k.bias_row(name, c * P, P), k.ones3, start=True, stop=False)
                            for i, (chunk, rows) in enumerate(chunks):
                                t = nc.tensor.matmul(o, wt[0:rows, i, c * P:(c + 1) * P], in_t[0:rows, chunk, :],
                                                     start=False, stop=i == KD - 1)
                    t.then_inc(qk_ready, 1)
                    after(pe, x_ready, n - 1)
                    o = p_vo[:, 0:D]
                    nc.tensor.matmul(o, k.ones3, k.bias_row(names[2]), start=True, stop=False)
                    for i, (chunk, rows) in enumerate(kv_chunks):
                        t = nc.tensor.matmul(o, in_t[0:rows, chunk, :], wv[0:rows, i, :], start=False,
                                             stop=i == KD - 1)
                    t.then_inc(v_ready, 1)
                if st.has(2):
                    n, s = st.n(2), st.slot(2)

                    def turn(i):
                        pe.wait_ge(exp_ready, STRIPS * n + i + 1)
                        for j in range(4):
                            t = nc.tensor.transpose(p_s[i][:, j * P:(j + 1) * P], prob[:, i, j * P:(j + 1) * P],
                                                    k.const("ident"))
                        t.then_inc(pt_ready, 1)

                    def weigh(i):
                        pe.wait_ge(pt_copied, STRIPS * n + i + 1)
                        for j in range(4):
                            h = 8 * (j // 2) + 2 * i + j % 2
                            t = nc.tensor.matmul(p_pv[:, h * (HD + 1):(h + 1) * (HD + 1)],
                                                 prob_t[:, i, j * P:(j + 1) * P], v1[:, s, h, :], start=True,
                                                 stop=True)
                        return t

                    turn(0)
                    turn(1)
                    pe.wait_ge(v_copied, n + 1)
                    after(pe, att_ready, n)
                    for i in range(STRIPS):
                        t = weigh(i)
                        if i + 2 < STRIPS:
                            turn(i + 2)
                    t.then_inc(pv_ready, 1)

            pipeline(pe, N, 3, work)


class Steps:

    def __init__(self, eng, sem):
        self.eng, self.sem, self.count = eng, sem, 0

    def then(self, instruction):
        instruction.then_inc(self.sem, 1)
        self.count += 1
        self.eng.wait_ge(self.sem, self.count)


def route(k):
    nc, w = k.nc, k.w
    with ExitStack() as ctx:
        def sb(name, shape, dt=F32):
            return ctx.enter_context(nc.sbuf_tensor("r_" + name, shape, dt))

        sem = ctx.enter_context(semaphores(nc, "r_"))

        wg = sb("wg", [P, KD, E])
        stats, mv, rstd = sb("stats", [P, 2, 6]), sb("mv", [P, 2, 2]), sb("rstd", [P, 2])
        xn, xn_all, xn_t = sb("xn", [P, 2, D]), sb("xn_all", [P, N, D]), sb("xn_t", [P, 2, D])
        logits, score = sb("logits", [P, N, E]), sb("score", [P, N, E])
        best = sb("best", [P, N])
        chosen, chosen16 = sb("chosen", [P, N, E]), sb("chosen16", [P, N + 1, E], BF16)
        rank = sb("rank", [P, N + 1, E])
        over = sb("over", [P, E, N])
        tiles_of, tri = sb("tiles_of", [P, E]), sb("tri", [P, E, E])
        first, last = sb("first", [P, E]), sb("last", [P, E])
        ends = sb("ends", [P, ROUTED + 1, E])
        tile_f = sb("tile_f", [P, ROUTED + 1])
        slot_f = sb("slot_f", [P, N])
        p_t = [ctx.enter_context(nc.psum_tensor(f"r_p_t{i}", [P, 512], F32)) for i in range(2)]
        p_lg = ctx.enter_context(nc.psum_tensor("r_p_lg", [P, 512], F32))
        p_rank = ctx.enter_context(nc.psum_tensor("r_p_rank", [P, 512], F32))

        w_loaded, ln, mv_ready, rstd_steps, xn_ready = (
            sem("w_loaded"), sem("ln"), sem("mv_ready"), sem("rstd_steps"), sem("xn_ready"))
        xn_kept, t_ready, t_copied, logits_ready = sem("xn_kept"), sem("t_ready"), sem("t_copied"), sem("logits_ready")
        steps, chosen_ready, rank_ready, slots_ready, sent = (
            sem("steps"), sem("chosen_ready"), sem("rank_ready"), sem("slots_ready"), sem("sent"))
        block = ctx.enter_context(nc.Block())

        @block.sync
        def _(sp):
            sp.dma_start(wg[:], w["gate"].rearrange("(c p) n -> p c n", p=P)).then_inc(w_loaded, 16)

        @block.gpsimd
        def _(pool):
            for n in range(N):
                s = n % 2
                pool.wait_ge(mv_ready, n + 1)
                inverse_root(k, pool, rstd[:, s:s + 1], mv[:, s, 1:2], rstd_steps, n)
            pool.wait_ge(slots_ready, 1)
            pool.wait_ge(xn_kept, N)
            pool.wait_ge(k.loaded["fill"], 16 * ROUTED)
            for n in range(N):
                nc.gpsimd.indirect_dma_start(
                    out=k.slots_in, out_offset=bass.IndirectOffsetOnAxis(ap=k.slot_i[:, n:n + 1], axis=0),
                    in_=xn_all[:, n, :], in_offset=None).then_inc(sent, 16)
            pool.wait_ge(sent, 16 * N)

        @block.scalar
        def _(act):
            def work(st):
                if st.has(2):
                    n, s = st.n(2), st.slot(2)
                    act.wait_ge(xn_ready, n + 1)
                    nc.scalar.copy(row(xn_all, n), xn[:, s, :]).then_inc(xn_kept, 1)
                    act.wait_ge(t_ready, n + 1)
                    after(act, logits_ready, n - 1)
                    nc.scalar.copy(xn_t[:, s, :], p_t[s][:, 0:D]).then_inc(t_copied, 1)

            pipeline(act, N, 2, work)

        @block.vector
        def _(dve):
            def work(st):
                if st.has(0):
                    n, s = st.n(0), st.slot(0)
                    nc.vector.bn_stats(stats[:, s, :], row(k.x, n)).then_inc(ln, 1)
                if st.has(1):
                    n, s = st.n(1), st.slot(1)
                    dve.wait_ge(rstd_steps, 2 * n + 2)
                    after(dve, t_ready, n - 1)
                    after(dve, xn_kept, n - 1)
                    nc.vector.tensor_scalar(xn[:, s, :], row(k.x, n), mv[:, s, 0:1], rstd[:, s:s + 1], ALU.subtract,
                                            ALU.mult).then_inc(xn_ready, 1)
                if st.has(0):
                    n, s = st.n(0), st.slot(0)
                    after(dve, xn_ready, n - 1)
                    hold(dve, ln, n + 1)
                    nc.vector.bn_aggr(mv[:, s, :], stats[:, s, :]).then_inc(mv_ready, 1)

            pipeline(dve, N, 2, work)
            chain = Steps(dve, steps)
            by_tile = [P, N, E]
            dve.wait_ge(logits_ready, N)
            chain.then(nc.vector.tensor_copy(logits[:], p_lg[:, 0:N * E].rearrange("p (n e) -> p n e", e=E)))
            chain.then(nc.vector.tensor_reduce(best[:], logits[:], AX.X, ALU.max))
            chain.then(nc.vector.tensor_tensor(score[:], logits[:], best[:].unsqueeze(2).to_broadcast(by_tile),
                                               ALU.is_ge))
            backward = k.const("backward").unsqueeze(1).to_broadcast(by_tile)
            chain.then(nc.vector.tensor_tensor(score[:], score[:], backward, ALU.mult))
            chain.then(nc.vector.tensor_reduce(best[:], score[:], AX.X, ALU.max))
            chain.then(nc.vector.tensor_tensor(chosen[:], backward, best[:].unsqueeze(2).to_broadcast(by_tile),
                                               ALU.is_equal))
            chain.then(nc.vector.memset(chosen16[:], 0.0))
            nc.vector.tensor_copy(chosen16[:, 0:N, :], chosen[:]).then_inc(chosen_ready, 1)
            dve.wait_ge(rank_ready, 1)
            chain.then(nc.vector.tensor_copy(rank[:], p_rank[:, 0:(N + 1) * E].rearrange("p (n e) -> p n e", e=E)))
            chain.then(nc.vector.tensor_tensor(over[:], rank[:, N, :].unsqueeze(2).to_broadcast([P, E, N]),
                                               k.const("steps").unsqueeze(1).to_broadcast([P, E, N]), ALU.is_gt))
            chain.then(nc.vector.tensor_reduce(tiles_of[:], over[:], AX.X, ALU.add))
            chain.then(nc.vector.tensor_tensor(tri[:], k.const("before").rearrange("p (a b) -> p a b", b=E),
                                               tiles_of[:].unsqueeze(1).to_broadcast([P, E, E]), ALU.mult))
            chain.then(nc.vector.tensor_reduce(first[:], tri[:], AX.X, ALU.add))
            chain.then(nc.vector.tensor_tensor(last[:], first[:], tiles_of[:], ALU.add))
            shape = [P, ROUTED + 1, E]
            chain.then(nc.vector.tensor_tensor(ends[:], k.const("tiles").unsqueeze(2).to_broadcast(shape),
                                               last[:].unsqueeze(1).to_broadcast(shape), ALU.is_ge))
            chain.then(nc.vector.tensor_reduce(tile_f[:], ends[:], AX.X, ALU.add))
            chain.then(nc.vector.tensor_scalar(k.tile_expert[:], tile_f[:], float(E - 1), None, ALU.min))
            chain.then(nc.vector.tensor_scalar(first[:], first[:], float(P), None, ALU.mult))
            chain.then(nc.vector.tensor_tensor(rank[:, 0:N, :], rank[:, 0:N, :],
                                               first[:].unsqueeze(1).to_broadcast(by_tile), ALU.add))
            chain.then(nc.vector.tensor_tensor(rank[:, 0:N, :], rank[:, 0:N, :], chosen[:], ALU.mult))
            chain.then(nc.vector.tensor_reduce(slot_f[:], rank[:, 0:N, :], AX.X, ALU.add))
            nc.vector.tensor_copy(k.slot_i[:], slot_f[:]).then_inc(slots_ready, 1)

        @block.tensor
        def _(pe):
            pe.wait_ge(w_loaded, 16)

            def work(st):
                if st.has(2):
                    n, s = st.n(2), st.slot(2)
                    pe.wait_ge(xn_ready, n + 1)
                    after(pe, t_copied, n - 1)
                    for c in range(KD):
                        t = nc.tensor.transpose(p_t[s][:, c * P:(c + 1) * P], xn[:, s, c * P:(c + 1) * P],
                                                k.const("ident"))
                    t.then_inc(t_ready, 1)
                if st.has(3):
                    n, s = st.n(3), st.slot(3)
                    o = p_lg[:, bass.ds(n * E, E)]
                    pe.wait_ge(t_copied, n + 1)
                    pe.nop(nofuse=True)
                    nc.tensor.matmul(o, k.ones3, k.bias_row("gate"), start=True, stop=False)
                    xt = halves(xn_t[:, s, :])
                    for i in range(KD):
                        t = nc.tensor.matmul(o, xt[:, i, :], wg[:, i, :], start=False, stop=i == KD - 1)
                    t.then_inc(logits_ready, 1)

            pipeline(pe, N, 3, work)
            pe.wait_ge(chosen_ready, 1)
            nc.tensor.matmul(p_rank[:, 0:(N + 1) * E], k.const16("upper"), chosen16[:].rearrange("p n e -> p (n e)"),
                             start=True, stop=False, skip_group_check=True)
            for n in range(N):
                later = N - n
                t = nc.tensor.matmul(p_rank[:, (n + 1) * E:(N + 1) * E].rearrange("p (n e) -> p n e", e=E),
                                     k.const16("ones"), chosen16[:, n:n + 1, :].to_broadcast([P, later, E]),
                                     start=False, stop=n == N - 1, skip_group_check=True)
            t.then_inc(rank_ready, 1)


def experts(k):
    nc = k.nc
    with ExitStack() as ctx:
        def sb(name, shape, dt=F32):
            return ctx.enter_context(nc.sbuf_tensor("e_" + name, shape, dt))

        sem = ctx.enter_context(semaphores(nc, "e_"))

        def ps(name, cols=512):
            return ctx.enter_context(nc.psum_tensor("e_" + name, [P, cols], F32))

        HC = F // P
        xs, xs_t = sb("xs", [P, 2, D]), sb("xs_t", [P, KD, P])
        hidden, hidden_t = sb("hidden", [P, F]), sb("hidden_t", [P, HC, P])
        y = sb("y", [P, 2, D])
        p_in, p_h, p_ht, p_y = ps("p_in"), ps("p_h", F), ps("p_ht", F), ps("p_y")
        loaded = [sem("loaded0"), sem("loaded1")]
        in_ready, in_copied, h_ready, relu_ready = sem("in_ready"), sem("in_copied"), sem("h_ready"), sem("relu_ready")
        ht_ready, ht_copied, y_ready, y_copied = sem("ht_ready"), sem("ht_copied"), sem("y_ready"), sem("y_copied")
        stored = [sem("stored0"), sem("stored1")]
        block = ctx.enter_context(nc.Block())

        @block.sync
        def _(sp):
            def work(st):
                if st.has(0):
                    n, s = st.n(0), st.slot(0)
                    after(sp, in_ready, n - 1)
                    sp.dma_start(xs[:, s, :], k.slots_in[bass.ds(n * P, P), :]).then_inc(loaded[s], 16)

            pipeline(sp, ROUTED, 1, work)

        @block.gpsimd
        def _(pool):
            def work(st):
                if st.has(1):
                    n, s = st.n(1), st.slot(1)
                    pool.wait_ge(y_copied, n + 1)
                    pool.nop(nofuse=True)
                    pool.dma_start(k.slots_out[bass.ds(n * P, P), :], y[:, s, :]).then_inc(stored[s], 16)

            pipeline(pool, ROUTED, 1, work)
            pool.wait_ge(stored[0], 16 * ((ROUTED + 1) // 2))
            pool.wait_ge(stored[1], 16 * (ROUTED // 2))

        @block.scalar
        def _(act):
            def work(st):
                if st.has(0):
                    n = st.n(0)
                    act.wait_ge(in_ready, n + 1)
                    after(act, h_ready, 2 * n)
                    nc.scalar.copy(xs_t[:], halves(p_in[:, 0:D])).then_inc(in_copied, 1)
                    for c in range(2):
                        act.wait_ge(h_ready, 2 * n + c + 1)
                        after(act, ht_ready, 2 * n)
                        nc.scalar.activation(hidden[:, c * 512:(c + 1) * 512], p_h[:, c * 512:(c + 1) * 512],
                                             ACT.Relu).then_inc(relu_ready, 1)

            pipeline(act, ROUTED, 1, work)

        @block.vector
        def _(dve):
            def work(st):
                if st.has(1):
                    n, s = st.n(1), st.slot(1)
                    for c in range(2):
                        dve.wait_ge(ht_ready, 2 * n + c + 1)
                        after(dve, y_ready, n)
                        nc.vector.tensor_copy(hidden_t[:, 4 * c:4 * c + 4, :],
                                              halves(p_ht[:, c * 512:(c + 1) * 512])).then_inc(ht_copied, 1)
                    dve.wait_ge(y_ready, n + 1)
                    after(dve, stored[s], 16 * st.use(1))
                    nc.vector.tensor_copy(y[:, s, :], p_y[:, 0:D]).then_inc(y_copied, 1)

            pipeline(dve, ROUTED, 1, work)

        @block.tensor
        def _(pe):
            pe.wait_ge(k.loaded["ffn"], 16 * 2 * E)

            def expert_of(n):
                e = pe.value_load(k.tile_expert[0:1, bass.ds(n, 1)], min_val=0, max_val=E - 1)
                return e, k.const16("select")[:, bass.ds(e * P, P)]

            def work(st):
                if st.has(0):
                    n, s = st.n(0), st.slot(0)
                    pe.wait_ge(loaded[s], 16 * (st.use(0) + 1))
                    after(pe, in_copied, n)
                    for c in range(KD):
                        t = nc.tensor.transpose(p_in[:, c * P:(c + 1) * P], xs[:, s, c * P:(c + 1) * P],
                                                k.const("ident"))
                    t.then_inc(in_ready, 1)
                if st.has(1):
                    n = st.n(1)
                    for c in range(2):
                        pe.wait_ge(relu_ready, 2 * n + c + 1)
                        after(pe, ht_copied, 2 * n)
                        for j in range(4 * c, 4 * c + 4):
                            t = nc.tensor.transpose(p_ht[:, j * P:(j + 1) * P], hidden[:, j * P:(j + 1) * P],
                                                    k.const("ident"))
                        t.then_inc(ht_ready, 1)
                if st.has(0):
                    n = st.n(0)
                    e, select = expert_of(n)
                    pe.wait_ge(in_copied, n + 1)
                    pe.nop(nofuse=True)
                    for c in range(2):
                        o = p_h[:, c * 512:(c + 1) * 512]
                        nc.tensor.matmul(o, select, k.expert_bias[:, c * 512:(c + 1) * 512], start=True, stop=False)
                        for i in range(KD):
                            t = nc.tensor.matmul(o, xs_t[:, i, :], k.w1[:, bass.ds(e, 1), i, c * 512:(c + 1) * 512]
                                                 .rearrange("p a n -> p (a n)"), start=False, stop=i == KD - 1)
                        t.then_inc(h_ready, 1)
                if st.has(1):
                    n = st.n(1)
                    e, select = expert_of(n)
                    pe.wait_ge(ht_copied, 2 * n + 2)
                    after(pe, y_copied, n)
                    pe.nop(nofuse=True)
                    nc.tensor.matmul(p_y[:, 0:D], select, k.expert_bias[:, F:F + D], start=True, stop=False)
                    for j in range(HC):
                        t = nc.tensor.matmul(p_y[:, 0:D], hidden_t[:, j, :], k.w2[:, bass.ds(e, 1), j, :].rearrange(
                            "p a n -> p (a n)"), start=False, stop=j == HC - 1)
                    t.then_inc(y_ready, 1)

            pipeline(pe, ROUTED, 1, work)


def perceiver(k):
    nc, w = k.nc, k.w
    with ExitStack() as ctx:
        def sb(name, shape, dt=F32):
            return ctx.enter_context(nc.sbuf_tensor("p_" + name, shape, dt))

        sem = ctx.enter_context(semaphores(nc, "p_"))

        def ps(name):
            return ctx.enter_context(nc.psum_tensor("p_" + name, [P, 512], F32))

        C1 = C - P
        wq, wl, wc, wo = (sb("wq", [P, KD, D]), sb("wl", [P, KD, 2 * D]), sb("wc", [P, KD, 2 * D]),
                          sb("wo", [P, KD, D]))
        mask_u8, allowed = sb("mask_u8", [1, N * S], U8), sb("allowed", [P, N, S], BF16)
        token = sb("token", [P, 2, C])
        stats, mv = sb("stats", [P, 2, 6]), sb("mv", [P, 2, 2])
        rstd, var2, rstd2 = sb("rstd", [P, 2]), sb("var2", [P, 1]), sb("rstd2", [P, 1])
        xn, cn = sb("xn", [P, D]), sb("cn", [P, C])
        in_t = sb("in_t", [P, 4, P])
        square = sb("square", [P, 3 * XH, XD])
        norm = sb("norm", [P, 3 * XH])
        qk = sb("qk", [P, 3 * XH, XD])
        v1 = sb("v1", [P, 2, 2, XH, XD + 1])
        q_t, k_t = sb("q_t", [P, 2, P]), sb("k_t", [P, 2, 2, P])
        smax, prob, prob_t = sb("smax", [P, 2, 2]), sb("prob", [P, 2, 512]), sb("prob_t", [P, 2, 512])
        rsum, att, att_t = sb("rsum", [P, XH]), sb("att", [P, D]), sb("att_t", [P, KD, P])
        p_in, p_q, p_l, p_c, p_k, p_pv = ps("p_in"), ps("p_q"), ps("p_l"), ps("p_c"), ps("p_k"), ps("p_pv")
        p_s = [ps("p_s0"), ps("p_s1")]

        w_loaded, mask_loaded, allowed_zero, allowed_ready, one_set = (
            sem("w_loaded"), sem("mask_loaded"), sem("allowed_zero"), sem("allowed_ready"), sem("one_set"))
        token_loaded = [sem("token0"), sem("token1")]
        ln, mv_ready, root_steps, xn_ready = sem("ln"), sem("mv_ready"), sem("root_steps"), sem("xn_ready")
        in_ready, in_copied, proj_ready, sq_ready, v_copied = (
            sem("in_ready"), sem("in_copied"), sem("proj_ready"), sem("sq_ready"), sem("v_copied"))
        ss_ready, norm_steps, rnorm_ready, qk_ready = sem("ss_ready"), sem("norm_steps"), sem("rnorm_ready"), sem("qk_ready")
        qkt_ready, qkt_copied, s_ready, max_ready, sub_ready, exp_ready = (
            sem("qkt_ready"), sem("qkt_copied"), sem("s_ready"), sem("max_ready"), sem("sub_ready"), sem("exp_ready"))
        pt_ready, pt_copied, pv_ready, rsum_ready, att_ready = (
            sem("pt_ready"), sem("pt_copied"), sem("pv_ready"), sem("rsum_ready"), sem("att_ready"))
        att_t_ready, att_t_copied, o_ready, x_ready = (
            sem("att_t_ready"), sem("att_t_copied"), sem("o_ready"), sem("x_ready"))
        block = ctx.enter_context(nc.Block())

        @block.sync
        def _(sp):
            for slot in range(2):
                sp.dma_start(token[:, slot, :], k.ctx_tok[slot]).then_inc(token_loaded[slot], 16)
            sp.dma_start(mask_u8[:], k.mask.rearrange("(a n) s -> a (n s)", a=1)).then_inc(mask_loaded, 16)
            for t, name in ((wq, "pq"), (wl, "pl"), (wo, "po")):
                sp.dma_start(t[:], w[name].rearrange("(c p) n -> p c n", p=P)).then_inc(w_loaded, 16)
            sp.dma_start(wc[:, 0, :], w["pc"][0:P, :]).then_inc(w_loaded, 16)
            sp.dma_start(wc[0:C1, 1, :], w["pc"][P:C, :]).then_inc(w_loaded, 16)
            with sp.Fori(1, N // 2) as pair:
                for slot in range(2):
                    sp.wait_ge(xn_ready, 2 * pair + slot - 1)
                    sp.dma_start(token[:, slot, :], k.ctx_tok[bass.ds(2 * pair + slot, 1)].rearrange(
                        "a s c -> (a s) c")).then_inc(token_loaded[slot], 16)

        @block.gpsimd
        def _(pool):
            nc.gpsimd.memset(v1[:], 1.0).then_inc(one_set, 1)
            nc.gpsimd.memset(allowed[:], 0.0).then_inc(allowed_zero, 1)

            def work(st):
                if st.has(0):
                    n = st.n(0)
                    hold(pool, mv_ready, n + 1)
                    nc.gpsimd.tensor_scalar(rstd[:], mv[:, :, 1], EPS, 1.0, ALU.add, ALU.mult).then_inc(root_steps, 1)
                    pool.wait_ge(root_steps, 7 * n + 1)
                    nc.gpsimd.tensor_tensor(rstd[:], rstd[:], k.const("power"), ALU.pow).then_inc(root_steps, 1)
                    pool.wait_ge(root_steps, 7 * n + 2)
                    nc.gpsimd.tensor_tensor(var2[:], rstd[:, 0:1], rstd[:, 0:1], ALU.mult).then_inc(root_steps, 1)
                    pool.wait_ge(root_steps, 7 * n + 3)
                    nc.gpsimd.tensor_tensor(var2[:], mv[:, 0, 1:2], var2[:], ALU.mult).then_inc(root_steps, 1)
                    hold(pool, root_steps, 7 * n + 4)
                    nc.gpsimd.tensor_scalar(rstd2[:], var2[:], EPS, 1.0, ALU.add, ALU.mult).then_inc(root_steps, 1)
                    pool.wait_ge(root_steps, 7 * n + 5)
                    nc.gpsimd.tensor_tensor(rstd2[:], rstd2[:], k.const("power")[:, 0:1], ALU.pow).then_inc(
                        root_steps, 1)
                    pool.wait_ge(root_steps, 7 * n + 6)
                    nc.gpsimd.tensor_tensor(rstd[:, 0:1], rstd[:, 0:1], rstd2[:], ALU.mult).then_inc(root_steps, 1)
                if st.has(1):
                    n = st.n(1)
                    pool.wait_ge(ss_ready, n + 1)
                    nc.gpsimd.tensor_tensor(norm[:], norm[:], k.const("root"), ALU.pow).then_inc(norm_steps, 1)

            pipeline(pool, N, 1, work)

        @block.scalar
        def _(act):
            act.wait_ge(one_set, 1)

            def work(st):
                if st.has(1):
                    n = st.n(1)
                    act.wait_ge(in_ready, n + 1)
                    after(act, proj_ready, n)
                    for i, (gain, shift, j, rows) in enumerate((("lg", "lb", 0, P), ("lg", "lb", 1, P),
                                                                ("xg", "xb", 0, P), ("xg", "xb", 1, C1))):
                        t = nc.scalar.activation(in_t[0:rows, i, :], p_in[0:rows, i * P:(i + 1) * P], ACT.Identity,
                                                 bias=k.col(shift, j, rows), scale=k.col(gain, j, rows))
                    t.then_inc(in_copied, 1)
                if st.has(2):
                    n = st.n(2)
                    act.wait_ge(qkt_ready, n + 1)
                    after(act, s_ready, 2 * n)
                    nc.scalar.activation(q_t[:], halves(p_q[:, D:2 * D]), ACT.Copy, scale=k.col("qn"))
                    nc.scalar.activation(k_t[:].rearrange("p a b c -> p (a b) c"), halves(p_k[:]), ACT.Copy,
                                         scale=k.col("kn")).then_inc(qkt_copied, 1)
                if st.has(3):
                    n = st.n(3)
                    act.wait_ge(att_t_ready, n + 1)
                    after(act, o_ready, n)
                    nc.scalar.copy(att_t[:], halves(p_k[:, 0:D])).then_inc(att_t_copied, 1)
                if st.has(1):
                    n, s = st.n(1), st.slot(1)
                    act.wait_ge(proj_ready, n + 1)
                    after(act, ss_ready, n)
                    for i, src in enumerate((p_q, p_l, p_c)):
                        t = nc.scalar.activation(square[:, i * XH:(i + 1) * XH, :],
                                                 src[:, 0:D].rearrange("p (h c) -> p h c", c=XD), ACT.Square)
                    t.then_inc(sq_ready, 1)
                    after(act, pv_ready, n - 1)
                    for i, src in enumerate((p_c, p_l)):
                        t = nc.scalar.copy(v1[:, s, i, :, 0:XD], src[:, D:2 * D].rearrange("p (h c) -> p h c", c=XD))
                    t.then_inc(v_copied, 1)
                if st.has(2):
                    n = st.n(2)
                    for i in range(2):
                        act.wait_ge(sub_ready, 2 * n + i + 1)
                        nc.scalar.activation(prob[:, i, :], prob[:, i, :], ACT.Exp, scale=XD ** -0.5).then_inc(
                            exp_ready, 1)
                    for i in range(2):
                        act.wait_ge(pt_ready, 2 * n + i + 1)
                        after(act, pv_ready, n)
                        nc.scalar.copy(prob_t[:, i, :], p_s[i][:]).then_inc(pt_copied, 1)

            pipeline(act, N, 3, work)

        @block.vector
        def _(dve):
            dve.wait_ge(mask_loaded, 16)
            dve.wait_ge(allowed_zero, 1)
            nc.vector.tensor_scalar(allowed[0:1].rearrange("p n s -> p (n s)"), mask_u8[:], -1.0, -FAR, ALU.add,
                                    ALU.mult).then_inc(allowed_ready, 1)

            def work(st):
                if st.has(0):
                    n, s = st.n(0), st.slot(0)
                    nc.vector.bn_stats(stats[:, 0, :], row(k.x, n))
                    dve.wait_ge(token_loaded[s], 16 * (st.use(0) + 1))
                    nc.vector.bn_stats(stats[:, 1, :], token[:, s, :]).then_inc(ln, 1)
                    after(dve, xn_ready, n)
                    hold(dve, ln, n + 1)
                    nc.vector.bn_aggr(mv[:, 0, :], stats[:, 0, :])
                    nc.vector.bn_aggr(mv[:, 1, :], stats[:, 1, :]).then_inc(mv_ready, 1)
                if st.has(1):
                    n = st.n(1)
                    dve.wait_ge(sq_ready, n + 1)
                    nc.vector.tensor_reduce(norm[:], square[:], AX.X, ALU.add).then_inc(ss_ready, 1)
                if st.has(2):
                    n = st.n(2)
                    for i in range(2):
                        sc = p_s[i][:].rearrange("p (a b) -> p a b", b=2 * P)
                        dve.wait_ge(s_ready, 2 * n + i + 1)
                        nc.vector.tensor_reduce(smax[:, i, :], sc, AX.X, ALU.max).then_inc(max_ready, 1)
                        dve.wait_ge(max_ready, 2 * n + i + 1)
                        after(dve, pt_ready, 2 * (n - 1) + i + 1)
                        nc.vector.tensor_tensor(prob[:, i, :].rearrange("p (a b) -> p a b", b=2 * P), sc,
                                                smax[:, i, :].unsqueeze(2).to_broadcast([P, 2, 2 * P]),
                                                ALU.subtract).then_inc(sub_ready, 1)
                if st.has(1):
                    n = st.n(1)
                    dve.wait_ge(norm_steps, n + 1)
                    nc.vector.tensor_scalar(norm[:], norm[:], XD ** -0.5, 1e-8, ALU.mult, ALU.max).then_inc(
                        rnorm_ready, 1)
                    dve.wait_ge(rnorm_ready, 2 * n + 1)
                    nc.vector.reciprocal(norm[:], norm[:]).then_inc(rnorm_ready, 1)
                    dve.wait_ge(rnorm_ready, 2 * n + 2)
                    dve.wait_ge(v_copied, n + 1)
                    after(dve, qkt_ready, n)
                    for i, src in enumerate((p_q, p_l, p_c)):
                        t = nc.vector.tensor_tensor(
                            qk[:, i * XH:(i + 1) * XH, :], src[:, 0:D].rearrange("p (h c) -> p h c", c=XD),
                            norm[:, i * XH:(i + 1) * XH].unsqueeze(2).to_broadcast([P, XH, XD]), ALU.mult)
                    t.then_inc(qk_ready, 1)
                if st.has(3):
                    n = st.n(3)
                    dve.wait_ge(o_ready, n + 1)
                    nc.vector.tensor_tensor(row(k.x, n), p_k[:, D:2 * D], row(k.x, n), ALU.add).then_inc(x_ready, 1)
                if st.has(0):
                    n, s = st.n(0), st.slot(0)
                    dve.wait_ge(root_steps, 7 * n + 7)
                    after(dve, in_ready, n)
                    nc.vector.tensor_scalar(xn[:], row(k.x, n), mv[:, 0, 0:1], rstd[:, 0:1], ALU.subtract, ALU.mult)
                    nc.vector.tensor_scalar(cn[:], token[:, s, :], mv[:, 1, 0:1], rstd[:, 1:2], ALU.subtract,
                                            ALU.mult).then_inc(xn_ready, 1)
                if st.has(2):
                    n = st.n(2)
                    pv = p_pv[:, 0:XH * (XD + 1)].rearrange("p (h c) -> p h c", c=XD + 1)
                    dve.wait_ge(pv_ready, n + 1)
                    nc.vector.reciprocal(rsum[:], pv[:, :, XD]).then_inc(rsum_ready, 1)
                    dve.wait_ge(rsum_ready, n + 1)
                    after(dve, att_t_ready, n)
                    nc.vector.tensor_tensor(att[:].rearrange("p (h c) -> p h c", c=XD), pv[:, :, 0:XD],
                                            rsum[:].unsqueeze(2).to_broadcast([P, XH, XD]), ALU.mult).then_inc(
                        att_ready, 1)

            pipeline(dve, N, 3, work)

        @block.tensor
        def _(pe):
            pe.wait_ge(w_loaded, 16 * 5)
            pe.wait_ge(allowed_ready, 1)
            ident = k.const("ident")

            def work(st):
                if st.has(1):
                    n = st.n(1)
                    pe.wait_ge(xn_ready, n + 1)
                    after(pe, in_copied, n)
                    nc.tensor.transpose(p_in[:, 0:P], xn[:, 0:P], ident)
                    nc.tensor.transpose(p_in[:, P:2 * P], xn[:, P:D], ident)
                    nc.tensor.transpose(p_in[:, 2 * P:3 * P], cn[:, 0:P], ident)
                    nc.tensor.transpose(p_in[0:C1, 3 * P:4 * P], cn[:, P:C], ident).then_inc(in_ready, 1)
                if st.has(2):
                    n = st.n(2)
                    pe.wait_ge(qk_ready, n + 1)
                    after(pe, qkt_copied, n)
                    after(pe, x_ready, n - 1)
                    flat = qk[:].rearrange("p h c -> p (h c)")
                    for m in range(2):
                        nc.tensor.transpose(p_q[:, D + m * P:D + (m + 1) * P], flat[:, m * P:(m + 1) * P], ident)
                        for i, src in enumerate((2, 1)):
                            t = nc.tensor.transpose(p_k[:, (2 * m + i) * P:(2 * m + i + 1) * P],
                                                    flat[:, src * D + m * P:src * D + (m + 1) * P], ident)
                    t.then_inc(qkt_ready, 1)
                if st.has(1):
                    n = st.n(1)
                    pe.wait_ge(in_copied, n + 1)
                    after(pe, qk_ready, n)
                    after(pe, qkt_copied, n)
                    for i in range(KD):
                        nc.tensor.matmul(p_q[:, 0:D], in_t[:, i, :], wq[:, i, :], start=i == 0, stop=i == KD - 1)
                    for i in range(KD):
                        nc.tensor.matmul(p_l[:], in_t[:, i, :], wl[:, i, :], start=i == 0, stop=i == KD - 1)
                    nc.tensor.matmul(p_c[:], in_t[:, 2, :], wc[:, 0, :], start=True, stop=False)
                    nc.tensor.matmul(p_c[:], in_t[0:C1, 3, :], wc[0:C1, 1, :], start=False, stop=True).then_inc(
                        proj_ready, 1)
                if st.has(3):
                    n = st.n(3)
                    pe.wait_ge(att_ready, n + 1)
                    if st.has(2):
                        pe.wait_ge(qkt_copied, n + 2)
                    for c in range(KD):
                        t = nc.tensor.transpose(p_k[:, c * P:(c + 1) * P], att[:, c * P:(c + 1) * P], ident)
                    t.then_inc(att_t_ready, 1)
                if st.has(2):
                    n = st.n(2)
                    pe.wait_ge(qkt_copied, n + 1)
                    after(pe, pt_copied, 2 * n)
                    pe.nop(nofuse=True)
                    for i in range(2):
                        sc = p_s[i][:].rearrange("p (m b) -> p m b", b=2 * P)
                        nc.tensor.matmul(sc[:, :, 0:P], k.const16("ones"), allowed[:, bass.ds(n, 1), :].to_broadcast(
                            [P, 2, P]), start=True, stop=False, skip_group_check=True)
                        rows = slice(i * XD, (i + 1) * XD)
                        for m in range(2):
                            t = nc.tensor.matmul(sc[:, m, :], q_t[rows, m, :],
                                                 k_t[rows, m].rearrange("p a b -> p (a b)"), start=False, stop=m == 1,
                                                 skip_group_check=True)
                        t.then_inc(s_ready, 1)
                if st.has(3):
                    n = st.n(3)
                    pe.wait_ge(att_t_copied, n + 1)
                    o = p_k[:, D:2 * D]
                    nc.tensor.matmul(o, k.ones3, k.bias_row("po"), start=True, stop=False)
                    for i in range(KD):
                        t = nc.tensor.matmul(o, att_t[:, i, :], wo[:, i, :], start=False, stop=i == KD - 1)
                    t.then_inc(o_ready, 1)
                if st.has(2):
                    n, s = st.n(2), st.slot(2)
                    for i in range(2):
                        pe.wait_ge(exp_ready, 2 * n + i + 1)
                        for j in range(4):
                            t = nc.tensor.transpose(p_s[i][:, j * P:(j + 1) * P], prob[:, i, j * P:(j + 1) * P],
                                                    ident)
                        t.then_inc(pt_ready, 1)
                    after(pe, att_ready, n)
                    for i in range(2):
                        pe.wait_ge(pt_copied, 2 * n + i + 1)
                        for m in range(2):
                            h = 2 * m + i
                            for c in range(2):
                                t = nc.tensor.matmul(p_pv[:, h * (XD + 1):(h + 1) * (XD + 1)],
                                                     prob_t[:, i, (2 * m + c) * P:(2 * m + c + 1) * P],
                                                     v1[:, s, c, h, :], start=c == 0, stop=c == 1)
                    t.then_inc(pv_ready, 1)

            pipeline(pe, N, 3, work)


def sentence_experts(k):
    nc, w = k.nc, k.w
    with ExitStack() as ctx:
        def sb(name, shape, dt=F32):
            return ctx.enter_context(nc.sbuf_tensor("s_" + name, shape, dt))

        sem = ctx.enter_context(semaphores(nc, "s_"))

        def ps(name):
            return ctx.enter_context(nc.psum_tensor("s_" + name, [P, 512], F32))

        wr, down, up = sb("wr", [P, KD, E]), sb("down", [P, E, KD, F1]), sb("up", [P, E, D])
        bn_gain, bn_shift = sb("bn_gain", [P, KD]), sb("bn_shift", [P, KD])
        stats, mv = sb("stats", [P, 2, 6]), sb("mv", [P, 2, 2])
        rstd, var2, rstd2 = sb("rstd", [P, 1]), sb("var2", [P, 1]), sb("rstd2", [P, 1])
        z = sb("z", [P, 2, D])
        z_t, z_sum, z_bn = sb("z_t", [P, 2, KD, P]), sb("z_sum", [P, KD]), sb("z_bn", [P, KD, P])
        best, score, total = sb("best", [P, 1]), sb("score", [P, E]), sb("total", [P, 1])
        gate, expert_f, expert_i = sb("gate", [P, 2]), sb("expert_f", [P, 1]), sb("expert_i", [P, 2], I32)
        shifted = sb("shifted", [P, E])
        hidden, hidden_t = sb("hidden", [P, F1]), sb("hidden_t", [P, P])
        result = sb("result", [P, 2, D])
        p_in, p_r, p_h, p_ht, p_y = ps("p_in"), ps("p_r"), ps("p_h"), ps("p_ht"), ps("p_y")
        w_loaded, bn_root, bn_steps, zero_set = sem("w_loaded"), sem("bn_root"), sem("bn_steps"), sem("zero_set")
        ln, mv_ready, root_steps, z_ready = sem("ln"), sem("mv_ready"), sem("root_steps"), sem("z_ready")
        in_ready, in_copied, bn_ready, logits_ready = sem("in_ready"), sem("in_copied"), sem("bn_ready"), sem("logits_ready")
        choice, exp_ready, expert_ready = sem("choice"), sem("exp_ready"), sem("expert_ready")
        h_ready, relu_ready, ht_ready, ht_copied, y_ready = (
            sem("h_ready"), sem("relu_ready"), sem("ht_ready"), sem("ht_copied"), sem("y_ready"))
        out_ready, stored = sem("out_ready"), [sem("stored0"), sem("stored1")]
        block = ctx.enter_context(nc.Block())

        @block.sync
        def _(sp):
            sp.dma_start(wr[:], w["wr"].rearrange("(c p) n -> p c n", p=P)).then_inc(w_loaded, 16)
            sp.dma_start(down[:], w["down"].rearrange("e (c p) n -> p e c n", p=P)).then_inc(w_loaded, 16)
            sp.dma_start(up[0:F1], w["up"].rearrange("e p n -> p e n")).then_inc(w_loaded, 16)
            with sp.Fori(0, N // 2) as pair:
                for slot in range(2):
                    n = 2 * pair + slot
                    sp.wait_ge(out_ready, n + 1)
                    sp.dma_start(k.out[bass.ds(n, 1)].rearrange("a s d -> (a s) d"), result[:, slot, :]).then_inc(
                        stored[slot], 16)
            sp.wait_ge(stored[0], 16 * (N // 2))
            sp.wait_ge(stored[1], 16 * (N // 2))

        @block.gpsimd
        def _(pool):
            nc.gpsimd.memset(up[F1:P], 0.0).then_inc(zero_set, 1)
            pool.wait_ge(zero_set, 1)
            nc.gpsimd.memset(hidden_t[F1:P, :], 0.0).then_inc(zero_set, 1)
            pool.wait_ge(zero_set, 2)
            inverse_root(k, pool, bn_gain[:], k.cols[:, COLS["bnv"][0]:COLS["bnv"][0] + 2], bn_root, 0)

            def work(st):
                if st.has(0):
                    n = st.n(0)
                    hold(pool, mv_ready, n + 1)
                    m = mv[:, st.slot(0), 1:2]
                    nc.gpsimd.tensor_scalar(rstd[:], m, EPS, 1.0, ALU.add, ALU.mult).then_inc(root_steps, 1)
                    pool.wait_ge(root_steps, 7 * n + 1)
                    nc.gpsimd.tensor_tensor(rstd[:], rstd[:], k.const("power")[:, 0:1], ALU.pow).then_inc(root_steps, 1)
                    pool.wait_ge(root_steps, 7 * n + 2)
                    nc.gpsimd.tensor_tensor(var2[:], rstd[:], rstd[:], ALU.mult).then_inc(root_steps, 1)
                    pool.wait_ge(root_steps, 7 * n + 3)
                    nc.gpsimd.tensor_tensor(var2[:], m, var2[:], ALU.mult).then_inc(root_steps, 1)
                    hold(pool, root_steps, 7 * n + 4)
                    nc.gpsimd.tensor_scalar(rstd2[:], var2[:], EPS, 1.0, ALU.add, ALU.mult).then_inc(root_steps, 1)
                    pool.wait_ge(root_steps, 7 * n + 5)
                    nc.gpsimd.tensor_tensor(rstd2[:], rstd2[:], k.const("power")[:, 0:1], ALU.pow).then_inc(
                        root_steps, 1)
                    pool.wait_ge(root_steps, 7 * n + 6)
                    nc.gpsimd.tensor_tensor(rstd[:], rstd[:], rstd2[:], ALU.mult).then_inc(root_steps, 1)

            pipeline(pool, N, 1, work)

        @block.scalar
        def _(act):
            act.wait_ge(zero_set, 2)

            def work(st):
                if st.has(1):
                    n, s = st.n(1), st.slot(1)
                    act.wait_ge(in_ready, n + 1)
                    after(act, h_ready, n - 1)
                    after(act, bn_ready, 2 * n)
                    for i in range(KD):
                        t = nc.scalar.activation(z_t[:, s, i, :], p_in[:, i * P:(i + 1) * P], ACT.Identity,
                                                 bias=k.col("fb", i), scale=k.col("fg", i),
                                                 accum_out=z_sum[:, i:i + 1])
                    t.then_inc(in_copied, 1)
                if st.has(2):
                    n, s = st.n(2), st.slot(2)
                    act.wait_ge(h_ready, n + 1)
                    after(act, ht_ready, n)
                    nc.scalar.activation(hidden[:], p_h[:, 0:F1], ACT.Relu).then_inc(relu_ready, 1)
                    act.wait_ge(ht_ready, n + 1)
                    after(act, y_ready, n)
                    nc.scalar.copy(hidden_t[0:F1, :], p_ht[0:F1, 0:P]).then_inc(ht_copied, 1)
                if st.has(1):
                    n = st.n(1)
                    act.wait_ge(choice, 5 * n + 2)
                    nc.scalar.activation(shifted[:], shifted[:], ACT.Exp, accum_out=total[:]).then_inc(exp_ready, 1)

            pipeline(act, N, 2, work)

        @block.vector
        def _(dve):
            link = Steps(dve, bn_steps)
            col = lambda name: k.cols[:, COLS[name][0]:COLS[name][0] + 2]
            dve.wait_ge(bn_root, 2)
            link.then(nc.vector.tensor_tensor(bn_gain[:], bn_gain[:], col("bng"), ALU.mult))
            link.then(nc.vector.tensor_tensor(bn_shift[:], bn_gain[:], col("bnm"), ALU.mult))
            link.then(nc.vector.tensor_tensor(bn_shift[:], col("bnb"), bn_shift[:], ALU.subtract))
            link.then(nc.vector.tensor_scalar(bn_gain[:], bn_gain[:], 1.0 / S, None, ALU.mult))

            def work(st):
                if st.has(0):
                    n, s = st.n(0), st.slot(0)
                    nc.vector.bn_stats(stats[:, s, :], row(k.x, n)).then_inc(ln, 1)
                    hold(dve, ln, n + 1)
                    nc.vector.bn_aggr(mv[:, s, :], stats[:, s, :]).then_inc(mv_ready, 1)
                if st.has(1):
                    n, s = st.n(1), st.slot(1)
                    dve.wait_ge(in_copied, n + 1)
                    after(dve, logits_ready, n)
                    nc.vector.tensor_tensor(z_sum[:], z_sum[:], bn_gain[:], ALU.mult).then_inc(bn_ready, 1)
                    dve.wait_ge(bn_ready, 2 * n + 1)
                    nc.vector.tensor_tensor(z_bn[:], z_sum[:].unsqueeze(2).to_broadcast([P, KD, P]),
                                            bn_shift[:].unsqueeze(2).to_broadcast([P, KD, P]), ALU.add).then_inc(
                        bn_ready, 1)
                if st.has(0):
                    n, s = st.n(0), st.slot(0)
                    dve.wait_ge(root_steps, 7 * n + 7)
                    after(dve, in_ready, n - 1)
                    nc.vector.tensor_scalar(z[:, s, :], row(k.x, n), mv[:, s, 0:1], rstd[:, 0:1], ALU.subtract,
                                            ALU.mult).then_inc(z_ready, 1)
                if st.has(2):
                    n, s = st.n(2), st.slot(2)
                    dve.wait_ge(y_ready, n + 1)
                    after(dve, stored[s], 16 * st.use(2))
                    nc.vector.scalar_tensor_tensor(out=result[:, s, :], in0=p_y[:, 0:D], scalar=gate[:, s:s + 1],
                                                   in1=row(k.x, n), op0=ALU.mult, op1=ALU.add).then_inc(out_ready, 1)
                if st.has(1):
                    n, s = st.n(1), st.slot(1)
                    dve.wait_ge(logits_ready, n + 1)
                    nc.vector.tensor_reduce(best[:], p_r[:, 0:E], AX.X, ALU.max).then_inc(choice, 1)
                    dve.wait_ge(choice, 5 * n + 1)
                    after(dve, exp_ready, n)
                    nc.vector.tensor_scalar(shifted[:], p_r[:, 0:E], best[:, 0:1], None, ALU.subtract).then_inc(
                        choice, 1)
                    nc.vector.scalar_tensor_tensor(out=score[:], in0=p_r[:, 0:E], scalar=best[:, 0:1],
                                                   in1=k.const("backward"), op0=ALU.is_ge, op1=ALU.mult).then_inc(
                        choice, 1)
                    dve.wait_ge(choice, 5 * n + 3)
                    nc.vector.tensor_reduce(expert_f[:], score[:], AX.X, ALU.max).then_inc(choice, 1)
                    dve.wait_ge(choice, 5 * n + 4)
                    nc.vector.tensor_scalar(expert_i[:, s:s + 1], expert_f[:], -1.0, float(E), ALU.mult,
                                            ALU.add).then_inc(choice, 1)
                    dve.wait_ge(exp_ready, n + 1)
                    nc.vector.reciprocal(gate[:, s:s + 1], total[:]).then_inc(expert_ready, 1)

            pipeline(dve, N, 2, work)

        @block.tensor
        def _(pe):
            pe.wait_ge(w_loaded, 48)
            ident = k.const("ident")

            def work(st):
                if st.has(1):
                    n, s = st.n(1), st.slot(1)
                    pe.wait_ge(z_ready, n + 1)
                    after(pe, in_copied, n)
                    for c in range(KD):
                        t = nc.tensor.transpose(p_in[:, c * P:(c + 1) * P], z[:, s, c * P:(c + 1) * P], ident)
                    t.then_inc(in_ready, 1)
                if st.has(2):
                    n, s = st.n(2), st.slot(2)
                    after(pe, relu_ready, n)
                    hold(pe, expert_ready, n + 1)
                    e = pe.value_load(expert_i[0:1, s:s + 1], min_val=0, max_val=E - 1)
                    select = k.const16("select")[:, bass.ds(e * P, P)]
                    nc.tensor.matmul(p_h[:, 0:F1], select, k.expert_bias[:, F + D:F + D + F1], start=True, stop=False)
                    for i in range(KD):
                        t = nc.tensor.matmul(p_h[:, 0:F1], z_t[:, s, i, :], down[:, bass.ds(e, 1), i, :].rearrange(
                            "p a n -> p (a n)"), start=False, stop=i == KD - 1)
                    t.then_inc(h_ready, 1)
                    after(pe, ht_copied, n)
                    hold(pe, relu_ready, n + 1)
                    nc.tensor.transpose(p_ht[0:F1, 0:P], hidden[:], ident).then_inc(ht_ready, 1)
                if st.has(1):
                    n = st.n(1)
                    pe.wait_ge(bn_ready, 2 * n + 2)
                    after(pe, expert_ready, n)
                    nc.tensor.matmul(p_r[:, 0:E], k.ones3, k.bias_row("route"), start=True, stop=False)
                    for i in range(KD):
                        t = nc.tensor.matmul(p_r[:, 0:E], z_bn[:, i, :], wr[:, i, :], start=False, stop=i == KD - 1)
                    t.then_inc(logits_ready, 1)
                if st.has(2):
                    n, s = st.n(2), st.slot(2)
                    after(pe, out_ready, n)
                    hold(pe, ht_copied, n + 1)
                    nc.tensor.matmul(p_y[:, 0:D], select, k.expert_bias[:, F + D + F1:], start=True, stop=False)
                    nc.tensor.matmul(p_y[:, 0:D], hidden_t[:], up[:, bass.ds(e, 1), :].rearrange(
                        "p a n -> p (a n)"), start=False, stop=True).then_inc(y_ready, 1)

            pipeline(pe, N, 2, work)


def lay_out(a):
    def c(x):
        return np.ascontiguousarray(x)

    l0, l1 = "L0_attn_", "L1_attn_"
    arrays = {
        "x_seq": c(np.transpose(a["x"], (1, 0, 2)).reshape(B * S, D)),
        "ctx": c(a["ctx_768"]),
        "mask": c(a["mask_BxS2_bk0"]),
        "w_q0": c(a[l0 + "Wq"].T),
        "w_kv0": c(np.concatenate([a[l0 + "Wk"], a[l0 + "Wv"]]).T),
        "w_v_gamma": c(a[l0 + "v_gamma"]), "w_v_beta": c(a[l0 + "v_beta"]),
        "w_xq": c(a["L0_xattn_Wq"]), "w_xk": c(a["L0_xattn_Wk"]), "w_xv": c(a["L0_xattn_Wv"]),
        "w_xo": c(a["L0_xattn_Wo"]),
        "w_gate": c(a["L0_ffn_gate_w"].T),
        "w_w1": c(np.transpose(a["L0_ffn_w1"], (0, 2, 1))), "w_w2": c(np.transpose(a["L0_ffn_w2"], (0, 2, 1))),
        "w_qkv1": c(a[l1 + "Wqkv"].T), "w_out1": c(a[l1 + "Wout"].T),
        "w_pq": c(a["L1_xattn_Wq"].T), "w_pc": c(a["L1_xattn_Wkv"].T), "w_pl": c(a["L1_xattn_Wlkv"].T),
        "w_po": c(a["L1_xattn_Wo"].T),
        "w_wr": c(a["L1_ffn_Wr"]), "w_down": c(a["L1_ffn_W_down"]), "w_up": c(a["L1_ffn_W_up"]),
    }
    bqkv = a[l1 + "bqkv"]
    rows = {"q0": a[l0 + "bq"], "k0": a[l0 + "bk"], "v0": a[l0 + "bv"], "xq": a["L0_xattn_bq"],
            "xk": a["L0_xattn_bk"], "xv": a["L0_xattn_bv"], "xo": a["L0_xattn_bo"], "gate": a["L0_ffn_gate_b"],
            "aq": bqkv[0:D], "ak": bqkv[D:2 * D], "av": bqkv[2 * D:], "ao": a[l1 + "bout"], "po": a["L1_xattn_bo"],
            "route": a["L1_ffn_br"]}
    bias = np.zeros(BIAS_N, np.float32)
    for name, (at, width) in BIAS_AT.items():
        bias[at:at + width] = rows[name]
    arrays["bias"] = bias.reshape(P, BIAS_G)
    arrays["expert_bias"] = c(np.concatenate([a["L0_ffn_b1"], a["L0_ffn_b2"], a["L1_ffn_b_down"],
                                              a["L1_ffn_b_up"]], 1))
    f, p = "L1_ffn_", "L1_xattn_"
    vectors = {"kg": a[l0 + "k_gamma"], "kb": a[l0 + "k_beta"], "xg": a[p + "ln_x_g"], "xb": a[p + "ln_x_b"],
               "lg": a[p + "ln_l_g"], "lb": a[p + "ln_l_b"], "qn": np.concatenate([a[p + "qn_g"]] * 2),
               "kn": np.concatenate([a[p + "kn_g"]] * 2), "fg": a[f + "ln_g"], "fb": a[f + "ln_b"],
               "bng": a[f + "bn_g"], "bnb": a[f + "bn_b"], "bnm": a[f + "bn_mean"], "bnv": a[f + "bn_var"]}
    cols = np.zeros((COLS_N, P), np.float32)
    for name, (at, width) in COLS.items():
        v = vectors[name]
        cols[at:at + width].reshape(-1)[:v.size] = v
    arrays["cols"] = c(cols.T)
    return arrays


def kernel(**inputs):
    import concourse.bacc as bacc
    import ml_dtypes
    from concourse.bass_utils import run_bass_kernel_spmd

    arrays = lay_out({n: np.asarray(v) for n, v in inputs.items()})
    c32, c16 = constants()
    arrays["consts"], arrays["consts16"] = c32, c16.astype(ml_dtypes.bfloat16)
    nc = bacc.Bacc("TRN2", target_bir_lowering=False, num_devices=1)
    aps = {n: nc.dram_tensor("in_" + n, a.shape, mybir.dt.from_np(a.dtype), kind="ExternalInput").ap()
           for n, a in arrays.items()}
    out = nc.dram_tensor("out", (B, S, D), F32, kind="ExternalOutput").ap()
    w = {n[2:]: ap for n, ap in aps.items() if n.startswith("w_")}
    decoder(nc, aps["x_seq"], aps["ctx"], aps["mask"], w, aps["cols"], aps["bias"], aps["expert_bias"],
            aps["consts"], aps["consts16"], out)
    result = run_bass_kernel_spmd(nc, [{"in_" + n: a for n, a in arrays.items()}], core_ids=[0])
    return result.results[0]["out"]
```

```python
from contextlib import ExitStack, contextmanager

import concourse.bass as bass
import numpy as np
from concourse import mybir

ALU = mybir.AluOpType
ACT = mybir.ActivationFunctionType
F32 = mybir.dt.float32
BF16 = mybir.dt.bfloat16
I32 = mybir.dt.int32
U8 = mybir.dt.uint8
AX = mybir.AxisListType

P = 128
B = 16
S = 128
D = 256
C = 192
N = B * S // P
KD = D // P
EPS = 1e-5
FAR = -1e30

QH, QK = 16, 64
H, HD = 16, 16
XH, XD = 4, 64
E, F = 8, 1024
F1 = 64
ROUTED = N + E - 1
WINDOW = 64

BIAS_ROWS = [("q0", QH * QK), ("k0", QK), ("v0", D), ("xq", D), ("xk", D), ("xv", D), ("xo", D), ("gate", E),
             ("aq", D), ("ak", D), ("av", D), ("ao", D), ("po", D), ("route", E)]
BIAS_AT, _n = {}, 0
for _name, _width in BIAS_ROWS:
    BIAS_AT[_name] = (_n, _width)
    _n += _width
BIAS_G = -(-_n // P)
BIAS_N = BIAS_G * P
EXPERT_BIAS = F + D + F1 + D

COLS = {}
for _name, _width in [("kg", 1), ("kb", 1), ("xg", 2), ("xb", 2), ("lg", 2), ("lb", 2), ("qn0", 1), ("qn1", 1), ("kn", 1),
                      ("fg", 2), ("fb", 2), ("bng", 2), ("bnb", 2), ("bnm", 2), ("bnv", 2)]:
    COLS[_name] = (sum(w for _, w in COLS.values()), _width)
COLS_N = sum(w for _, w in COLS.values())

CONSTS = {}
for _name, _width in [("ident", P), ("gram", P), ("parity", 2), ("steps", N), ("before", E * E), ("backward", E),
                      ("tiles", ROUTED + 1), ("power", 2), ("root", 3 * XH)]:
    CONSTS[_name] = (sum(w for _, w in CONSTS.values()), _width)
CONSTS_N = sum(w for _, w in CONSTS.values())
CONSTS16 = {}
for _name, _width in [("ident", P), ("upper", P), ("ones", P), ("window", P), ("select", E * P)]:
    CONSTS16[_name] = (sum(w for _, w in CONSTS16.values()), _width)
CONSTS16_N = sum(w for _, w in CONSTS16.values())


def constants():
    c = np.zeros((P, CONSTS_N), np.float32)

    def put(name, a):
        at, width = CONSTS[name]
        c[:, at:at + width] = a

    row, col = np.arange(P)[:, None], np.arange(P)[None, :]
    put("ident", np.eye(P))
    same = (row // B == col // B) & (row % B <= col % B)
    put("gram", same / np.sqrt(col % B + 1.0) / QH)
    head = np.arange(P) // HD % 2
    put("parity", np.stack([head == 0, head == 1], 1) * (HD ** -0.5))
    put("steps", np.arange(N)[None, :] * P)
    put("before", (np.arange(E)[None, :] < np.arange(E)[:, None]).reshape(1, -1))
    put("backward", E - np.arange(E)[None, :])
    put("power", -0.5)
    put("root", 0.5)
    put("tiles", np.arange(ROUTED + 1)[None, :])
    c16 = np.zeros((P, CONSTS16_N), np.float32)

    def put16(name, a):
        at, width = CONSTS16[name]
        c16[:, at:at + width] = a

    put16("ident", np.eye(P))
    put16("upper", row < col)
    put16("ones", 1.0)
    put16("window", np.where((row >= col) & (row - col < WINDOW), 0.0, FAR))
    select = (row[:, :, None] < 3 * E) & (row[:, :, None] % E == np.arange(E)[None, :, None])
    put16("select", np.broadcast_to(select, (P, E, P)).reshape(P, -1))
    return c, c16


class Step:

    def __init__(self, pair, slot, tiles):
        self.pair, self.parity, self.tiles = pair, slot, tiles
        self.step = 2 * pair + slot

    def starts(self, step):
        return isinstance(self.pair, int) and self.step == step

    def has(self, k):
        return not isinstance(self.pair, int) or 0 <= self.step - k < self.tiles

    def n(self, k):
        return self.step - k

    def slot(self, k):
        return (self.parity - k) % 2

    def use(self, k):
        return self.pair + (self.parity - k) // 2


def pipeline(eng, tiles, lag, work):
    first = -(-(lag + 2) // 2)
    for s in range(2 * first):
        work(Step(s // 2, s % 2, tiles))
    with eng.Fori(first, tiles // 2) as pair:
        for slot in range(2):
            work(Step(pair, slot, tiles))
    for s in range(tiles // 2 * 2, tiles + lag):
        work(Step(s // 2, s % 2, tiles))


@contextmanager
def semaphores(nc, prefix):
    taken = []

    def sem(name):
        taken.append(nc.alloc_semaphore(name=prefix + name))
        return taken[-1]

    yield sem
    nc.clear_and_free_semaphores(taken)
    nc.all_engine_barrier()


def after(eng, sem, count):
    if not isinstance(count, int) or count > 0:
        eng.wait_ge(sem, count)


def hold(eng, sem, count):
    after(eng, sem, count)
    eng.nop(nofuse=True)


def inverse_root(k, pool, out, var, computed, count):
    n = out.shape[1]
    k.nc.gpsimd.tensor_scalar(out, var, EPS, 1.0, ALU.add, ALU.mult).then_inc(computed, 1)
    pool.wait_ge(computed, 2 * count + 1)
    k.nc.gpsimd.tensor_tensor(out, out, k.const("power")[:, 0:n], ALU.pow).then_inc(computed, 1)


def row(t, n):
    return t[:, bass.ds(n, 1), :].rearrange("p a d -> p (a d)")


def halves(t):
    return t.rearrange("p (a b) -> p a b", b=P)


class Core:
    pass


def decoder(nc, x_seq, ctx_tok, mask, w, cols, bias, expert_bias, consts, consts16, out):
    k = Core()
    k.nc, k.w, k.ctx_tok, k.mask, k.out = nc, w, ctx_tok, mask, out
    k.x1_dram = nc.dram_tensor("x1_by_sequence", (B * S, D), F32).ap()
    k.slots_in = nc.dram_tensor("tokens_by_expert", (ROUTED * P, D), F32).ap()
    k.slots_out = nc.dram_tensor("experts_output", (ROUTED * P, D), F32).ap()
    k.bias_dram = nc.dram_tensor("bias_parts", (3, BIAS_N), BF16).ap()
    with ExitStack() as ctx:
        def sb(name, shape, dt=F32):
            return ctx.enter_context(nc.sbuf_tensor(name, shape, dt))

        k.sb_c, k.sb_c16 = sb("constants", [P, CONSTS_N]), sb("constants16", [P, CONSTS16_N], BF16)
        k.cols = sb("cols", [P, COLS_N])
        k.bias = sb("bias_rows", [P, BIAS_N], BF16)
        k.expert_bias = sb("expert_bias", [P, EXPERT_BIAS], BF16)
        k.x = sb("x", [P, N, D])
        k.slot_i = sb("slot_of_token", [P, N], I32)
        k.tile_expert = sb("expert_of_tile", [P, ROUTED + 1], I32)
        k.loaded = {n: ctx.enter_context(nc.semaphore(n + "_loaded")) for n in (
            "consts", "bias", "ffn", "wa1", "fill")}

        def const(name, table=CONSTS, t=k.sb_c):
            at, width = table[name]
            return t[:, at:at + width]

        k.const = const
        k.const16 = lambda name: const(name, CONSTS16, k.sb_c16)
        k.col = lambda name, i=0, rows=P: k.cols[0:rows, COLS[name][0] + i:COLS[name][0] + i + 1]
        k.bias_row = lambda name, a=0, n=None: k.bias[:, BIAS_AT[name][0] + a:BIAS_AT[name][0] + (
            BIAS_AT[name][1] if n is None else a + n)]
        k.ones = k.const16("ones")

        with ExitStack() as first:
            k.w1 = first.enter_context(nc.sbuf_tensor("w1", [P, E, KD, F], F32))
            k.w2 = first.enter_context(nc.sbuf_tensor("w2", [P, E, F // P, D], F32))
            linear_attention(k, x_seq, cols, bias, expert_bias, consts, consts16)
            softmax_attention(k, 0)
            route(k)
            experts(k)
        k.wq1, k.wo1 = sb("wqkv1", [P, KD, 3 * D]), sb("wout1", [P, KD, D])
        softmax_attention(k, 1)
        perceiver(k)
        sentence_experts(k)


def linear_attention(k, x_seq, cols, bias, expert_bias, consts, consts16):
    nc, w = k.nc, k.w
    with ExitStack() as ctx:
        def sb(name, shape, dt=F32):
            return ctx.enter_context(nc.sbuf_tensor("l_" + name, shape, dt))

        sem = ctx.enter_context(semaphores(nc, "l_"))

        def ps(name, cols=512):
            return ctx.enter_context(nc.psum_tensor("l_" + name, [P, cols], F32))

        wq, wkv = sb("wq", [P, KD, QH * QK]), sb("wkv", [P, KD, QK + D])
        v_gain, v_shift = sb("v_gain", [P, D]), sb("v_shift", [P, D])
        bias_f, bias_r = sb("bias_f", [P, BIAS_G]), sb("bias_r", [P, BIAS_G])
        bias_p = sb("bias_p", [P, 3, BIAS_G], BF16)
        eb_f = sb("eb_f", [E, EXPERT_BIAS])
        eb_p = sb("eb_p", [E, EXPERT_BIAS], BF16)
        stats, mv, rstd = sb("stats", [P, 6]), sb("mv", [P, 2]), sb("rstd", [P, 1])
        xn = sb("xn", [P, 2, D])
        xn_t = sb("xn_t", [P, 2, D])
        qmax, qsum = sb("qmax", [P, QH]), sb("qsum", [P, QH])
        qexp = sb("qexp", [P, QH * QK])
        qprob = sb("qprob", [P, QH * QK])
        qk = sb("qk", [P, 2, 2 * QK])
        kvstats, kvmv, kvr = sb("kvstats", [P, 12]), sb("kvmv", [P, 4]), sb("kvr", [P, 2])
        v = sb("v", [P, 2, D])
        qk_t = sb("qk_t", [P, 2, P])
        gram = sb("gram", [P, P])

        p_xt, p_kv, p_qkt, p_out = ps("p_xt"), ps("p_kv"), ps("p_qkt"), ps("p_out")
        p_q = [ps("p_q0", 1024), ps("p_q1", 1024)]

        mv_ready, rstd_steps, kvmv_ready, kvr_steps = (
            sem("mv_ready"), sem("rstd_steps"), sem("kvmv_ready"), sem("kvr_steps"))
        ln, xn_ready, xt_ready, xt_copied = sem("ln"), sem("xn_ready"), sem("xt_ready"), sem("xt_copied")
        q_ready, kv_ready = sem("q_ready"), sem("kv_ready")
        max_ready, sub_ready, exp_ready = sem("max_ready"), sem("sub_ready"), sem("exp_ready")
        sum_ready, rsum_ready, prob_ready, qmean_ready = (
            sem("sum_ready"), sem("rsum_ready"), sem("prob_ready"), sem("qmean_ready"))
        kv_ln, kn_ready, vn_ready, vgain_ready, v_ready = (
            sem("kv_ln"), sem("kn_ready"), sem("vn_ready"), sem("vgain_ready"), sem("v_ready"))
        qkt_ready, qkt_copied = sem("qkt_ready"), sem("qkt_copied")
        gram_ready, gram_masked, att_ready, x1_ready = (
            sem("gram_ready"), sem("gram_masked"), sem("att_ready"), sem("x1_ready"))
        bias_loaded, eb_loaded, x_head, x_loaded = sem("bias_loaded"), sem("eb_loaded"), sem("x_head"), sem("x_loaded")
        wq_loaded, wkv_loaded, stored = sem("wq_loaded"), sem("wkv_loaded"), sem("stored")
        b_hi, b_res, b_mid, b_res2, b_parts = sem("b_hi"), sem("b_res"), sem("b_mid"), sem("b_res2"), sem("b_parts")
        b_stored, eb_moved, v_rows = sem("b_stored"), sem("eb_moved"), sem("v_rows")
        eb_steps, zeroed = sem("eb_steps"), sem("zeroed")
        zero = sb("zero", [P, D])
        block = ctx.enter_context(nc.Block())

        @block.sync
        def _(sp):
            sp.dma_start(bias_f[:], bias).then_inc(bias_loaded, 16)
            sp.dma_start(k.sb_c[:], consts).then_inc(k.loaded["consts"], 16)

            def load_x(a, loaded):
                sp.dma_start(k.x[:, a:a + 4, :], x_seq.rearrange("(n p) d -> p n d", p=P)[:, a:a + 4, :]).then_inc(
                    loaded, 16)

            load_x(0, x_head)
            sp.wait_ge(b_parts, 1)
            for part in range(3):
                sp.dma_start(k.bias_dram[part].rearrange("(p g) -> p g", p=P), bias_p[:, part, :]).then_inc(b_stored, 16)
            sp.dma_start(wkv[:], w["kv0"].rearrange("(c p) n -> p c n", p=P)).then_inc(wkv_loaded, 16)
            sp.wait_ge(b_stored, 48)
            sp.wait_ge(zeroed, 1)
            sp.dma_start(k.bias[0:3, :], k.bias_dram).then_inc(k.loaded["bias"], 16)
            for a in range(4, N, 4):
                load_x(a, x_loaded)
            sp.wait_ge(zeroed, 2)
            for part in range(3):
                sp.wait_ge(eb_steps, 2 * part + 1)
                sp.dma_start(k.expert_bias[part * E:(part + 1) * E, :], eb_p[:]).then_inc(eb_moved, 16)
                sp.wait_ge(eb_moved, 16 * (part + 1))
            for e in range(E):
                sp.dma_start(k.w1[:, e], w["w1"][e].rearrange("(c p) n -> p c n", p=P)).then_inc(k.loaded["ffn"], 16)
                sp.dma_start(k.w2[:, e], w["w2"][e].rearrange("(c p) n -> p c n", p=P)).then_inc(k.loaded["ffn"], 16)
            sp.wait_ge(zeroed, 4)
            for i in range(ROUTED):
                sp.dma_start(k.slots_in[i * P:(i + 1) * P, :], zero[:]).then_inc(k.loaded["fill"], 16)
            with sp.Fori(0, N) as n:
                hold(sp, x1_ready, n + 1)
                sp.dma_start(k.x1_dram[bass.ds(n * P, P), :], row(k.x, n)).then_inc(stored, 16)
            sp.wait_ge(stored, 16 * N)

        @block.gpsimd
        def _(pool):
            nc.gpsimd.memset(k.bias[:].bitcast(F32), 0.0).then_inc(zeroed, 1)
            nc.gpsimd.memset(k.expert_bias[:].bitcast(F32), 0.0).then_inc(zeroed, 1)
            pool.wait_ge(zeroed, 2)
            nc.gpsimd.memset(qk_t[QK:P], 0.0).then_inc(zeroed, 1)
            pool.wait_ge(zeroed, 3)
            nc.gpsimd.memset(zero[:], 0.0).then_inc(zeroed, 1)
            pool.wait_ge(k.loaded["consts"], 48)

            def work(st):
                if st.has(0):
                    n = st.n(0)
                    hold(pool, mv_ready, n + 1)
                    inverse_root(k, pool, rstd[:], mv[:, 1:2], rstd_steps, n)
                if st.has(2):
                    n, s = st.n(2), st.slot(2)
                    hold(pool, kvmv_ready, n + 1)
                    inverse_root(k, pool, kvr[:], kvmv[:].rearrange("p (a b) -> p a b", b=2)[:, :, 1], kvr_steps, n)
                    if st.starts(2):
                        pool.wait_ge(v_rows, 32)
                    pool.wait_ge(vn_ready, n + 1)
                    nc.gpsimd.tensor_tensor(v[:, s, :], v[:, s, :], v_gain[:], ALU.mult).then_inc(vgain_ready, 1)
                    pool.wait_ge(vgain_ready, n + 1)
                    nc.gpsimd.tensor_tensor(v[:, s, :], v[:, s, :], v_shift[:], ALU.add).then_inc(v_ready, 1)
                    pool.wait_ge(rsum_ready, n + 1)
                    after(pool, qmean_ready, n)
                    nc.gpsimd.tensor_tensor(
                        qprob[:].rearrange("p (h k) -> p h k", k=QK), qexp[:].rearrange("p (h k) -> p h k", k=QK),
                        qsum[:].unsqueeze(2).to_broadcast([P, QH, QK]), ALU.mult).then_inc(prob_ready, 1)

            pipeline(pool, N, 4, work)

        @block.scalar
        def _(act):
            act.dma_start(k.sb_c16[:], consts16).then_inc(k.loaded["consts"], 16)
            act.dma_start(k.cols[:], cols).then_inc(k.loaded["consts"], 16)
            act.dma_start(wq[:], w["q0"].rearrange("(c p) n -> p c n", p=P)).then_inc(wq_loaded, 16)
            act.dma_start(eb_f[:], expert_bias).then_inc(eb_loaded, 16)
            act.dma_start(v_gain[:], w["v_gamma"].partition_broadcast(P)).then_inc(v_rows, 16)
            act.dma_start(v_shift[:], w["v_beta"].partition_broadcast(P)).then_inc(v_rows, 16)
            act.wait_ge(k.loaded["consts"], 48)

            def work(st):
                if st.has(1):
                    n = st.n(1)
                    act.wait_ge(xt_ready, n + 1)
                    after(act, kv_ready, n - 1)
                    nc.scalar.copy(xn_t[:, st.slot(1), :], p_xt[:, 0:D]).then_inc(xt_copied, 1)
                if st.has(2):
                    n = st.n(2)
                    act.wait_ge(sub_ready, n + 1)
                    nc.scalar.activation(qexp[:], qexp[:], ACT.Exp).then_inc(exp_ready, 1)
                if st.has(3):
                    n = st.n(3)
                    act.wait_ge(qkt_ready, n + 1)
                    after(act, gram_ready, n)
                    nc.scalar.copy(qk_t[0:QK, 0, :], p_qkt[0:QK, 0:P])
                    nc.scalar.activation(qk_t[0:QK, 1, :], p_qkt[0:QK, P:2 * P], ACT.Identity, bias=k.col("kb", rows=QK),
                                         scale=k.col("kg", rows=QK)).then_inc(qkt_copied, 1)

            pipeline(act, N, 4, work)

        @block.vector
        def _(dve):
            dve.wait_ge(bias_loaded, 16)
            nc.vector.tensor_copy(bias_p[:, 0, :], bias_f[:]).then_inc(b_hi, 1)
            dve.wait_ge(b_hi, 1)
            nc.vector.tensor_tensor(bias_r[:], bias_f[:], bias_p[:, 0, :], ALU.subtract).then_inc(b_res, 1)
            dve.wait_ge(b_res, 1)
            nc.vector.tensor_copy(bias_p[:, 1, :], bias_r[:]).then_inc(b_mid, 1)
            dve.wait_ge(b_mid, 1)
            nc.vector.tensor_tensor(bias_r[:], bias_r[:], bias_p[:, 1, :], ALU.subtract).then_inc(b_res2, 1)
            dve.wait_ge(b_res2, 1)
            nc.vector.tensor_copy(bias_p[:, 2, :], bias_r[:]).then_inc(b_parts, 1)
            dve.wait_ge(eb_loaded, 16)
            for part in range(3):
                after(dve, eb_steps, 2 * part)
                after(dve, eb_moved, 16 * part)
                nc.vector.tensor_copy(eb_p[:], eb_f[:]).then_inc(eb_steps, 1)
                if part < 2:
                    dve.wait_ge(eb_steps, 2 * part + 1)
                    nc.vector.tensor_tensor(eb_f[:], eb_f[:], eb_p[:], ALU.subtract).then_inc(eb_steps, 1)
            dve.wait_ge(k.loaded["consts"], 48)
            dve.wait_ge(x_head, 16)

            def work(st):
                if st.has(4):
                    n = st.n(4)
                    dve.wait_ge(gram_ready, n + 1)
                    after(dve, att_ready, n)
                    nc.vector.tensor_tensor(gram[:], p_out[:, D:D + P], k.const("gram"), ALU.mult).then_inc(
                        gram_masked, 1)
                if st.has(0):
                    n, s = st.n(0), st.slot(0)
                    if st.starts(4):
                        dve.wait_ge(x_loaded, 16 * (N // 4 - 1))
                    nc.vector.bn_stats(stats[:], row(k.x, n)).then_inc(ln, 1)
                    after(dve, xn_ready, n)
                    hold(dve, ln, n + 1)
                    nc.vector.bn_aggr(mv[:], stats[:]).then_inc(mv_ready, 1)
                if st.has(2):
                    n, s = st.n(2), st.slot(2)
                    q3 = p_q[s][:].rearrange("p (h k) -> p h k", k=QK)
                    e3 = qexp[:].rearrange("p (h k) -> p h k", k=QK)
                    dve.wait_ge(kv_ready, n + 1)
                    nc.vector.bn_stats(kvstats[:, 0:6], p_kv[:, 0:QK])
                    nc.vector.bn_stats(kvstats[:, 6:12], p_kv[:, QK:QK + D]).then_inc(kv_ln, 1)
                    hold(dve, kv_ln, n + 1)
                    nc.vector.bn_aggr(kvmv[:, 0:2], kvstats[:, 0:6])
                    nc.vector.bn_aggr(kvmv[:, 2:4], kvstats[:, 6:12]).then_inc(kvmv_ready, 1)
                    nc.vector.tensor_reduce(qmax[:], q3, AX.X, ALU.max).then_inc(max_ready, 1)
                    dve.wait_ge(max_ready, n + 1)
                    after(dve, prob_ready, n)
                    nc.vector.tensor_tensor(e3, q3, qmax[:].unsqueeze(2).to_broadcast([P, QH, QK]),
                                            ALU.subtract).then_inc(sub_ready, 1)
                if st.has(3):
                    n, s = st.n(3), st.slot(3)
                    dve.wait_ge(prob_ready, n + 1)
                    nc.vector.tensor_reduce(qk[:, s, 0:QK], qprob[:].rearrange("p (h k) -> p k h", k=QK), AX.X,
                                            ALU.add).then_inc(qmean_ready, 1)
                if st.has(0):
                    n, s = st.n(0), st.slot(0)
                    dve.wait_ge(rstd_steps, 2 * n + 2)
                    after(dve, xt_ready, n - 1)
                    nc.vector.tensor_scalar(xn[:, s, :], row(k.x, n), mv[:, 0:1], rstd[:, 0:1], ALU.subtract,
                                            ALU.mult).then_inc(xn_ready, 1)
                if st.has(4):
                    n = st.n(4)
                    dve.wait_ge(att_ready, n + 1)
                    nc.vector.tensor_tensor(row(k.x, n), p_out[:, 0:D], row(k.x, n), ALU.add).then_inc(x1_ready, 1)
                if st.has(2):
                    n, s = st.n(2), st.slot(2)
                    dve.wait_ge(kvr_steps, 2 * n + 2)
                    after(dve, qkt_ready, n - 1)
                    nc.vector.tensor_scalar(qk[:, s, QK:2 * QK], p_kv[:, 0:QK], kvmv[:, 0:1], kvr[:, 0:1],
                                            ALU.subtract, ALU.mult).then_inc(kn_ready, 1)
                    after(dve, att_ready, n - 1)
                    nc.vector.tensor_scalar(v[:, s, :], p_kv[:, QK:QK + D], kvmv[:, 2:3], kvr[:, 1:2], ALU.subtract,
                                            ALU.mult).then_inc(vn_ready, 1)
                    dve.wait_ge(exp_ready, n + 1)
                    nc.vector.tensor_reduce(qsum[:], e3, AX.X, ALU.add).then_inc(sum_ready, 1)
                    dve.wait_ge(sum_ready, n + 1)
                    nc.vector.reciprocal(qsum[:], qsum[:]).then_inc(rsum_ready, 1)

            pipeline(dve, N, 4, work)

        @block.tensor
        def _(pe):
            pe.wait_ge(k.loaded["consts"], 48)
            pe.wait_ge(zeroed, 3)

            def work(st):
                def project_q(c):
                    n, s = st.n(1), st.slot(1)
                    xt, o = halves(xn_t[:, s, :]), p_q[s][:, c * 512:(c + 1) * 512]
                    nc.tensor.matmul(o, k.ones, k.bias_row("q0", c * 512, 512), start=True, stop=False)
                    for i in range(KD):
                        t = nc.tensor.matmul(o, xt[:, i, :], wq[:, i, c * 512:(c + 1) * 512], start=False,
                                             stop=i == KD - 1)
                    return t

                if st.has(1):
                    n, s = st.n(1), st.slot(1)
                    pe.wait_ge(xn_ready, n + 1)
                    after(pe, xt_copied, n)
                    for c in range(KD):
                        t = nc.tensor.transpose(p_xt[:, c * P:(c + 1) * P], xn[:, s, c * P:(c + 1) * P],
                                                k.const("ident"))
                    t.then_inc(xt_ready, 1)
                if st.has(4):
                    n, s = st.n(4), st.slot(4)
                    pe.wait_ge(gram_masked, n + 1)
                    pe.wait_ge(v_ready, n + 1)
                    nc.tensor.matmul(p_out[:, 0:D], gram[:], v[:, s, :], start=True, stop=True).then_inc(att_ready, 1)
                if st.has(1):
                    n = st.n(1)
                    if st.starts(1):
                        pe.wait_ge(wq_loaded, 16)
                        pe.wait_ge(k.loaded["bias"], 16)
                    pe.wait_ge(xt_copied, n + 1)
                    after(pe, sub_ready, n - 1)
                    project_q(0)
                    project_q(1).then_inc(q_ready, 1)
                if st.has(3):
                    n, s = st.n(3), st.slot(3)
                    pe.wait_ge(qmean_ready, n + 1)
                    after(pe, qkt_copied, n)
                    hold(pe, kn_ready, n + 1)
                    for c in range(2):
                        t = nc.tensor.transpose(p_qkt[0:QK, c * P:(c + 1) * P], qk[:, s, c * QK:(c + 1) * QK],
                                                k.const("ident"))
                    t.then_inc(qkt_ready, 1)
                if st.has(1):
                    n, s = st.n(1), st.slot(1)
                    xt, o = halves(xn_t[:, s, :]), p_kv[:, 0:QK + D]
                    if st.starts(1):
                        pe.wait_ge(wkv_loaded, 16)
                    after(pe, vn_ready, n)
                    nc.tensor.matmul(o, k.ones, k.bias[:, BIAS_AT["k0"][0]:BIAS_AT["k0"][0] + QK + D], start=True,
                                     stop=False)
                    for i in range(KD):
                        t = nc.tensor.matmul(o, xt[:, i, :], wkv[:, i, :], start=False, stop=i == KD - 1)
                    t.then_inc(kv_ready, 1)
                if st.has(3):
                    n = st.n(3)
                    pe.wait_ge(qkt_copied, n + 1)
                    after(pe, x1_ready, n)
                    nc.tensor.matmul(p_out[:, D:D + P], qk_t[:, 1, :], qk_t[:, 0, :], start=True,
                                     stop=True).then_inc(gram_ready, 1)

            pipeline(pe, N, 4, work)


def softmax_attention(k, layer):
    nc, w = k.nc, k.w
    cross = layer == 0
    with ExitStack() as ctx:
        def sb(name, shape, dt=F32):
            return ctx.enter_context(nc.sbuf_tensor(f"a{layer}_" + name, shape, dt))

        sem = ctx.enter_context(semaphores(nc, f"a{layer}_"))

        def ps(name):
            return ctx.enter_context(nc.psum_tensor(f"a{layer}_" + name, [P, 512], F32))

        STRIPS = 4
        MOVED = 2
        KC = 4 if cross else 2
        if cross:
            wq, wk, wv, wo = (sb("w" + c, [P, KD, D]) for c in "qkvo")
            token = sb("token", [P, 2, C])
        else:
            wq, wk, wv, wo = k.wq1[:, :, 0:D], k.wq1[:, :, D:2 * D], k.wq1[:, :, 2 * D:3 * D], k.wo1
            moe = sb("moe", [P, 2, D])
        stats, mv, rstd = sb("stats", [P, 6]), sb("mv", [P, 2]), sb("rstd", [P, 1])
        xn = sb("xn", [P, 2, D])
        in_t = sb("in_t", [P, KC, P])
        q_t = sb("q_t", [P, 2, 2, P])
        q_pad = sb("q_pad", [P, STRIPS, 2, 2, P])
        k_t = sb("k_t", [P, 2, 2, P])
        v1 = sb("v1", [P, 2, H, 32])
        smax = sb("smax", [P, 4, STRIPS])
        prob = sb("prob", [P, STRIPS, 512])
        prob_t = sb("prob_t", [P, STRIPS, 512])
        rsum = sb("rsum", [P, H])
        pv_t = sb("pv_t", [P, 512])
        att, att_t = pv_t[:, 0:D], halves(pv_t[:, D:2 * D])

        p_s = [ps(f"p_s{i}") for i in range(STRIPS)]
        p_in, p_qk, p_vo, p_pv = ps("p_in"), ps("p_qk"), ps("p_vo"), ps("p_pv")

        w_loaded, x_loaded = sem("w_loaded"), sem("x_loaded")
        token_loaded = [sem("token0"), sem("token1")]
        mv_ready, rstd_steps = sem("mv_ready"), sem("rstd_steps")
        one_set, x_summed, ln, xn_ready = sem("one_set"), sem("x_summed"), sem("ln"), sem("xn_ready")
        in_ready, in_copied, qk_ready, q_copied, k_copied = (
            sem("in_ready"), sem("in_copied"), sem("qk_ready"), sem("q_copied"), sem("k_copied"))
        pad_zero, q_placed = sem("pad_zero"), sem("q_placed")
        pvt_copied, turned_back = sem("pvt_copied"), sem("turned_back")
        v_ready, v_copied = sem("v_ready"), sem("v_copied")
        s_ready, max_ready, sub_ready, exp_ready = sem("s_ready"), sem("max_ready"), sem("sub_ready"), sem("exp_ready")
        pt_ready, pt_copied, pt_moved, pv_ready = sem("pt_ready"), sem("pt_copied"), sem("pt_moved"), sem("pv_ready")
        rsum_ready, att_ready, att_t_ready, att_t_copied = (
            sem("rsum_ready"), sem("att_ready"), sem("att_t_ready"), sem("att_t_copied"))
        o_ready, x_ready = sem("o_ready"), sem("x_ready")
        block = ctx.enter_context(nc.Block())

        @block.sync
        def _(sp):
            if cross:
                for slot in range(2):
                    sp.dma_start(token[:, slot, :], k.ctx_tok[slot]).then_inc(token_loaded[slot], 16)
                for a in range(0, N, 4):
                    sp.dma_start(k.x[:, a:a + 4, :], k.x1_dram.rearrange("(s n) d -> s n d", n=N)[:, a:a + 4, :]
                                 ).then_inc(x_loaded, 16)
                for t, name in ((wq, "xq"), (wo, "xo")):
                    sp.dma_start(t[:], w[name].rearrange("(c p) n -> p c n", p=P)).then_inc(w_loaded, 16)
                for t, name in ((wk, "xk"), (wv, "xv")):
                    sp.dma_start(t[:, 0, :], w[name][0:P, :]).then_inc(w_loaded, 16)
                    sp.dma_start(t[0:C - P, 1, :], w[name][P:C, :]).then_inc(w_loaded, 16)
            else:
                sp.dma_start(k.wq1[:], w["qkv1"].rearrange("(c p) n -> p c n", p=P)).then_inc(k.loaded["wa1"], 16)
                sp.dma_start(k.wo1[:], w["out1"].rearrange("(c p) n -> p c n", p=P)).then_inc(k.loaded["wa1"], 16)
            sp.wait_ge(pad_zero, 1)

            def work(st):
                if st.has(1):
                    n = st.n(1)
                    hold(sp, q_copied, n + 1)
                    after(sp, s_ready, STRIPS * n)
                    for i in range(STRIPS):
                        rows = slice(32 * i, 32 * i + 32)
                        sp.dma_start(q_pad[rows, i], q_t[rows]).then_inc(q_placed, 16)
                if cross and st.has(0) and (not isinstance(st.pair, int) or st.pair > 0):
                    n, s = st.n(0), st.slot(0)
                    after(sp, in_ready, n - 1)
                    sp.dma_start(token[:, s, :], k.ctx_tok[bass.ds(n, 1)].rearrange("a s c -> (a s) c")).then_inc(
                        token_loaded[s], 16)

            pipeline(sp, N, 1, work)

        @block.gpsimd
        def _(pool):
            nc.gpsimd.memset(q_pad[:], 0.0).then_inc(pad_zero, 1)
            nc.gpsimd.memset(v1[:], 1.0).then_inc(one_set, 1)

            def gather(n, slot):
                nc.gpsimd.indirect_dma_start(
                    out=moe[:, slot, :], out_offset=None, in_=k.slots_out,
                    in_offset=bass.IndirectOffsetOnAxis(ap=k.slot_i[:, n:n + 1], axis=0)).then_inc(
                    token_loaded[slot], 16)

            if not cross:
                gather(0, 0)
            for n in range(N):
                if not cross and n + 1 < N:
                    after(pool, x_summed, n)
                    gather(n + 1, (n + 1) % 2)
                hold(pool, mv_ready, n + 1)
                inverse_root(k, pool, rstd[:], mv[:, 1:2], rstd_steps, n)

        @block.scalar
        def _(act):
            act.wait_ge(one_set, 1)

            def work(st):
                def exponential(i):
                    act.wait_ge(sub_ready, STRIPS * st.n(2) + i + 1)
                    nc.scalar.activation(prob[:, i, :], prob[:, i, :], ACT.Exp).then_inc(exp_ready, 1)

                if st.has(3):
                    n = st.n(3)
                    act.wait_ge(pv_ready, n + 1)
                    after(act, o_ready, n)
                    nc.scalar.copy(pv_t[:], p_pv[:]).then_inc(pvt_copied, 1)
                if st.has(2):
                    exponential(0)
                if st.has(1):
                    n = st.n(1)
                    act.wait_ge(in_ready, n + 1)
                    after(act, v_ready, n)
                    if cross:
                        nc.scalar.copy(in_t[:, 0:3, :], halves(p_in[:, 0:3 * P]))
                        nc.scalar.copy(in_t[0:C - P, 3, :], p_in[0:C - P, 3 * P:]).then_inc(in_copied, 1)
                    else:
                        nc.scalar.copy(in_t[:], halves(p_in[:, 0:D])).then_inc(in_copied, 1)
                if st.has(2):
                    exponential(1)
                    exponential(2)
                if st.has(1):
                    n, s = st.n(1), st.slot(1)
                    act.wait_ge(q_copied, n + 1)
                    after(act, s_ready, STRIPS * (n - 1))
                    nc.scalar.copy(k_t[:, s], halves(p_qk[:, D:2 * D])).then_inc(k_copied, 1)
                if st.has(1):
                    n, s = st.n(1), st.slot(1)
                    act.wait_ge(v_ready, n + 1)
                    after(act, pv_ready, n - 1)
                    nc.scalar.copy(v1[:, s, :, 0:HD], p_vo[:, 0:D].rearrange("p (h c) -> p h c", c=HD)).then_inc(
                        v_copied, 1)
                if st.has(2):
                    exponential(3)
                if st.has(2):
                    n = st.n(2)
                    after(act, pv_ready, n)
                    for i in (i for i in range(STRIPS) if i != MOVED):
                        act.wait_ge(pt_ready, STRIPS * n + i + 1)
                        nc.scalar.copy(prob_t[:, i, :], p_s[i][:]).then_inc(pt_copied, 1)
                if st.has(3):
                    n = st.n(3)
                    act.wait_ge(att_t_ready, n + 1)
                    nc.scalar.copy(att_t, halves(p_vo[:, 0:D])).then_inc(att_t_copied, 1)

            pipeline(act, N, 3, work)

        @block.vector
        def _(dve):
            if cross:
                dve.wait_ge(x_loaded, 16 * (N // 4))

            def work(st):
                def shift(i):
                    n, sc = st.n(2), halves(p_s[i][:])
                    dve.wait_ge(s_ready, STRIPS * n + i + 1)
                    nc.vector.tensor_reduce(smax[:, :, i], sc, AX.X, ALU.max).then_inc(max_ready, 1)
                    dve.wait_ge(max_ready, STRIPS * n + i + 1)
                    after(dve, pt_ready, STRIPS * (n - 1) + i + 1)
                    nc.vector.tensor_tensor(halves(prob[:, i, :]), sc, smax[:, :, i].unsqueeze(2).to_broadcast(
                        [P, 4, P]), ALU.subtract).then_inc(sub_ready, 1)

                if st.has(2):
                    shift(0)
                    shift(1)
                    shift(2)
                if st.has(0):
                    n, s = st.n(0), st.slot(0)
                    if not cross:
                        dve.wait_ge(token_loaded[s], 16 * (st.use(0) + 1))
                        nc.vector.tensor_tensor(row(k.x, n), moe[:, s, :], row(k.x, n), ALU.add).then_inc(x_summed, 1)
                        hold(dve, x_summed, n + 1)
                    nc.vector.bn_stats(stats[:], row(k.x, n)).then_inc(ln, 1)
                    after(dve, xn_ready, n)
                    hold(dve, ln, n + 1)
                    nc.vector.bn_aggr(mv[:], stats[:]).then_inc(mv_ready, 1)
                if st.has(1):
                    n, s = st.n(1), st.slot(1)
                    dve.wait_ge(qk_ready, n + 1)
                    after(dve, q_placed, 16 * STRIPS * n)
                    for parity in range(2):
                        t = nc.vector.tensor_scalar(q_t[:, parity], halves(p_qk[:, 0:D]),
                                                    k.const("parity")[:, parity:parity + 1], None, ALU.mult)
                    t.then_inc(q_copied, 1)
                if st.has(2):
                    shift(3)
                if st.has(3):
                    n = st.n(3)
                    pv = p_pv[:].rearrange("p (h c) -> p h c", c=32)
                    dve.wait_ge(turned_back, n + 1)
                    nc.vector.reciprocal(rsum[:], pv[:, :, HD]).then_inc(rsum_ready, 1)
                    dve.wait_ge(rsum_ready, n + 1)
                    nc.vector.tensor_tensor(att.rearrange("p (h c) -> p h c", c=HD), pv[:, :, 0:HD],
                                            rsum[:].unsqueeze(2).to_broadcast([P, H, HD]), ALU.mult).then_inc(
                        att_ready, 1)
                if st.has(2):
                    n = st.n(2)
                    dve.wait_ge(pt_ready, STRIPS * n + MOVED + 1)
                    after(dve, pv_ready, n)
                    nc.vector.tensor_copy(prob_t[:, MOVED, :], p_s[MOVED][:]).then_inc(pt_moved, 1)
                if st.has(0):
                    n, s = st.n(0), st.slot(0)
                    dve.wait_ge(rstd_steps, 2 * n + 2)
                    after(dve, in_ready, n - 1)
                    nc.vector.tensor_scalar(xn[:, s, :], row(k.x, n), mv[:, 0:1], rstd[:, 0:1], ALU.subtract,
                                            ALU.mult).then_inc(xn_ready, 1)
                if st.has(3):
                    n = st.n(3)
                    dve.wait_ge(o_ready, n + 1)
                    nc.vector.tensor_tensor(row(k.x, n), p_vo[:, D:2 * D], row(k.x, n), ALU.add).then_inc(x_ready, 1)

            pipeline(dve, N, 3, work)

        @block.tensor
        def _(pe):
            if cross:
                pe.wait_ge(w_loaded, 16 * 6)
            else:
                pe.wait_ge(k.loaded["wa1"], 32)
            names = ("xq", "xk", "xv", "xo") if cross else ("aq", "ak", "av", "ao")
            kv_chunks = [(2, P), (3, C - P)] if cross else [(0, P), (1, P)]

            def project(o, name, at, wt, chunks):
                nc.tensor.matmul(o, k.bias_row(name, at, P), k.ones, start=True, stop=False)
                for i, (chunk, rows) in enumerate(chunks):
                    t = nc.tensor.matmul(o, wt[0:rows, i, at:at + P], in_t[0:rows, chunk, :], start=False,
                                         stop=i == KD - 1)
                return t

            def work(st):
                def score(i):
                    for j in range(4):
                        if j == 0 and not cross:
                            nc.tensor.matmul(halves(p_s[i][:]), k.const16("ident"), k.const16("window").unsqueeze(
                                1).to_broadcast([P, 4, P]), start=True, stop=False, skip_group_check=True)
                        half, parity = j // 2, j % 2
                        t = nc.tensor.matmul(p_s[i][:, j * P:(j + 1) * P], q_pad[:, i, parity, half, :],
                                             k_t[:, st.slot(2), half, :], start=cross, stop=True,
                                             skip_group_check=not cross)
                    t.then_inc(s_ready, 1)

                if st.has(2):
                    n = st.n(2)
                    pe.wait_ge(q_placed, 16 * STRIPS * (n + 1))
                    pe.wait_ge(k_copied, n + 1)
                    after(pe, pt_copied, 3 * n)
                    after(pe, pt_moved, n)
                    score(0)
                    score(1)
                if st.has(1):
                    n, s = st.n(1), st.slot(1)
                    pe.wait_ge(xn_ready, n + 1)
                    after(pe, in_copied, n)
                    for c in range(KD):
                        t = nc.tensor.transpose(p_in[:, c * P:(c + 1) * P], xn[:, s, c * P:(c + 1) * P],
                                                k.const("ident"))
                    if cross:
                        pe.wait_ge(token_loaded[s], 16 * (st.use(1) + 1))
                        nc.tensor.transpose(p_in[:, 2 * P:3 * P], token[:, s, 0:P], k.const("ident"))
                        t = nc.tensor.transpose(p_in[0:C - P, 3 * P:4 * P], token[:, s, P:C], k.const("ident"))
                    t.then_inc(in_ready, 1)
                if st.has(2):
                    score(2)
                    score(3)
                if st.has(1):
                    n, s = st.n(1), st.slot(1)
                    pe.wait_ge(in_copied, n + 1)
                    after(pe, q_copied, n)
                    after(pe, k_copied, n)
                    for c in range(KD):
                        project(p_qk[:, c * P:(c + 1) * P], names[0], c * P, wq, [(0, P), (1, P)])
                    for c in range(KD):
                        t = project(p_qk[:, D + c * P:D + (c + 1) * P], names[1], c * P, wk, kv_chunks)
                    t.then_inc(qk_ready, 1)
                if st.has(3):
                    n = st.n(3)
                    pe.wait_ge(pvt_copied, n + 1)
                    for c in range(4):
                        t = nc.tensor.transpose(p_pv[:, c * P:(c + 1) * P], pv_t[:, c * P:(c + 1) * P],
                                                k.const("ident"))
                    t.then_inc(turned_back, 1)
                if st.has(1):
                    n = st.n(1)
                    after(pe, x_ready, n - 2)
                    o = p_vo[:, 0:D]
                    nc.tensor.matmul(o, k.ones, k.bias_row(names[2]), start=True, stop=False)
                    for i, (chunk, rows) in enumerate(kv_chunks):
                        t = nc.tensor.matmul(o, in_t[0:rows, chunk, :], wv[0:rows, i, :], start=False,
                                             stop=i == KD - 1)
                    t.then_inc(v_ready, 1)
                if st.has(2):
                    n, s = st.n(2), st.slot(2)

                    def turn(i):
                        pe.wait_ge(exp_ready, STRIPS * n + i + 1)
                        for j in range(4):
                            t = nc.tensor.transpose(p_s[i][:, j * P:(j + 1) * P], prob[:, i, j * P:(j + 1) * P],
                                                    k.const("ident"))
                        t.then_inc(pt_ready, 1)

                    for i in range(STRIPS):
                        turn(i)
                if st.has(3):
                    n = st.n(3)
                    pe.wait_ge(att_ready, n + 1)
                    after(pe, v_copied, n + 3 if st.has(1) else N)
                    for c in range(KD):
                        t = nc.tensor.transpose(p_vo[:, c * P:(c + 1) * P], att[:, c * P:(c + 1) * P],
                                                k.const("ident"))
                    t.then_inc(att_t_ready, 1)
                if st.has(2):
                    n, s = st.n(2), st.slot(2)

                    def weigh(i):
                        if i == MOVED:
                            pe.wait_ge(pt_moved, n + 1)
                        else:
                            pe.wait_ge(pt_copied, 3 * n + i + (i < MOVED))
                        for j in range(4):
                            h = 8 * (j // 2) + 2 * i + j % 2
                            at = 32 * (h % 4)
                            t = nc.tensor.matmul(p_pv[at:at + 32, h // 4 * P:(h // 4 + 1) * P], v1[:, s, h, :],
                                                 prob_t[:, i, j * P:(j + 1) * P], start=True, stop=True)
                        return t

                    pe.wait_ge(v_copied, n + 1)
                    after(pe, att_ready, n)
                    for i in range(STRIPS):
                        t = weigh(i)
                    t.then_inc(pv_ready, 1)
                if st.has(3):
                    n = st.n(3)
                    pe.wait_ge(att_t_copied, n + 1)
                    o = p_vo[:, D:2 * D]
                    nc.tensor.matmul(o, k.ones, k.bias_row(names[3]), start=True, stop=False)
                    for i in range(KD):
                        t = nc.tensor.matmul(o, att_t[:, i, :], wo[:, i, :], start=False, stop=i == KD - 1)
                    t.then_inc(o_ready, 1)

            pipeline(pe, N, 3, work)


class Steps:

    def __init__(self, eng, sem):
        self.eng, self.sem, self.count = eng, sem, 0

    def then(self, instruction):
        instruction.then_inc(self.sem, 1)
        self.count += 1
        self.eng.wait_ge(self.sem, self.count)


def route(k):
    nc, w = k.nc, k.w
    with ExitStack() as ctx:
        def sb(name, shape, dt=F32):
            return ctx.enter_context(nc.sbuf_tensor("r_" + name, shape, dt))

        sem = ctx.enter_context(semaphores(nc, "r_"))

        wg = sb("wg", [P, KD, E])
        stats, mv, rstd = sb("stats", [P, 2, 6]), sb("mv", [P, 2, 2]), sb("rstd", [P, 2])
        xn, xn_all, xn_t = sb("xn", [P, 2, D]), sb("xn_all", [P, N, D]), sb("xn_t", [P, 2, D])
        logits, score = sb("logits", [P, N, E]), sb("score", [P, N, E])
        best = sb("best", [P, N])
        chosen, chosen16 = sb("chosen", [P, N, E]), sb("chosen16", [P, N + 1, E], BF16)
        rank = sb("rank", [P, N + 1, E])
        over = sb("over", [P, E, N])
        tiles_of, tri = sb("tiles_of", [P, E]), sb("tri", [P, E, E])
        first, last = sb("first", [P, E]), sb("last", [P, E])
        ends = sb("ends", [P, ROUTED + 1, E])
        tile_f = sb("tile_f", [P, ROUTED + 1])
        slot_f = sb("slot_f", [P, N])
        p_t = [ctx.enter_context(nc.psum_tensor(f"r_p_t{i}", [P, 512], F32)) for i in range(2)]
        p_lg = ctx.enter_context(nc.psum_tensor("r_p_lg", [P, 512], F32))
        p_rank = ctx.enter_context(nc.psum_tensor("r_p_rank", [P, 512], F32))

        w_loaded, ln, mv_ready, rstd_steps, xn_ready = (
            sem("w_loaded"), sem("ln"), sem("mv_ready"), sem("rstd_steps"), sem("xn_ready"))
        xn_kept, t_ready, t_copied, logits_ready = sem("xn_kept"), sem("t_ready"), sem("t_copied"), sem("logits_ready")
        steps, chosen_ready, rank_ready, slots_ready, sent = (
            sem("steps"), sem("chosen_ready"), sem("rank_ready"), sem("slots_ready"), sem("sent"))
        block = ctx.enter_context(nc.Block())

        @block.sync
        def _(sp):
            sp.dma_start(wg[:], w["gate"].rearrange("(c p) n -> p c n", p=P)).then_inc(w_loaded, 16)

        @block.gpsimd
        def _(pool):
            for n in range(N):
                s = n % 2
                pool.wait_ge(mv_ready, n + 1)
                inverse_root(k, pool, rstd[:, s:s + 1], mv[:, s, 1:2], rstd_steps, n)
            pool.wait_ge(slots_ready, 1)
            pool.wait_ge(xn_kept, N)
            pool.wait_ge(k.loaded["fill"], 16 * ROUTED)
            for n in range(N):
                nc.gpsimd.indirect_dma_start(
                    out=k.slots_in, out_offset=bass.IndirectOffsetOnAxis(ap=k.slot_i[:, n:n + 1], axis=0),
                    in_=xn_all[:, n, :], in_offset=None).then_inc(sent, 16)
            pool.wait_ge(sent, 16 * N)

        @block.scalar
        def _(act):
            def work(st):
                if st.has(2):
                    n, s = st.n(2), st.slot(2)
                    act.wait_ge(xn_ready, n + 1)
                    nc.scalar.copy(row(xn_all, n), xn[:, s, :]).then_inc(xn_kept, 1)
                    act.wait_ge(t_ready, n + 1)
                    after(act, logits_ready, n - 1)
                    nc.scalar.copy(xn_t[:, s, :], p_t[s][:, 0:D]).then_inc(t_copied, 1)

            pipeline(act, N, 2, work)

        @block.vector
        def _(dve):
            def work(st):
                if st.has(0):
                    n, s = st.n(0), st.slot(0)
                    nc.vector.bn_stats(stats[:, s, :], row(k.x, n)).then_inc(ln, 1)
                if st.has(1):
                    n, s = st.n(1), st.slot(1)
                    dve.wait_ge(rstd_steps, 2 * n + 2)
                    after(dve, t_ready, n - 1)
                    after(dve, xn_kept, n - 1)
                    nc.vector.tensor_scalar(xn[:, s, :], row(k.x, n), mv[:, s, 0:1], rstd[:, s:s + 1], ALU.subtract,
                                            ALU.mult).then_inc(xn_ready, 1)
                if st.has(0):
                    n, s = st.n(0), st.slot(0)
                    after(dve, xn_ready, n - 1)
                    hold(dve, ln, n + 1)
                    nc.vector.bn_aggr(mv[:, s, :], stats[:, s, :]).then_inc(mv_ready, 1)

            pipeline(dve, N, 2, work)
            chain = Steps(dve, steps)
            by_tile = [P, N, E]
            dve.wait_ge(logits_ready, N)
            chain.then(nc.vector.tensor_copy(logits[:], p_lg[:, 0:N * E].rearrange("p (n e) -> p n e", e=E)))
            chain.then(nc.vector.tensor_reduce(best[:], logits[:], AX.X, ALU.max))
            chain.then(nc.vector.tensor_tensor(score[:], logits[:], best[:].unsqueeze(2).to_broadcast(by_tile),
                                               ALU.is_ge))
            backward = k.const("backward").unsqueeze(1).to_broadcast(by_tile)
            chain.then(nc.vector.tensor_tensor(score[:], score[:], backward, ALU.mult))
            chain.then(nc.vector.tensor_reduce(best[:], score[:], AX.X, ALU.max))
            chain.then(nc.vector.tensor_tensor(chosen[:], backward, best[:].unsqueeze(2).to_broadcast(by_tile),
                                               ALU.is_equal))
            chain.then(nc.vector.memset(chosen16[:], 0.0))
            nc.vector.tensor_copy(chosen16[:, 0:N, :], chosen[:]).then_inc(chosen_ready, 1)
            dve.wait_ge(rank_ready, 1)
            chain.then(nc.vector.tensor_copy(rank[:], p_rank[:, 0:(N + 1) * E].rearrange("p (n e) -> p n e", e=E)))
            chain.then(nc.vector.tensor_tensor(over[:], rank[:, N, :].unsqueeze(2).to_broadcast([P, E, N]),
                                               k.const("steps").unsqueeze(1).to_broadcast([P, E, N]), ALU.is_gt))
            chain.then(nc.vector.tensor_reduce(tiles_of[:], over[:], AX.X, ALU.add))
            chain.then(nc.vector.tensor_tensor(tri[:], k.const("before").rearrange("p (a b) -> p a b", b=E),
                                               tiles_of[:].unsqueeze(1).to_broadcast([P, E, E]), ALU.mult))
            chain.then(nc.vector.tensor_reduce(first[:], tri[:], AX.X, ALU.add))
            chain.then(nc.vector.tensor_tensor(last[:], first[:], tiles_of[:], ALU.add))
            shape = [P, ROUTED + 1, E]
            chain.then(nc.vector.tensor_tensor(ends[:], k.const("tiles").unsqueeze(2).to_broadcast(shape),
                                               last[:].unsqueeze(1).to_broadcast(shape), ALU.is_ge))
            chain.then(nc.vector.tensor_reduce(tile_f[:], ends[:], AX.X, ALU.add))
            chain.then(nc.vector.tensor_scalar(k.tile_expert[:], tile_f[:], float(E - 1), None, ALU.min))
            chain.then(nc.vector.tensor_scalar(first[:], first[:], float(P), None, ALU.mult))
            chain.then(nc.vector.tensor_tensor(rank[:, 0:N, :], rank[:, 0:N, :],
                                               first[:].unsqueeze(1).to_broadcast(by_tile), ALU.add))
            chain.then(nc.vector.tensor_tensor(rank[:, 0:N, :], rank[:, 0:N, :], chosen[:], ALU.mult))
            chain.then(nc.vector.tensor_reduce(slot_f[:], rank[:, 0:N, :], AX.X, ALU.add))
            nc.vector.tensor_copy(k.slot_i[:], slot_f[:]).then_inc(slots_ready, 1)

        @block.tensor
        def _(pe):
            pe.wait_ge(w_loaded, 16)

            def work(st):
                if st.has(2):
                    n, s = st.n(2), st.slot(2)
                    pe.wait_ge(xn_ready, n + 1)
                    after(pe, t_copied, n - 1)
                    for c in range(KD):
                        t = nc.tensor.transpose(p_t[s][:, c * P:(c + 1) * P], xn[:, s, c * P:(c + 1) * P],
                                                k.const("ident"))
                    t.then_inc(t_ready, 1)
                if st.has(3):
                    n, s = st.n(3), st.slot(3)
                    o = p_lg[:, bass.ds(n * E, E)]
                    pe.wait_ge(t_copied, n + 1)
                    pe.nop(nofuse=True)
                    nc.tensor.matmul(o, k.ones, k.bias_row("gate"), start=True, stop=False)
                    xt = halves(xn_t[:, s, :])
                    for i in range(KD):
                        t = nc.tensor.matmul(o, xt[:, i, :], wg[:, i, :], start=False, stop=i == KD - 1)
                    t.then_inc(logits_ready, 1)

            pipeline(pe, N, 3, work)
            pe.wait_ge(chosen_ready, 1)
            nc.tensor.matmul(p_rank[:, 0:(N + 1) * E], k.const16("upper"), chosen16[:].rearrange("p n e -> p (n e)"),
                             start=True, stop=False, skip_group_check=True)
            for n in range(N):
                later = N - n
                t = nc.tensor.matmul(p_rank[:, (n + 1) * E:(N + 1) * E].rearrange("p (n e) -> p n e", e=E),
                                     k.const16("ones"), chosen16[:, n:n + 1, :].to_broadcast([P, later, E]),
                                     start=False, stop=n == N - 1, skip_group_check=True)
            t.then_inc(rank_ready, 1)


def experts(k):
    nc = k.nc
    with ExitStack() as ctx:
        def sb(name, shape, dt=F32):
            return ctx.enter_context(nc.sbuf_tensor("e_" + name, shape, dt))

        sem = ctx.enter_context(semaphores(nc, "e_"))

        def ps(name, cols=512):
            return ctx.enter_context(nc.psum_tensor("e_" + name, [P, cols], F32))

        HC = F // P
        xs, xs_t = sb("xs", [P, 2, D]), sb("xs_t", [P, KD, P])
        hidden, hidden_t = sb("hidden", [P, F]), sb("hidden_t", [P, HC, P])
        y = sb("y", [P, 2, D])
        p_in, p_h, p_ht, p_y = ps("p_in"), ps("p_h", F), ps("p_ht", F), ps("p_y")
        loaded = [sem("loaded0"), sem("loaded1")]
        in_ready, in_copied, h_ready, relu_ready = sem("in_ready"), sem("in_copied"), sem("h_ready"), sem("relu_ready")
        ht_ready, ht_copied, y_ready, y_copied = sem("ht_ready"), sem("ht_copied"), sem("y_ready"), sem("y_copied")
        stored = [sem("stored0"), sem("stored1")]
        block = ctx.enter_context(nc.Block())

        @block.sync
        def _(sp):
            def work(st):
                if st.has(0):
                    n, s = st.n(0), st.slot(0)
                    after(sp, in_ready, n - 1)
                    sp.dma_start(xs[:, s, :], k.slots_in[bass.ds(n * P, P), :]).then_inc(loaded[s], 16)

            pipeline(sp, ROUTED, 1, work)

        @block.gpsimd
        def _(pool):
            def work(st):
                if st.has(1):
                    n, s = st.n(1), st.slot(1)
                    pool.wait_ge(y_copied, n + 1)
                    pool.nop(nofuse=True)
                    pool.dma_start(k.slots_out[bass.ds(n * P, P), :], y[:, s, :]).then_inc(stored[s], 16)

            pipeline(pool, ROUTED, 1, work)
            pool.wait_ge(stored[0], 16 * ((ROUTED + 1) // 2))
            pool.wait_ge(stored[1], 16 * (ROUTED // 2))

        @block.scalar
        def _(act):
            def work(st):
                if st.has(0):
                    n = st.n(0)
                    act.wait_ge(in_ready, n + 1)
                    after(act, h_ready, 2 * n)
                    nc.scalar.copy(xs_t[:], halves(p_in[:, 0:D])).then_inc(in_copied, 1)
                    for c in range(2):
                        act.wait_ge(h_ready, 2 * n + c + 1)
                        after(act, ht_ready, 2 * n)
                        nc.scalar.activation(hidden[:, c * 512:(c + 1) * 512], p_h[:, c * 512:(c + 1) * 512],
                                             ACT.Relu).then_inc(relu_ready, 1)

            pipeline(act, ROUTED, 1, work)

        @block.vector
        def _(dve):
            def work(st):
                if st.has(1):
                    n, s = st.n(1), st.slot(1)
                    for c in range(2):
                        dve.wait_ge(ht_ready, 2 * n + c + 1)
                        after(dve, y_ready, n)
                        nc.vector.tensor_copy(hidden_t[:, 4 * c:4 * c + 4, :],
                                              halves(p_ht[:, c * 512:(c + 1) * 512])).then_inc(ht_copied, 1)
                    dve.wait_ge(y_ready, n + 1)
                    after(dve, stored[s], 16 * st.use(1))
                    nc.vector.tensor_copy(y[:, s, :], p_y[:, 0:D]).then_inc(y_copied, 1)

            pipeline(dve, ROUTED, 1, work)

        @block.tensor
        def _(pe):
            pe.wait_ge(k.loaded["ffn"], 16 * 2 * E)

            def expert_of(n):
                e = pe.value_load(k.tile_expert[0:1, bass.ds(n, 1)], min_val=0, max_val=E - 1)
                return e, k.const16("select")[:, bass.ds(e * P, P)]

            def work(st):
                if st.has(0):
                    n, s = st.n(0), st.slot(0)
                    pe.wait_ge(loaded[s], 16 * (st.use(0) + 1))
                    after(pe, in_copied, n)
                    for c in range(KD):
                        t = nc.tensor.transpose(p_in[:, c * P:(c + 1) * P], xs[:, s, c * P:(c + 1) * P],
                                                k.const("ident"))
                    t.then_inc(in_ready, 1)
                if st.has(1):
                    n = st.n(1)
                    for c in range(2):
                        pe.wait_ge(relu_ready, 2 * n + c + 1)
                        after(pe, ht_copied, 2 * n)
                        for j in range(4 * c, 4 * c + 4):
                            t = nc.tensor.transpose(p_ht[:, j * P:(j + 1) * P], hidden[:, j * P:(j + 1) * P],
                                                    k.const("ident"))
                        t.then_inc(ht_ready, 1)
                if st.has(0):
                    n = st.n(0)
                    e, select = expert_of(n)
                    pe.wait_ge(in_copied, n + 1)
                    pe.nop(nofuse=True)
                    for c in range(2):
                        o = p_h[:, c * 512:(c + 1) * 512]
                        nc.tensor.matmul(o, select, k.expert_bias[:, c * 512:(c + 1) * 512], start=True, stop=False)
                        for i in range(KD):
                            t = nc.tensor.matmul(o, xs_t[:, i, :], k.w1[:, bass.ds(e, 1), i, c * 512:(c + 1) * 512]
                                                 .rearrange("p a n -> p (a n)"), start=False, stop=i == KD - 1)
                        t.then_inc(h_ready, 1)
                if st.has(1):
                    n = st.n(1)
                    e, select = expert_of(n)
                    pe.wait_ge(ht_copied, 2 * n + 2)
                    after(pe, y_copied, n)
                    pe.nop(nofuse=True)
                    nc.tensor.matmul(p_y[:, 0:D], select, k.expert_bias[:, F:F + D], start=True, stop=False)
                    for j in range(HC):
                        t = nc.tensor.matmul(p_y[:, 0:D], hidden_t[:, j, :], k.w2[:, bass.ds(e, 1), j, :].rearrange(
                            "p a n -> p (a n)"), start=False, stop=j == HC - 1)
                    t.then_inc(y_ready, 1)

            pipeline(pe, ROUTED, 1, work)


def perceiver(k):
    nc, w = k.nc, k.w
    with ExitStack() as ctx:
        def sb(name, shape, dt=F32):
            return ctx.enter_context(nc.sbuf_tensor("p_" + name, shape, dt))

        sem = ctx.enter_context(semaphores(nc, "p_"))

        def ps(name):
            return ctx.enter_context(nc.psum_tensor("p_" + name, [P, 512], F32))

        C1 = C - P
        wq, wl, wc, wo = (sb("wq", [P, KD, D]), sb("wl", [P, KD, 2 * D]), sb("wc", [P, KD, 2 * D]),
                          sb("wo", [P, KD, D]))
        mask_u8, allowed = sb("mask_u8", [1, N * S], U8), sb("allowed", [P, N, S], BF16)
        token = sb("token", [P, 2, C])
        stats, mv = sb("stats", [P, 2, 6]), sb("mv", [P, 2, 2])
        rstd, var2, rstd2 = sb("rstd", [P, 2]), sb("var2", [P, 1]), sb("rstd2", [P, 1])
        xn, cn = sb("xn", [P, D]), sb("cn", [P, C])
        in_t = sb("in_t", [P, 4, P])
        square = sb("square", [P, 3 * XH, XD])
        norm = sb("norm", [P, 3 * XH])
        qk = sb("qk", [P, 3 * XH, XD])
        v1 = sb("v1", [P, 2, 2, XH, P])
        q_t, k_t = sb("q_t", [P, 2, 2, P]), sb("k_t", [P, 2, 2, P])
        smax, prob, prob_t = sb("smax", [P, 2, 2]), sb("prob", [P, 2, 512]), sb("prob_t", [P, 2, 512])
        pv_t = sb("pv_t", [P, 512])
        rsum, att, att_t = sb("rsum", [P, XH]), sb("att", [P, D]), sb("att_t", [P, KD, P])
        p_in, p_q, p_l, p_c, p_k, p_pv = ps("p_in"), ps("p_q"), ps("p_l"), ps("p_c"), ps("p_k"), ps("p_pv")
        p_s = [ps("p_s0"), ps("p_s1")]

        w_loaded, mask_loaded, allowed_zero, allowed_ready, one_set = (
            sem("w_loaded"), sem("mask_loaded"), sem("allowed_zero"), sem("allowed_ready"), sem("one_set"))
        token_loaded = [sem("token0"), sem("token1")]
        ln, mv_ready, root_steps, xn_ready = sem("ln"), sem("mv_ready"), sem("root_steps"), sem("xn_ready")
        in_ready, in_copied, proj_ready, sq_ready, v_copied = (
            sem("in_ready"), sem("in_copied"), sem("proj_ready"), sem("sq_ready"), sem("v_copied"))
        pvt_copied, turned_back, pad_zero = sem("pvt_copied"), sem("turned_back"), sem("pad_zero")
        ss_ready, norm_steps, rnorm_ready, qk_ready = sem("ss_ready"), sem("norm_steps"), sem("rnorm_ready"), sem("qk_ready")
        qkt_ready, qkt_copied, s_ready, max_ready, sub_ready, exp_ready = (
            sem("qkt_ready"), sem("qkt_copied"), sem("s_ready"), sem("max_ready"), sem("sub_ready"), sem("exp_ready"))
        pt_ready, pt_copied, pv_ready, rsum_ready, att_ready = (
            sem("pt_ready"), sem("pt_copied"), sem("pv_ready"), sem("rsum_ready"), sem("att_ready"))
        att_t_ready, att_t_copied, o_ready, x_ready = (
            sem("att_t_ready"), sem("att_t_copied"), sem("o_ready"), sem("x_ready"))
        block = ctx.enter_context(nc.Block())

        @block.sync
        def _(sp):
            for slot in range(2):
                sp.dma_start(token[:, slot, :], k.ctx_tok[slot]).then_inc(token_loaded[slot], 16)
            sp.dma_start(mask_u8[:], k.mask.rearrange("(a n) s -> a (n s)", a=1)).then_inc(mask_loaded, 16)
            for t, name in ((wq, "pq"), (wl, "pl"), (wo, "po")):
                sp.dma_start(t[:], w[name].rearrange("(c p) n -> p c n", p=P)).then_inc(w_loaded, 16)
            sp.dma_start(wc[:, 0, :], w["pc"][0:P, :]).then_inc(w_loaded, 16)
            sp.dma_start(wc[0:C1, 1, :], w["pc"][P:C, :]).then_inc(w_loaded, 16)
            with sp.Fori(1, N // 2) as pair:
                for slot in range(2):
                    sp.wait_ge(xn_ready, 2 * pair + slot - 1)
                    sp.dma_start(token[:, slot, :], k.ctx_tok[bass.ds(2 * pair + slot, 1)].rearrange(
                        "a s c -> (a s) c")).then_inc(token_loaded[slot], 16)

        @block.gpsimd
        def _(pool):
            nc.gpsimd.memset(wc[C1:P, 1, :], 0.0).then_inc(pad_zero, 1)
            pool.wait_ge(pad_zero, 1)
            nc.gpsimd.memset(in_t[C1:P, 3, :], 0.0).then_inc(pad_zero, 1)
            pool.wait_ge(pad_zero, 2)
            nc.gpsimd.memset(v1[:], 1.0).then_inc(one_set, 1)
            nc.gpsimd.memset(allowed[:], 0.0).then_inc(allowed_zero, 1)

            def work(st):
                if st.has(0):
                    n = st.n(0)
                    hold(pool, mv_ready, n + 1)
                    nc.gpsimd.tensor_scalar(rstd[:], mv[:, :, 1], EPS, 1.0, ALU.add, ALU.mult).then_inc(root_steps, 1)
                    pool.wait_ge(root_steps, 7 * n + 1)
                    nc.gpsimd.tensor_tensor(rstd[:], rstd[:], k.const("power"), ALU.pow).then_inc(root_steps, 1)
                    pool.wait_ge(root_steps, 7 * n + 2)
                    nc.gpsimd.tensor_tensor(var2[:], rstd[:, 0:1], rstd[:, 0:1], ALU.mult).then_inc(root_steps, 1)
                    pool.wait_ge(root_steps, 7 * n + 3)
                    nc.gpsimd.tensor_tensor(var2[:], mv[:, 0, 1:2], var2[:], ALU.mult).then_inc(root_steps, 1)
                    hold(pool, root_steps, 7 * n + 4)
                    nc.gpsimd.tensor_scalar(rstd2[:], var2[:], EPS, 1.0, ALU.add, ALU.mult).then_inc(root_steps, 1)
                    pool.wait_ge(root_steps, 7 * n + 5)
                    nc.gpsimd.tensor_tensor(rstd2[:], rstd2[:], k.const("power")[:, 0:1], ALU.pow).then_inc(
                        root_steps, 1)
                    pool.wait_ge(root_steps, 7 * n + 6)
                    nc.gpsimd.tensor_tensor(rstd[:, 0:1], rstd[:, 0:1], rstd2[:], ALU.mult).then_inc(root_steps, 1)
                if st.has(1):
                    n = st.n(1)
                    pool.wait_ge(ss_ready, n + 1)
                    nc.gpsimd.tensor_tensor(norm[:], norm[:], k.const("root"), ALU.pow).then_inc(norm_steps, 1)

            pipeline(pool, N, 4, work)

        @block.scalar
        def _(act):
            act.wait_ge(one_set, 1)

            def work(st):
                def exponential(i):
                    act.wait_ge(sub_ready, 2 * st.n(3) + i + 1)
                    nc.scalar.activation(prob[:, i, :], prob[:, i, :], ACT.Exp, scale=XD ** -0.5).then_inc(
                        exp_ready, 1)

                def square_of(i, src):
                    nc.scalar.activation(square[:, i * XH:(i + 1) * XH, :],
                                         src[:, 0:D].rearrange("p (h c) -> p h c", c=XD), ACT.Square).then_inc(
                        sq_ready, 1)

                if st.has(2):
                    n, s = st.n(2), st.slot(2)
                    after(act, pv_ready, n - 1)
                    for i, src in enumerate((p_c, p_l)):
                        t = nc.scalar.copy(v1[:, s, i, :, 0:XD], src[:, D:2 * D].rearrange("p (h c) -> p h c", c=XD))
                    t.then_inc(v_copied, 1)
                if st.has(4):
                    n = st.n(4)
                    act.wait_ge(pv_ready, n + 1)
                    after(act, turned_back, n)
                    nc.scalar.copy(pv_t[:], p_pv[:]).then_inc(pvt_copied, 1)
                if st.has(1):
                    n = st.n(1)
                    act.wait_ge(in_ready, n + 1)
                    after(act, proj_ready, 3 * n)
                    for i, (gain, shift, j, rows) in enumerate((("lg", "lb", 0, P), ("lg", "lb", 1, P),
                                                                ("xg", "xb", 0, P), ("xg", "xb", 1, C1))):
                        t = nc.scalar.activation(in_t[0:rows, i, :], p_in[0:rows, i * P:(i + 1) * P], ACT.Identity,
                                                 bias=k.col(shift, j, rows), scale=k.col(gain, j, rows))
                        if j == 1:
                            t.then_inc(in_copied, 1)
                if st.has(2):
                    n = st.n(2)
                    act.wait_ge(qkt_ready, n + 1)
                    after(act, s_ready, 2 * n)
                    for i, gain in enumerate(("qn0", "qn1")):
                        nc.scalar.activation(q_t[:, i], halves(p_q[:, D:2 * D]), ACT.Copy, scale=k.col(gain))
                    nc.scalar.activation(k_t[:].rearrange("p a b c -> p (a b) c"), halves(p_k[:]), ACT.Copy,
                                         scale=k.col("kn")).then_inc(qkt_copied, 1)
                if st.has(3):
                    exponential(0)
                    exponential(1)
                if st.has(1):
                    n = st.n(1)
                    act.wait_ge(proj_ready, 3 * n + 2)
                    after(act, ss_ready, n)
                    square_of(0, p_q)
                    square_of(1, p_l)
                    act.wait_ge(proj_ready, 3 * n + 3)
                    square_of(2, p_c)
                if st.has(4):
                    n = st.n(4)
                    act.wait_ge(att_t_ready, n + 1)
                    after(act, o_ready, n)
                    nc.scalar.copy(att_t[:], halves(p_k[:, 0:D])).then_inc(att_t_copied, 1)
                if st.has(3):
                    n = st.n(3)
                    for i in range(2):
                        act.wait_ge(pt_ready, 2 * n + i + 1)
                        after(act, pv_ready, n)
                        nc.scalar.copy(prob_t[:, i, :], p_s[i][:]).then_inc(pt_copied, 1)

            pipeline(act, N, 4, work)

        @block.vector
        def _(dve):
            dve.wait_ge(mask_loaded, 16)
            dve.wait_ge(allowed_zero, 1)
            nc.vector.tensor_scalar(allowed[0:1].rearrange("p n s -> p (n s)"), mask_u8[:], -1.0, -FAR, ALU.add,
                                    ALU.mult).then_inc(allowed_ready, 1)

            def work(st):
                def shift(i):
                    n, sc = st.n(3), p_s[i][:].rearrange("p (a b) -> p a b", b=2 * P)
                    dve.wait_ge(s_ready, 2 * n + i + 1)
                    nc.vector.tensor_reduce(smax[:, i, :], sc, AX.X, ALU.max).then_inc(max_ready, 1)
                    dve.wait_ge(max_ready, 2 * n + i + 1)
                    after(dve, pt_ready, 2 * (n - 1) + i + 1)
                    nc.vector.tensor_tensor(prob[:, i, :].rearrange("p (a b) -> p a b", b=2 * P), sc,
                                            smax[:, i, :].unsqueeze(2).to_broadcast([P, 2, 2 * P]),
                                            ALU.subtract).then_inc(sub_ready, 1)

                if st.has(0):
                    n, s = st.n(0), st.slot(0)
                    nc.vector.bn_stats(stats[:, 0, :], row(k.x, n))
                    dve.wait_ge(token_loaded[s], 16 * (st.use(0) + 1))
                    nc.vector.bn_stats(stats[:, 1, :], token[:, s, :]).then_inc(ln, 1)
                    after(dve, xn_ready, n)
                    hold(dve, ln, n + 1)
                    nc.vector.bn_aggr(mv[:, 0, :], stats[:, 0, :])
                    nc.vector.bn_aggr(mv[:, 1, :], stats[:, 1, :]).then_inc(mv_ready, 1)
                if st.has(2):
                    n = st.n(2)
                    dve.wait_ge(norm_steps, n + 1)
                    nc.vector.tensor_scalar(norm[:], norm[:], XD ** -0.5, 1e-8, ALU.mult, ALU.max).then_inc(
                        rnorm_ready, 1)
                    dve.wait_ge(rnorm_ready, 2 * n + 1)
                    nc.vector.reciprocal(norm[:], norm[:]).then_inc(rnorm_ready, 1)
                    dve.wait_ge(rnorm_ready, 2 * n + 2)
                    dve.wait_ge(v_copied, n + 1)
                    after(dve, qkt_ready, n)
                    for i, src in enumerate((p_q, p_l, p_c)):
                        t = nc.vector.tensor_tensor(
                            qk[:, i * XH:(i + 1) * XH, :], src[:, 0:D].rearrange("p (h c) -> p h c", c=XD),
                            norm[:, i * XH:(i + 1) * XH].unsqueeze(2).to_broadcast([P, XH, XD]), ALU.mult)
                    t.then_inc(qk_ready, 1)
                if st.has(3):
                    shift(0)
                    shift(1)
                if st.has(4):
                    n = st.n(4)
                    pv = p_pv[:].rearrange("p (h c) -> p h c", c=P)
                    dve.wait_ge(turned_back, n + 1)
                    nc.vector.reciprocal(rsum[:], pv[:, :, XD]).then_inc(rsum_ready, 1)
                    dve.wait_ge(rsum_ready, n + 1)
                    after(dve, att_t_ready, n)
                    nc.vector.tensor_tensor(att[:].rearrange("p (h c) -> p h c", c=XD), pv[:, :, 0:XD],
                                            rsum[:].unsqueeze(2).to_broadcast([P, XH, XD]), ALU.mult).then_inc(
                        att_ready, 1)
                if st.has(0):
                    n, s = st.n(0), st.slot(0)
                    dve.wait_ge(root_steps, 7 * n + 7)
                    after(dve, in_ready, n)
                    nc.vector.tensor_scalar(xn[:], row(k.x, n), mv[:, 0, 0:1], rstd[:, 0:1], ALU.subtract, ALU.mult)
                    nc.vector.tensor_scalar(cn[:], token[:, s, :], mv[:, 1, 0:1], rstd[:, 1:2], ALU.subtract,
                                            ALU.mult).then_inc(xn_ready, 1)
                if st.has(1):
                    n = st.n(1)
                    dve.wait_ge(sq_ready, 3 * n + 3)
                    nc.vector.tensor_reduce(norm[:], square[:], AX.X, ALU.add).then_inc(ss_ready, 1)
                if st.has(4):
                    n = st.n(4)
                    dve.wait_ge(o_ready, n + 1)
                    nc.vector.tensor_tensor(row(k.x, n), p_k[:, D:2 * D], row(k.x, n), ALU.add).then_inc(x_ready, 1)

            pipeline(dve, N, 4, work)

        @block.tensor
        def _(pe):
            pe.wait_ge(w_loaded, 16 * 5)
            pe.wait_ge(pad_zero, 2)
            pe.wait_ge(allowed_ready, 1)
            ident = k.const("ident")

            def work(st):
                def project(o, chunks, weights):
                    for i in range(KD):
                        t = nc.tensor.matmul(o, in_t[:, chunks + i, :], weights[:, i, :], start=i == 0,
                                             stop=i == KD - 1)
                    t.then_inc(proj_ready, 1)

                if st.has(3):
                    n = st.n(3)
                    pe.wait_ge(qkt_copied, n + 1)
                    after(pe, pt_copied, 2 * n)
                    pe.nop(nofuse=True)
                    for i in range(2):
                        sc = p_s[i][:].rearrange("p (m b) -> p m b", b=2 * P)
                        nc.tensor.matmul(sc[:, :, 0:P], k.const16("ones"), allowed[:, bass.ds(n, 1), :].to_broadcast(
                            [P, 2, P]), start=True, stop=False, skip_group_check=True)
                        for m in range(2):
                            t = nc.tensor.matmul(sc[:, m, :], q_t[:, i, m, :],
                                                 k_t[:, m].rearrange("p a b -> p (a b)"), start=False, stop=m == 1,
                                                 skip_group_check=True)
                        t.then_inc(s_ready, 1)
                if st.has(1):
                    n = st.n(1)
                    pe.wait_ge(xn_ready, n + 1)
                    after(pe, in_copied, 2 * n)
                    nc.tensor.transpose(p_in[:, 0:P], xn[:, 0:P], ident)
                    nc.tensor.transpose(p_in[:, P:2 * P], xn[:, P:D], ident)
                    nc.tensor.transpose(p_in[:, 2 * P:3 * P], cn[:, 0:P], ident)
                    nc.tensor.transpose(p_in[0:C1, 3 * P:4 * P], cn[:, P:C], ident).then_inc(in_ready, 1)
                if st.has(4):
                    n = st.n(4)
                    pe.wait_ge(pvt_copied, n + 1)
                    for c in range(4):
                        t = nc.tensor.transpose(p_pv[:, c * P:(c + 1) * P], pv_t[:, c * P:(c + 1) * P], ident)
                    t.then_inc(turned_back, 1)
                if st.has(2):
                    n = st.n(2)
                    pe.wait_ge(qk_ready, n + 1)
                    after(pe, qkt_copied, n)
                    after(pe, x_ready, n - 2)
                    flat = qk[:].rearrange("p h c -> p (h c)")
                    for m in range(2):
                        nc.tensor.transpose(p_q[:, D + m * P:D + (m + 1) * P], flat[:, m * P:(m + 1) * P], ident)
                        for i, src in enumerate((2, 1)):
                            t = nc.tensor.transpose(p_k[:, (2 * m + i) * P:(2 * m + i + 1) * P],
                                                    flat[:, src * D + m * P:src * D + (m + 1) * P], ident)
                    t.then_inc(qkt_ready, 1)
                if st.has(1):
                    n = st.n(1)
                    pe.wait_ge(in_copied, 2 * n + 1)
                    after(pe, qk_ready, n)
                    project(p_l[:], 0, wl)
                    after(pe, qkt_copied, n)
                    project(p_q[:, 0:D], 0, wq)
                    pe.wait_ge(in_copied, 2 * n + 2)
                    project(p_c[:], 2, wc)
                if st.has(4):
                    n = st.n(4)
                    pe.wait_ge(att_ready, n + 1)
                    if st.has(2):
                        pe.wait_ge(qkt_copied, n + 3)
                    for c in range(KD):
                        t = nc.tensor.transpose(p_k[:, c * P:(c + 1) * P], att[:, c * P:(c + 1) * P], ident)
                    t.then_inc(att_t_ready, 1)
                if st.has(3):
                    n = st.n(3)
                    for i in range(2):
                        pe.wait_ge(exp_ready, 2 * n + i + 1)
                        for j in range(4):
                            t = nc.tensor.transpose(p_s[i][:, j * P:(j + 1) * P], prob[:, i, j * P:(j + 1) * P],
                                                    ident)
                        t.then_inc(pt_ready, 1)
                if st.has(4):
                    n = st.n(4)
                    pe.wait_ge(att_t_copied, n + 1)
                    o = p_k[:, D:2 * D]
                    nc.tensor.matmul(o, k.ones, k.bias_row("po"), start=True, stop=False)
                    for i in range(KD):
                        t = nc.tensor.matmul(o, att_t[:, i, :], wo[:, i, :], start=False, stop=i == KD - 1)
                    t.then_inc(o_ready, 1)
                if st.has(3):
                    n, s = st.n(3), st.slot(3)
                    after(pe, att_ready, n)
                    for i in range(2):
                        pe.wait_ge(pt_copied, 2 * n + i + 1)
                        for m in range(2):
                            h = 2 * m + i
                            for c in range(2):
                                t = nc.tensor.matmul(p_pv[:, h * P:(h + 1) * P], v1[:, s, c, h, :],
                                                     prob_t[:, i, (2 * m + c) * P:(2 * m + c + 1) * P],
                                                     start=c == 0, stop=c == 1)
                    t.then_inc(pv_ready, 1)

            pipeline(pe, N, 4, work)


def sentence_experts(k):
    nc, w = k.nc, k.w
    with ExitStack() as ctx:
        def sb(name, shape, dt=F32):
            return ctx.enter_context(nc.sbuf_tensor("s_" + name, shape, dt))

        sem = ctx.enter_context(semaphores(nc, "s_"))

        def ps(name):
            return ctx.enter_context(nc.psum_tensor("s_" + name, [P, 512], F32))

        wr, down, up = sb("wr", [P, KD, E]), sb("down", [P, E, KD, F1]), sb("up", [P, E, D])
        bn_gain, bn_shift = sb("bn_gain", [P, KD]), sb("bn_shift", [P, KD])
        stats, mv = sb("stats", [P, 2, 6]), sb("mv", [P, 2, 2])
        rstd, var2, rstd2 = sb("rstd", [P, 1]), sb("var2", [P, 1]), sb("rstd2", [P, 1])
        z = sb("z", [P, 2, D])
        z_t, z_sum, z_bn = sb("z_t", [P, 2, KD, P]), sb("z_sum", [P, KD]), sb("z_bn", [P, KD, P])
        best, score, total = sb("best", [P, 1]), sb("score", [P, E]), sb("total", [P, 1])
        gate, expert_f, expert_i = sb("gate", [P, 2]), sb("expert_f", [P, 1]), sb("expert_i", [P, 2], I32)
        shifted = sb("shifted", [P, E])
        hidden, hidden_t = sb("hidden", [P, F1]), sb("hidden_t", [P, P])
        result = sb("result", [P, 2, D])
        p_in, p_r, p_h, p_ht, p_y = ps("p_in"), ps("p_r"), ps("p_h"), ps("p_ht"), ps("p_y")
        w_loaded, bn_root, bn_steps, zero_set = sem("w_loaded"), sem("bn_root"), sem("bn_steps"), sem("zero_set")
        ln, mv_ready, root_steps, z_ready = sem("ln"), sem("mv_ready"), sem("root_steps"), sem("z_ready")
        in_ready, in_copied, bn_ready, logits_ready = sem("in_ready"), sem("in_copied"), sem("bn_ready"), sem("logits_ready")
        choice, exp_ready, expert_ready = sem("choice"), sem("exp_ready"), sem("expert_ready")
        h_ready, relu_ready, ht_ready, ht_copied, y_ready = (
            sem("h_ready"), sem("relu_ready"), sem("ht_ready"), sem("ht_copied"), sem("y_ready"))
        out_ready, stored = sem("out_ready"), [sem("stored0"), sem("stored1")]
        block = ctx.enter_context(nc.Block())

        @block.sync
        def _(sp):
            sp.dma_start(wr[:], w["wr"].rearrange("(c p) n -> p c n", p=P)).then_inc(w_loaded, 16)
            sp.dma_start(down[:], w["down"].rearrange("e (c p) n -> p e c n", p=P)).then_inc(w_loaded, 16)
            sp.dma_start(up[0:F1], w["up"].rearrange("e p n -> p e n")).then_inc(w_loaded, 16)
            with sp.Fori(0, N // 2) as pair:
                for slot in range(2):
                    n = 2 * pair + slot
                    sp.wait_ge(out_ready, n + 1)
                    sp.dma_start(k.out[bass.ds(n, 1)].rearrange("a s d -> (a s) d"), result[:, slot, :]).then_inc(
                        stored[slot], 16)
            sp.wait_ge(stored[0], 16 * (N // 2))
            sp.wait_ge(stored[1], 16 * (N // 2))

        @block.gpsimd
        def _(pool):
            nc.gpsimd.memset(up[F1:P], 0.0).then_inc(zero_set, 1)
            pool.wait_ge(zero_set, 1)
            nc.gpsimd.memset(hidden_t[F1:P, :], 0.0).then_inc(zero_set, 1)
            pool.wait_ge(zero_set, 2)
            inverse_root(k, pool, bn_gain[:], k.cols[:, COLS["bnv"][0]:COLS["bnv"][0] + 2], bn_root, 0)

            def work(st):
                if st.has(0):
                    n = st.n(0)
                    hold(pool, mv_ready, n + 1)
                    m = mv[:, st.slot(0), 1:2]
                    nc.gpsimd.tensor_scalar(rstd[:], m, EPS, 1.0, ALU.add, ALU.mult).then_inc(root_steps, 1)
                    pool.wait_ge(root_steps, 7 * n + 1)
                    nc.gpsimd.tensor_tensor(rstd[:], rstd[:], k.const("power")[:, 0:1], ALU.pow).then_inc(root_steps, 1)
                    pool.wait_ge(root_steps, 7 * n + 2)
                    nc.gpsimd.tensor_tensor(var2[:], rstd[:], rstd[:], ALU.mult).then_inc(root_steps, 1)
                    pool.wait_ge(root_steps, 7 * n + 3)
                    nc.gpsimd.tensor_tensor(var2[:], m, var2[:], ALU.mult).then_inc(root_steps, 1)
                    hold(pool, root_steps, 7 * n + 4)
                    nc.gpsimd.tensor_scalar(rstd2[:], var2[:], EPS, 1.0, ALU.add, ALU.mult).then_inc(root_steps, 1)
                    pool.wait_ge(root_steps, 7 * n + 5)
                    nc.gpsimd.tensor_tensor(rstd2[:], rstd2[:], k.const("power")[:, 0:1], ALU.pow).then_inc(
                        root_steps, 1)
                    pool.wait_ge(root_steps, 7 * n + 6)
                    nc.gpsimd.tensor_tensor(rstd[:], rstd[:], rstd2[:], ALU.mult).then_inc(root_steps, 1)

            pipeline(pool, N, 1, work)

        @block.scalar
        def _(act):
            act.wait_ge(zero_set, 2)

            def work(st):
                if st.has(1):
                    n, s = st.n(1), st.slot(1)
                    act.wait_ge(in_ready, n + 1)
                    after(act, h_ready, n - 1)
                    after(act, bn_ready, 2 * n)
                    for i in range(KD):
                        t = nc.scalar.activation(z_t[:, s, i, :], p_in[:, i * P:(i + 1) * P], ACT.Identity,
                                                 bias=k.col("fb", i), scale=k.col("fg", i),
                                                 accum_out=z_sum[:, i:i + 1])
                    t.then_inc(in_copied, 1)
                if st.has(2):
                    n, s = st.n(2), st.slot(2)
                    act.wait_ge(h_ready, n + 1)
                    after(act, ht_ready, n)
                    nc.scalar.activation(hidden[:], p_h[:, 0:F1], ACT.Relu).then_inc(relu_ready, 1)
                    act.wait_ge(ht_ready, n + 1)
                    after(act, y_ready, n)
                    nc.scalar.copy(hidden_t[0:F1, :], p_ht[0:F1, 0:P]).then_inc(ht_copied, 1)
                if st.has(1):
                    n = st.n(1)
                    act.wait_ge(choice, 5 * n + 2)
                    nc.scalar.activation(shifted[:], shifted[:], ACT.Exp, accum_out=total[:]).then_inc(exp_ready, 1)

            pipeline(act, N, 2, work)

        @block.vector
        def _(dve):
            link = Steps(dve, bn_steps)
            col = lambda name: k.cols[:, COLS[name][0]:COLS[name][0] + 2]
            dve.wait_ge(bn_root, 2)
            link.then(nc.vector.tensor_tensor(bn_gain[:], bn_gain[:], col("bng"), ALU.mult))
            link.then(nc.vector.tensor_tensor(bn_shift[:], bn_gain[:], col("bnm"), ALU.mult))
            link.then(nc.vector.tensor_tensor(bn_shift[:], col("bnb"), bn_shift[:], ALU.subtract))
            link.then(nc.vector.tensor_scalar(bn_gain[:], bn_gain[:], 1.0 / S, None, ALU.mult))

            def work(st):
                if st.has(0):
                    n, s = st.n(0), st.slot(0)
                    nc.vector.bn_stats(stats[:, s, :], row(k.x, n)).then_inc(ln, 1)
                    hold(dve, ln, n + 1)
                    nc.vector.bn_aggr(mv[:, s, :], stats[:, s, :]).then_inc(mv_ready, 1)
                if st.has(1):
                    n, s = st.n(1), st.slot(1)
                    dve.wait_ge(in_copied, n + 1)
                    after(dve, logits_ready, n)
                    nc.vector.tensor_tensor(z_sum[:], z_sum[:], bn_gain[:], ALU.mult).then_inc(bn_ready, 1)
                    dve.wait_ge(bn_ready, 2 * n + 1)
                    nc.vector.tensor_tensor(z_bn[:], z_sum[:].unsqueeze(2).to_broadcast([P, KD, P]),
                                            bn_shift[:].unsqueeze(2).to_broadcast([P, KD, P]), ALU.add).then_inc(
                        bn_ready, 1)
                if st.has(0):
                    n, s = st.n(0), st.slot(0)
                    dve.wait_ge(root_steps, 7 * n + 7)
                    after(dve, in_ready, n - 1)
                    nc.vector.tensor_scalar(z[:, s, :], row(k.x, n), mv[:, s, 0:1], rstd[:, 0:1], ALU.subtract,
                                            ALU.mult).then_inc(z_ready, 1)
                if st.has(2):
                    n, s = st.n(2), st.slot(2)
                    dve.wait_ge(y_ready, n + 1)
                    after(dve, stored[s], 16 * st.use(2))
                    nc.vector.scalar_tensor_tensor(out=result[:, s, :], in0=p_y[:, 0:D], scalar=gate[:, s:s + 1],
                                                   in1=row(k.x, n), op0=ALU.mult, op1=ALU.add).then_inc(out_ready, 1)
                if st.has(1):
                    n, s = st.n(1), st.slot(1)
                    dve.wait_ge(logits_ready, n + 1)
                    nc.vector.tensor_reduce(best[:], p_r[:, 0:E], AX.X, ALU.max).then_inc(choice, 1)
                    dve.wait_ge(choice, 5 * n + 1)
                    after(dve, exp_ready, n)
                    nc.vector.tensor_scalar(shifted[:], p_r[:, 0:E], best[:, 0:1], None, ALU.subtract).then_inc(
                        choice, 1)
                    nc.vector.scalar_tensor_tensor(out=score[:], in0=p_r[:, 0:E], scalar=best[:, 0:1],
                                                   in1=k.const("backward"), op0=ALU.is_ge, op1=ALU.mult).then_inc(
                        choice, 1)
                    dve.wait_ge(choice, 5 * n + 3)
                    nc.vector.tensor_reduce(expert_f[:], score[:], AX.X, ALU.max).then_inc(choice, 1)
                    dve.wait_ge(choice, 5 * n + 4)
                    nc.vector.tensor_scalar(expert_i[:, s:s + 1], expert_f[:], -1.0, float(E), ALU.mult,
                                            ALU.add).then_inc(choice, 1)
                    dve.wait_ge(exp_ready, n + 1)
                    nc.vector.reciprocal(gate[:, s:s + 1], total[:]).then_inc(expert_ready, 1)

            pipeline(dve, N, 2, work)

        @block.tensor
        def _(pe):
            pe.wait_ge(w_loaded, 48)
            ident = k.const("ident")

            def work(st):
                if st.has(1):
                    n, s = st.n(1), st.slot(1)
                    pe.wait_ge(z_ready, n + 1)
                    after(pe, in_copied, n)
                    for c in range(KD):
                        t = nc.tensor.transpose(p_in[:, c * P:(c + 1) * P], z[:, s, c * P:(c + 1) * P], ident)
                    t.then_inc(in_ready, 1)
                if st.has(2):
                    n, s = st.n(2), st.slot(2)
                    after(pe, relu_ready, n)
                    hold(pe, expert_ready, n + 1)
                    e = pe.value_load(expert_i[0:1, s:s + 1], min_val=0, max_val=E - 1)
                    select = k.const16("select")[:, bass.ds(e * P, P)]
                    nc.tensor.matmul(p_h[:, 0:F1], select, k.expert_bias[:, F + D:F + D + F1], start=True, stop=False)
                    for i in range(KD):
                        t = nc.tensor.matmul(p_h[:, 0:F1], z_t[:, s, i, :], down[:, bass.ds(e, 1), i, :].rearrange(
                            "p a n -> p (a n)"), start=False, stop=i == KD - 1)
                    t.then_inc(h_ready, 1)
                    after(pe, ht_copied, n)
                    hold(pe, relu_ready, n + 1)
                    nc.tensor.transpose(p_ht[0:F1, 0:P], hidden[:], ident).then_inc(ht_ready, 1)
                if st.has(1):
                    n = st.n(1)
                    pe.wait_ge(bn_ready, 2 * n + 2)
                    after(pe, expert_ready, n)
                    nc.tensor.matmul(p_r[:, 0:E], k.ones, k.bias_row("route"), start=True, stop=False)
                    for i in range(KD):
                        t = nc.tensor.matmul(p_r[:, 0:E], z_bn[:, i, :], wr[:, i, :], start=False, stop=i == KD - 1)
                    t.then_inc(logits_ready, 1)
                if st.has(2):
                    n, s = st.n(2), st.slot(2)
                    after(pe, out_ready, n)
                    hold(pe, ht_copied, n + 1)
                    nc.tensor.matmul(p_y[:, 0:D], select, k.expert_bias[:, F + D + F1:], start=True, stop=False)
                    nc.tensor.matmul(p_y[:, 0:D], hidden_t[:], up[:, bass.ds(e, 1), :].rearrange(
                        "p a n -> p (a n)"), start=False, stop=True).then_inc(y_ready, 1)

            pipeline(pe, N, 2, work)


def lay_out(a):
    def c(x):
        return np.ascontiguousarray(x)

    l0, l1 = "L0_attn_", "L1_attn_"
    arrays = {
        "x_seq": c(np.transpose(a["x"], (1, 0, 2)).reshape(B * S, D)),
        "ctx": c(a["ctx_768"]),
        "mask": c(a["mask_BxS2_bk0"]),
        "w_q0": c(a[l0 + "Wq"].T),
        "w_kv0": c(np.concatenate([a[l0 + "Wk"], a[l0 + "Wv"]]).T),
        "w_v_gamma": c(a[l0 + "v_gamma"]), "w_v_beta": c(a[l0 + "v_beta"]),
        "w_xq": c(a["L0_xattn_Wq"]), "w_xk": c(a["L0_xattn_Wk"]), "w_xv": c(a["L0_xattn_Wv"]),
        "w_xo": c(a["L0_xattn_Wo"]),
        "w_gate": c(a["L0_ffn_gate_w"].T),
        "w_w1": c(np.transpose(a["L0_ffn_w1"], (0, 2, 1))), "w_w2": c(np.transpose(a["L0_ffn_w2"], (0, 2, 1))),
        "w_qkv1": c(a[l1 + "Wqkv"].T), "w_out1": c(a[l1 + "Wout"].T),
        "w_pq": c(a["L1_xattn_Wq"].T), "w_pc": c(a["L1_xattn_Wkv"].T), "w_pl": c(a["L1_xattn_Wlkv"].T),
        "w_po": c(a["L1_xattn_Wo"].T),
        "w_wr": c(a["L1_ffn_Wr"]), "w_down": c(a["L1_ffn_W_down"]), "w_up": c(a["L1_ffn_W_up"]),
    }
    bqkv = a[l1 + "bqkv"]
    rows = {"q0": a[l0 + "bq"], "k0": a[l0 + "bk"], "v0": a[l0 + "bv"], "xq": a["L0_xattn_bq"],
            "xk": a["L0_xattn_bk"], "xv": a["L0_xattn_bv"], "xo": a["L0_xattn_bo"], "gate": a["L0_ffn_gate_b"],
            "aq": bqkv[0:D], "ak": bqkv[D:2 * D], "av": bqkv[2 * D:], "ao": a[l1 + "bout"], "po": a["L1_xattn_bo"],
            "route": a["L1_ffn_br"]}
    bias = np.zeros(BIAS_N, np.float32)
    for name, (at, width) in BIAS_AT.items():
        bias[at:at + width] = rows[name]
    arrays["bias"] = bias.reshape(P, BIAS_G)
    arrays["expert_bias"] = c(np.concatenate([a["L0_ffn_b1"], a["L0_ffn_b2"], a["L1_ffn_b_down"],
                                              a["L1_ffn_b_up"]], 1))
    f, p = "L1_ffn_", "L1_xattn_"
    vectors = {"kg": a[l0 + "k_gamma"], "kb": a[l0 + "k_beta"], "xg": a[p + "ln_x_g"], "xb": a[p + "ln_x_b"],
               "lg": a[p + "ln_l_g"], "lb": a[p + "ln_l_b"],
               "qn0": np.concatenate([a[p + "qn_g"], np.zeros(XD, np.float32)]),
               "qn1": np.concatenate([np.zeros(XD, np.float32), a[p + "qn_g"]]),
               "kn": np.concatenate([a[p + "kn_g"]] * 2), "fg": a[f + "ln_g"], "fb": a[f + "ln_b"],
               "bng": a[f + "bn_g"], "bnb": a[f + "bn_b"], "bnm": a[f + "bn_mean"], "bnv": a[f + "bn_var"]}
    cols = np.zeros((COLS_N, P), np.float32)
    for name, (at, width) in COLS.items():
        v = vectors[name]
        cols[at:at + width].reshape(-1)[:v.size] = v
    arrays["cols"] = c(cols.T)
    return arrays


def kernel(**inputs):
    import concourse.bacc as bacc
    import ml_dtypes
    from concourse.bass_utils import run_bass_kernel_spmd

    arrays = lay_out({n: np.asarray(v) for n, v in inputs.items()})
    c32, c16 = constants()
    arrays["consts"], arrays["consts16"] = c32, c16.astype(ml_dtypes.bfloat16)
    nc = bacc.Bacc("TRN2", target_bir_lowering=False, num_devices=1)
    aps = {n: nc.dram_tensor("in_" + n, a.shape, mybir.dt.from_np(a.dtype), kind="ExternalInput").ap()
           for n, a in arrays.items()}
    out = nc.dram_tensor("out", (B, S, D), F32, kind="ExternalOutput").ap()
    w = {n[2:]: ap for n, ap in aps.items() if n.startswith("w_")}
    decoder(nc, aps["x_seq"], aps["ctx"], aps["mask"], w, aps["cols"], aps["bias"], aps["expert_bias"],
            aps["consts"], aps["consts16"], out)
    result = run_bass_kernel_spmd(nc, [{"in_" + n: a for n, a in arrays.items()}], core_ids=[0])
    return result.results[0]["out"]
```

```python
from contextlib import ExitStack, contextmanager

import concourse.bass as bass
import numpy as np
from concourse import mybir

ALU = mybir.AluOpType
ACT = mybir.ActivationFunctionType
F32 = mybir.dt.float32
BF16 = mybir.dt.bfloat16
I32 = mybir.dt.int32
U8 = mybir.dt.uint8
AX = mybir.AxisListType

P = 128
B = 16
S = 128
D = 256
C = 192
N = B * S // P
KD = D // P
EPS = 1e-5
FAR = -1e30

QH, QK = 16, 64
H, HD = 16, 16
XH, XD = 4, 64
E, F = 8, 1024
F1 = 64
ROUTED = N + E - 1
WINDOW = 64

BIAS_ROWS = [("q0", QH * QK), ("k0", QK), ("v0", D), ("xq", D), ("xk", D), ("xv", D), ("xo", D), ("gate", E),
             ("aq", D), ("ak", D), ("av", D), ("ao", D), ("po", D), ("route", E)]
BIAS_AT, _n = {}, 0
for _name, _width in BIAS_ROWS:
    BIAS_AT[_name] = (_n, _width)
    _n += _width
BIAS_G = -(-_n // P)
BIAS_N = BIAS_G * P
EXPERT_BIAS = F + D + F1 + D

COLS = {}
for _name, _width in [("kg", 1), ("kb", 1), ("xg", 2), ("xb", 2), ("lg", 2), ("lb", 2), ("qn0", 1), ("qn1", 1), ("kn", 1),
                      ("fg", 2), ("fb", 2), ("bng", 2), ("bnb", 2), ("bnm", 2), ("bnv", 2)]:
    COLS[_name] = (sum(w for _, w in COLS.values()), _width)
COLS_N = sum(w for _, w in COLS.values())

CONSTS = {}
for _name, _width in [("ident", P), ("gram", P), ("parity", 2), ("steps", N), ("before", E * E), ("backward", E),
                      ("tiles", ROUTED + 1), ("power", N), ("root", 3 * XH)]:
    CONSTS[_name] = (sum(w for _, w in CONSTS.values()), _width)
CONSTS_N = sum(w for _, w in CONSTS.values())
CONSTS16 = {}
for _name, _width in [("ident", P), ("upper", P), ("ones", P), ("window", P), ("select", E * P)]:
    CONSTS16[_name] = (sum(w for _, w in CONSTS16.values()), _width)
CONSTS16_N = sum(w for _, w in CONSTS16.values())


def constants():
    c = np.zeros((P, CONSTS_N), np.float32)

    def put(name, a):
        at, width = CONSTS[name]
        c[:, at:at + width] = a

    row, col = np.arange(P)[:, None], np.arange(P)[None, :]
    put("ident", np.eye(P))
    same = (row // B == col // B) & (row % B <= col % B)
    put("gram", same / np.sqrt(col % B + 1.0) / QH)
    head = np.arange(P) // HD % 2
    put("parity", np.stack([head == 0, head == 1], 1) * (HD ** -0.5))
    put("steps", np.arange(N)[None, :] * P)
    put("before", (np.arange(E)[None, :] < np.arange(E)[:, None]).reshape(1, -1))
    put("backward", E - np.arange(E)[None, :])
    put("power", -0.5)
    put("root", 0.5)
    put("tiles", np.arange(ROUTED + 1)[None, :])
    c16 = np.zeros((P, CONSTS16_N), np.float32)

    def put16(name, a):
        at, width = CONSTS16[name]
        c16[:, at:at + width] = a

    put16("ident", np.eye(P))
    put16("upper", row < col)
    put16("ones", 1.0)
    put16("window", np.where((row >= col) & (row - col < WINDOW), 0.0, FAR))
    select = (row[:, :, None] < 3 * E) & (row[:, :, None] % E == np.arange(E)[None, :, None])
    put16("select", np.broadcast_to(select, (P, E, P)).reshape(P, -1))
    return c, c16


class Step:

    def __init__(self, pair, slot, tiles):
        self.pair, self.parity, self.tiles = pair, slot, tiles
        self.step = 2 * pair + slot

    def starts(self, step):
        return isinstance(self.pair, int) and self.step == step

    def has(self, k):
        return not isinstance(self.pair, int) or 0 <= self.step - k < self.tiles

    def n(self, k):
        return self.step - k

    def slot(self, k):
        return (self.parity - k) % 2

    def use(self, k):
        return self.pair + (self.parity - k) // 2


def pipeline(eng, tiles, lag, work):
    first = -(-(lag + 2) // 2)
    for s in range(2 * first):
        work(Step(s // 2, s % 2, tiles))
    with eng.Fori(first, tiles // 2) as pair:
        for slot in range(2):
            work(Step(pair, slot, tiles))
    for s in range(tiles // 2 * 2, tiles + lag):
        work(Step(s // 2, s % 2, tiles))


@contextmanager
def semaphores(nc, prefix):
    taken = []

    def sem(name):
        taken.append(nc.alloc_semaphore(name=prefix + name))
        return taken[-1]

    yield sem
    nc.clear_and_free_semaphores(taken)
    nc.all_engine_barrier()


def after(eng, sem, count):
    if not isinstance(count, int) or count > 0:
        eng.wait_ge(sem, count)


def hold(eng, sem, count):
    after(eng, sem, count)
    eng.nop(nofuse=True)


def inverse_root(k, pool, out, var, computed, count):
    n = out.shape[1]
    k.nc.gpsimd.tensor_scalar(out, var, EPS, 1.0, ALU.add, ALU.mult).then_inc(computed, 1)
    pool.wait_ge(computed, 2 * count + 1)
    k.nc.gpsimd.tensor_tensor(out, out, k.const("power")[:, 0:n], ALU.pow).then_inc(computed, 1)


def twice_normalised(k, out, var):
    return k.nc.gpsimd.tensor_scalar(out, var, 1.0 + EPS, EPS * EPS, ALU.mult, ALU.add)


def row(t, n):
    return t[:, bass.ds(n, 1), :].rearrange("p a d -> p (a d)")


def halves(t):
    return t.rearrange("p (a b) -> p a b", b=P)


class Core:
    pass


def decoder(nc, x_seq, ctx_tok, mask, w, cols, bias, expert_bias, consts, consts16, out):
    k = Core()
    k.nc, k.w, k.ctx_tok, k.mask, k.out = nc, w, ctx_tok, mask, out
    k.x1_dram = nc.dram_tensor("x1_by_sequence", (B * S, D), F32).ap()
    k.slots_in = nc.dram_tensor("tokens_by_expert", (ROUTED * P, D), F32).ap()
    k.slots_out = nc.dram_tensor("experts_output", (ROUTED * P, D), F32).ap()
    k.bias_dram = nc.dram_tensor("bias_parts", (3, BIAS_N), BF16).ap()
    with ExitStack() as ctx:
        def sb(name, shape, dt=F32):
            return ctx.enter_context(nc.sbuf_tensor(name, shape, dt))

        k.sb_c, k.sb_c16 = sb("constants", [P, CONSTS_N]), sb("constants16", [P, CONSTS16_N], BF16)
        k.cols = sb("cols", [P, COLS_N])
        k.bias = sb("bias_rows", [P, BIAS_N], BF16)
        k.expert_bias = sb("expert_bias", [P, EXPERT_BIAS], BF16)
        k.x = sb("x", [P, N, D])
        k.wa = sb("attention_weights", [P, 4, KD, D])
        k.slot_i = sb("slot_of_token", [P, N], I32)
        k.tile_expert = sb("expert_of_tile", [P, ROUTED + 1], I32)
        k.loaded = {n: ctx.enter_context(nc.semaphore(n + "_loaded")) for n in (
            "consts", "bias", "ffn", "wa0", "wa1", "wp", "ws", "fill")}

        def const(name, table=CONSTS, t=k.sb_c):
            at, width = table[name]
            return t[:, at:at + width]

        k.const = const
        k.const16 = lambda name: const(name, CONSTS16, k.sb_c16)
        k.col = lambda name, i=0, rows=P: k.cols[0:rows, COLS[name][0] + i:COLS[name][0] + i + 1]
        k.bias_row = lambda name, a=0, n=None: k.bias[:, BIAS_AT[name][0] + a:BIAS_AT[name][0] + (
            BIAS_AT[name][1] if n is None else a + n)]
        k.ones = k.const16("ones")

        with ExitStack() as first:
            k.w1 = first.enter_context(nc.sbuf_tensor("w1", [P, E, KD, F], F32))
            k.w2 = first.enter_context(nc.sbuf_tensor("w2", [P, E, F // P, D], F32))
            linear_attention(k, x_seq, cols, bias, expert_bias, consts, consts16)
            softmax_attention(k, 0)
            route(k)
            experts(k)
        k.stats = sb("stats", [P, N, 6])
        k.wq, k.wl, k.wc, k.wo = (sb("p_wq", [P, KD, D]), sb("p_wl", [P, KD, 2 * D]), sb("p_wc", [P, KD, 2 * D]),
                                  sb("p_wo", [P, KD, D]))
        k.wr, k.down, k.up = sb("s_wr", [P, KD, E]), sb("s_down", [P, E, KD, F1]), sb("s_up", [P, E, D])
        softmax_attention(k, 1)
        perceiver(k)
        sentence_experts(k)


def linear_attention(k, x_seq, cols, bias, expert_bias, consts, consts16):
    nc, w = k.nc, k.w
    with ExitStack() as ctx:
        def sb(name, shape, dt=F32):
            return ctx.enter_context(nc.sbuf_tensor("l_" + name, shape, dt))

        sem = ctx.enter_context(semaphores(nc, "l_"))

        def ps(name, cols=512):
            return ctx.enter_context(nc.psum_tensor("l_" + name, [P, cols], F32))

        wq, wkv = sb("wq", [P, KD, QH * QK]), sb("wkv", [P, KD, QK + D])
        v_gain, v_shift = sb("v_gain", [P, D]), sb("v_shift", [P, D])
        bias_f, bias_r = sb("bias_f", [P, BIAS_G]), sb("bias_r", [P, BIAS_G])
        bias_p = sb("bias_p", [P, 3, BIAS_G], BF16)
        eb_f = sb("eb_f", [E, EXPERT_BIAS])
        eb_p = sb("eb_p", [E, EXPERT_BIAS], BF16)
        stats, mv, rstd = sb("stats", [P, 6]), sb("mv", [P, 2]), sb("rstd", [P, 1])
        xn = sb("xn", [P, 2, D])
        xn_t = sb("xn_t", [P, 2, D])
        qmax, qsum = sb("qmax", [P, QH]), sb("qsum", [P, QH])
        qexp = sb("qexp", [P, QH * QK])
        qprob = sb("qprob", [P, QH * QK])
        qk = sb("qk", [P, 2, 2 * QK])
        kvstats, kvmv, kvr = sb("kvstats", [P, 12]), sb("kvmv", [P, 4]), sb("kvr", [P, 2])
        less_mean = sb("less_mean", [P, 2])
        v = sb("v", [P, 2, D])
        qk_t = sb("qk_t", [P, 2, P])
        gram = sb("gram", [P, P])

        p_xt, p_kv, p_qkt, p_out = ps("p_xt"), ps("p_kv"), ps("p_qkt"), ps("p_out")
        p_q = [ps("p_q0", 1024), ps("p_q1", 1024)]

        mv_ready, rstd_steps, kvmv_ready, kvr_steps = (
            sem("mv_ready"), sem("rstd_steps"), sem("kvmv_ready"), sem("kvr_steps"))
        ln, xn_ready, xt_ready, xt_copied = sem("ln"), sem("xn_ready"), sem("xt_ready"), sem("xt_copied")
        q_ready, kv_ready = sem("q_ready"), sem("kv_ready")
        max_ready, sub_ready, exp_ready = sem("max_ready"), sem("sub_ready"), sem("exp_ready")
        sum_ready, rsum_ready, prob_ready, qmean_ready = (
            sem("sum_ready"), sem("rsum_ready"), sem("prob_ready"), sem("qmean_ready"))
        less_mean_ready, kv_centred, kv_ln, kn_ready, vn_ready, vgain_ready, v_ready = (
            sem("less_mean_ready"), sem("kv_centred"), sem("kv_ln"), sem("kn_ready"), sem("vn_ready"), sem("vgain_ready"), sem("v_ready"))
        qkt_ready, qkt_copied = sem("qkt_ready"), sem("qkt_copied")
        gram_ready, gram_masked, att_ready, x1_ready = (
            sem("gram_ready"), sem("gram_masked"), sem("att_ready"), sem("x1_ready"))
        bias_loaded, eb_loaded, x_head, x_loaded = sem("bias_loaded"), sem("eb_loaded"), sem("x_head"), sem("x_loaded")
        wq_loaded, wkv_loaded, stored = sem("wq_loaded"), sem("wkv_loaded"), sem("stored")
        b_hi, b_res, b_mid, b_res2, b_parts = sem("b_hi"), sem("b_res"), sem("b_mid"), sem("b_res2"), sem("b_parts")
        b_stored, eb_moved, v_rows = sem("b_stored"), sem("eb_moved"), sem("v_rows")
        eb_steps, zeroed = sem("eb_steps"), sem("zeroed")
        zero = sb("zero", [P, D])
        block = ctx.enter_context(nc.Block())

        @block.sync
        def _(sp):
            sp.dma_start(bias_f[:], bias).then_inc(bias_loaded, 16)
            sp.dma_start(k.sb_c[:], consts).then_inc(k.loaded["consts"], 16)

            def load_x(a, loaded):
                sp.dma_start(k.x[:, a:a + 4, :], x_seq.rearrange("(n p) d -> p n d", p=P)[:, a:a + 4, :]).then_inc(
                    loaded, 16)

            load_x(0, x_head)
            sp.wait_ge(b_parts, 1)
            for part in range(3):
                sp.dma_start(k.bias_dram[part].rearrange("(p g) -> p g", p=P), bias_p[:, part, :]).then_inc(b_stored, 16)
            sp.dma_start(wkv[:], w["kv0"].rearrange("(c p) n -> p c n", p=P)).then_inc(wkv_loaded, 16)
            sp.wait_ge(b_stored, 48)
            sp.wait_ge(zeroed, 1)
            sp.dma_start(k.bias[0:3, :], k.bias_dram).then_inc(k.loaded["bias"], 16)
            for a in range(4, N, 4):
                load_x(a, x_loaded)
            sp.wait_ge(zeroed, 2)
            for part in range(3):
                sp.wait_ge(eb_steps, 2 * part + 1)
                sp.dma_start(k.expert_bias[part * E:(part + 1) * E, :], eb_p[:]).then_inc(eb_moved, 16)
            for i, name in enumerate(("xq", "xk", "xv", "xo")):
                if name in ("xk", "xv"):
                    sp.dma_start(k.wa[:, i, 0, :], w[name][0:P, :]).then_inc(k.loaded["wa0"], 16)
                    sp.dma_start(k.wa[0:C - P, i, 1, :], w[name][P:C, :]).then_inc(k.loaded["wa0"], 16)
                else:
                    sp.dma_start(k.wa[:, i], w[name].rearrange("(c p) n -> p c n", p=P)).then_inc(k.loaded["wa0"], 16)
            for e in range(E):
                sp.dma_start(k.w1[:, e], w["w1"][e].rearrange("(c p) n -> p c n", p=P)).then_inc(k.loaded["ffn"], 16)
                sp.dma_start(k.w2[:, e], w["w2"][e].rearrange("(c p) n -> p c n", p=P)).then_inc(k.loaded["ffn"], 16)
            sp.wait_ge(zeroed, 4)
            for i in range(ROUTED):
                sp.dma_start(k.slots_in[i * P:(i + 1) * P, :], zero[:]).then_inc(k.loaded["fill"], 16)
            with sp.Fori(0, N) as n:
                hold(sp, x1_ready, n + 1)
                sp.dma_start(k.x1_dram[bass.ds(n * P, P), :], row(k.x, n)).then_inc(stored, 16)
            sp.wait_ge(stored, 16 * N)
            sp.wait_ge(eb_moved, 48)

        @block.gpsimd
        def _(pool):
            nc.gpsimd.memset(k.bias[:].bitcast(F32), 0.0).then_inc(zeroed, 1)
            nc.gpsimd.memset(k.expert_bias[:].bitcast(F32), 0.0).then_inc(zeroed, 1)
            pool.wait_ge(zeroed, 2)
            nc.gpsimd.memset(qk_t[QK:P], 0.0).then_inc(zeroed, 1)
            pool.wait_ge(zeroed, 3)
            nc.gpsimd.memset(zero[:], 0.0).then_inc(zeroed, 1)
            pool.wait_ge(k.loaded["consts"], 48)

            def work(st):
                if st.has(0):
                    n = st.n(0)
                    hold(pool, mv_ready, n + 1)
                    inverse_root(k, pool, rstd[:], mv[:, 1:2], rstd_steps, n)
                if st.has(2):
                    n, s = st.n(2), st.slot(2)
                    hold(pool, kvmv_ready, n + 1)
                    inverse_root(k, pool, kvr[:], kvmv[:].rearrange("p (a b) -> p a b", b=2)[:, :, 1], kvr_steps, n)
                    if st.starts(2):
                        pool.wait_ge(v_rows, 32)
                    pool.wait_ge(vn_ready, n + 1)
                    nc.gpsimd.tensor_tensor(v[:, s, :], v[:, s, :], v_gain[:], ALU.mult).then_inc(vgain_ready, 1)
                    pool.wait_ge(vgain_ready, n + 1)
                    nc.gpsimd.tensor_tensor(v[:, s, :], v[:, s, :], v_shift[:], ALU.add).then_inc(v_ready, 1)
                    pool.wait_ge(rsum_ready, n + 1)
                    after(pool, qmean_ready, n)
                    nc.gpsimd.tensor_tensor(
                        qprob[:].rearrange("p (h k) -> p h k", k=QK), qexp[:].rearrange("p (h k) -> p h k", k=QK),
                        qsum[:].unsqueeze(2).to_broadcast([P, QH, QK]), ALU.mult).then_inc(prob_ready, 1)

            pipeline(pool, N, 4, work)

        @block.scalar
        def _(act):
            act.dma_start(k.sb_c16[:], consts16).then_inc(k.loaded["consts"], 16)
            act.dma_start(k.cols[:], cols).then_inc(k.loaded["consts"], 16)
            act.dma_start(wq[:], w["q0"].rearrange("(c p) n -> p c n", p=P)).then_inc(wq_loaded, 16)
            act.dma_start(eb_f[:], expert_bias).then_inc(eb_loaded, 16)
            act.dma_start(v_gain[:], w["v_gamma"].partition_broadcast(P)).then_inc(v_rows, 16)
            act.dma_start(v_shift[:], w["v_beta"].partition_broadcast(P)).then_inc(v_rows, 16)
            act.wait_ge(k.loaded["consts"], 48)

            def work(st):
                if st.has(1):
                    n = st.n(1)
                    act.wait_ge(xt_ready, n + 1)
                    after(act, kv_ready, n - 1)
                    nc.scalar.copy(xn_t[:, st.slot(1), :], p_xt[:, 0:D]).then_inc(xt_copied, 1)
                if st.has(2):
                    n, s = st.n(2), st.slot(2)
                    key, value = qk[:, s, QK:2 * QK], v[:, s, :]
                    act.wait_ge(less_mean_ready, n + 1)
                    after(act, qkt_ready, n - 1)
                    nc.scalar.activation(key, p_kv[:, 0:QK], ACT.Identity, bias=less_mean[:, 0:1])
                    after(act, att_ready, n - 1)
                    nc.scalar.activation(value, p_kv[:, QK:QK + D], ACT.Identity, bias=less_mean[:, 1:2]).then_inc(
                        kv_centred, 1)
                    act.wait_ge(kvr_steps, 2 * n + 2)
                    act.wait_ge(kv_centred, n + 1)
                    nc.scalar.activation(key, key, ACT.Copy, scale=kvr[:, 0:1]).then_inc(kn_ready, 1)
                    nc.scalar.activation(value, value, ACT.Copy, scale=kvr[:, 1:2]).then_inc(vn_ready, 1)
                    act.wait_ge(sub_ready, n + 1)
                    nc.scalar.activation(qexp[:], qexp[:], ACT.Exp).then_inc(exp_ready, 1)
                if st.has(3):
                    n = st.n(3)
                    act.wait_ge(qkt_ready, n + 1)
                    after(act, gram_ready, n)
                    nc.scalar.copy(qk_t[0:QK, 0, :], p_qkt[0:QK, 0:P])
                    nc.scalar.activation(qk_t[0:QK, 1, :], p_qkt[0:QK, P:2 * P], ACT.Identity, bias=k.col("kb", rows=QK),
                                         scale=k.col("kg", rows=QK)).then_inc(qkt_copied, 1)

            pipeline(act, N, 4, work)

        @block.vector
        def _(dve):
            dve.wait_ge(bias_loaded, 16)
            nc.vector.tensor_copy(bias_p[:, 0, :], bias_f[:]).then_inc(b_hi, 1)
            dve.wait_ge(b_hi, 1)
            nc.vector.tensor_tensor(bias_r[:], bias_f[:], bias_p[:, 0, :], ALU.subtract).then_inc(b_res, 1)
            dve.wait_ge(b_res, 1)
            nc.vector.tensor_copy(bias_p[:, 1, :], bias_r[:]).then_inc(b_mid, 1)
            dve.wait_ge(b_mid, 1)
            nc.vector.tensor_tensor(bias_r[:], bias_r[:], bias_p[:, 1, :], ALU.subtract).then_inc(b_res2, 1)
            dve.wait_ge(b_res2, 1)
            nc.vector.tensor_copy(bias_p[:, 2, :], bias_r[:]).then_inc(b_parts, 1)

            def split_expert_biases(part):
                dve.wait_ge(eb_loaded, 16)
                after(dve, eb_steps, 2 * part)
                after(dve, eb_moved, 16 * part)
                nc.vector.tensor_copy(eb_p[:], eb_f[:]).then_inc(eb_steps, 1)
                if part < 2:
                    dve.wait_ge(eb_steps, 2 * part + 1)
                    nc.vector.tensor_tensor(eb_f[:], eb_f[:], eb_p[:], ALU.subtract).then_inc(eb_steps, 1)

            dve.wait_ge(k.loaded["consts"], 48)
            dve.wait_ge(x_head, 16)

            def work(st):
                for part in range(3):
                    if st.starts(part + 1):
                        split_expert_biases(part)
                if st.has(4):
                    n = st.n(4)
                    dve.wait_ge(gram_ready, n + 1)
                    after(dve, att_ready, n)
                    nc.vector.tensor_tensor(gram[:], p_out[:, D:D + P], k.const("gram"), ALU.mult).then_inc(
                        gram_masked, 1)
                if st.has(0):
                    n, s = st.n(0), st.slot(0)
                    if st.starts(4):
                        dve.wait_ge(x_loaded, 16 * (N // 4 - 1))
                    nc.vector.bn_stats(stats[:], row(k.x, n)).then_inc(ln, 1)
                if st.has(2):
                    n, s = st.n(2), st.slot(2)
                    dve.wait_ge(kv_ready, n + 1)
                    nc.vector.bn_stats(kvstats[:, 0:6], p_kv[:, 0:QK])
                    nc.vector.bn_stats(kvstats[:, 6:12], p_kv[:, QK:QK + D]).then_inc(kv_ln, 1)
                if st.has(0):
                    n = st.n(0)
                    after(dve, xn_ready, n)
                    hold(dve, ln, n + 1)
                    nc.vector.bn_aggr(mv[:], stats[:]).then_inc(mv_ready, 1)
                if st.has(2):
                    n, s = st.n(2), st.slot(2)
                    q3 = p_q[s][:].rearrange("p (h k) -> p h k", k=QK)
                    e3 = qexp[:].rearrange("p (h k) -> p h k", k=QK)
                    nc.vector.tensor_reduce(qmax[:], q3, AX.X, ALU.max).then_inc(max_ready, 1)
                    hold(dve, kv_ln, n + 1)
                    nc.vector.bn_aggr(kvmv[:, 0:2], kvstats[:, 0:6])
                    nc.vector.bn_aggr(kvmv[:, 2:4], kvstats[:, 6:12]).then_inc(kvmv_ready, 1)
                    after(dve, kv_centred, n)
                    dve.wait_ge(kvmv_ready, n + 1)
                    nc.vector.tensor_scalar(less_mean[:], kvmv[:].rearrange("p (a b) -> p a b", b=2)[:, :, 0], -1.0,
                                            None, ALU.mult).then_inc(less_mean_ready, 1)
                    dve.wait_ge(max_ready, n + 1)
                    after(dve, prob_ready, n)
                    nc.vector.tensor_tensor(e3, q3, qmax[:].unsqueeze(2).to_broadcast([P, QH, QK]),
                                            ALU.subtract).then_inc(sub_ready, 1)
                if st.has(3):
                    n, s = st.n(3), st.slot(3)
                    dve.wait_ge(prob_ready, n + 1)
                    nc.vector.tensor_reduce(qk[:, s, 0:QK], qprob[:].rearrange("p (h k) -> p k h", k=QK), AX.X,
                                            ALU.add).then_inc(qmean_ready, 1)
                if st.has(0):
                    n, s = st.n(0), st.slot(0)
                    dve.wait_ge(rstd_steps, 2 * n + 2)
                    after(dve, xt_ready, n - 1)
                    nc.vector.tensor_scalar(xn[:, s, :], row(k.x, n), mv[:, 0:1], rstd[:, 0:1], ALU.subtract,
                                            ALU.mult).then_inc(xn_ready, 1)
                if st.has(4):
                    n = st.n(4)
                    dve.wait_ge(att_ready, n + 1)
                    nc.vector.tensor_tensor(row(k.x, n), p_out[:, 0:D], row(k.x, n), ALU.add).then_inc(x1_ready, 1)
                if st.has(2):
                    n, s = st.n(2), st.slot(2)
                    dve.wait_ge(exp_ready, n + 1)
                    nc.vector.tensor_reduce(qsum[:], e3, AX.X, ALU.add).then_inc(sum_ready, 1)
                    dve.wait_ge(sum_ready, n + 1)
                    nc.vector.reciprocal(qsum[:], qsum[:]).then_inc(rsum_ready, 1)

            pipeline(dve, N, 4, work)

        @block.tensor
        def _(pe):
            pe.wait_ge(k.loaded["consts"], 48)
            pe.wait_ge(zeroed, 3)

            def work(st):
                def project_q(c):
                    n, s = st.n(1), st.slot(1)
                    xt, o = halves(xn_t[:, s, :]), p_q[s][:, c * 512:(c + 1) * 512]
                    nc.tensor.matmul(o, k.ones, k.bias_row("q0", c * 512, 512), start=True, stop=False)
                    for i in range(KD):
                        t = nc.tensor.matmul(o, xt[:, i, :], wq[:, i, c * 512:(c + 1) * 512], start=False,
                                             stop=i == KD - 1)
                    return t

                if st.has(1):
                    n, s = st.n(1), st.slot(1)
                    pe.wait_ge(xn_ready, n + 1)
                    after(pe, xt_copied, n)
                    for c in range(KD):
                        t = nc.tensor.transpose(p_xt[:, c * P:(c + 1) * P], xn[:, s, c * P:(c + 1) * P],
                                                k.const("ident"))
                    t.then_inc(xt_ready, 1)
                if st.has(4):
                    n, s = st.n(4), st.slot(4)
                    pe.wait_ge(gram_masked, n + 1)
                    pe.wait_ge(v_ready, n + 1)
                    nc.tensor.matmul(p_out[:, 0:D], gram[:], v[:, s, :], start=True, stop=True).then_inc(att_ready, 1)
                if st.has(1):
                    n = st.n(1)
                    if st.starts(1):
                        pe.wait_ge(wq_loaded, 16)
                        pe.wait_ge(k.loaded["bias"], 16)
                    pe.wait_ge(xt_copied, n + 1)
                    after(pe, sub_ready, n - 1)
                    project_q(0)
                    project_q(1).then_inc(q_ready, 1)
                if st.has(3):
                    n, s = st.n(3), st.slot(3)
                    pe.wait_ge(qmean_ready, n + 1)
                    after(pe, qkt_copied, n)
                    hold(pe, kn_ready, n + 1)
                    for c in range(2):
                        t = nc.tensor.transpose(p_qkt[0:QK, c * P:(c + 1) * P], qk[:, s, c * QK:(c + 1) * QK],
                                                k.const("ident"))
                    t.then_inc(qkt_ready, 1)
                if st.has(1):
                    n, s = st.n(1), st.slot(1)
                    xt, o = halves(xn_t[:, s, :]), p_kv[:, 0:QK + D]
                    if st.starts(1):
                        pe.wait_ge(wkv_loaded, 16)
                    after(pe, kv_centred, n)
                    nc.tensor.matmul(o, k.ones, k.bias[:, BIAS_AT["k0"][0]:BIAS_AT["k0"][0] + QK + D], start=True,
                                     stop=False)
                    for i in range(KD):
                        t = nc.tensor.matmul(o, xt[:, i, :], wkv[:, i, :], start=False, stop=i == KD - 1)
                    t.then_inc(kv_ready, 1)
                if st.has(3):
                    n = st.n(3)
                    pe.wait_ge(qkt_copied, n + 1)
                    after(pe, x1_ready, n)
                    nc.tensor.matmul(p_out[:, D:D + P], qk_t[:, 1, :], qk_t[:, 0, :], start=True,
                                     stop=True).then_inc(gram_ready, 1)

            pipeline(pe, N, 4, work)


def softmax_attention(k, layer):
    nc, w = k.nc, k.w
    cross = layer == 0
    with ExitStack() as ctx:
        def sb(name, shape, dt=F32):
            return ctx.enter_context(nc.sbuf_tensor(f"a{layer}_" + name, shape, dt))

        sem = ctx.enter_context(semaphores(nc, f"a{layer}_"))

        def ps(name):
            return ctx.enter_context(nc.psum_tensor(f"a{layer}_" + name, [P, 512], F32))

        STRIPS = 4
        MOVED = 2
        KC = 4 if cross else 2
        wq, wk, wv, wo = (k.wa[:, i] for i in range(4))
        if cross:
            token = sb("token", [P, 2, C])
        else:
            moe = sb("moe", [P, 2, D])
        stats, mv, rstd = sb("stats", [P, 6]), sb("mv", [P, 2]), sb("rstd", [P, 1])
        xn = sb("xn", [P, 2, D])
        in_t = sb("in_t", [P, KC, P])
        q_t = sb("q_t", [P, 2, 2, P])
        q_pad = sb("q_pad", [P, STRIPS, 2, 2, P])
        k_t = sb("k_t", [P, 2, 2, P])
        v1 = sb("v1", [P, 2, H, 32])
        smax = sb("smax", [P, 4, STRIPS])
        prob = sb("prob", [P, STRIPS, 512])
        prob_t = sb("prob_t", [P, STRIPS, 512])
        rsum = sb("rsum", [P, H])
        pv_t = sb("pv_t", [P, 512])
        att, att_t = pv_t[:, 0:D], halves(pv_t[:, D:2 * D])

        p_s = [ps(f"p_s{i}") for i in range(STRIPS)]
        p_in, p_qk, p_vo, p_pv = ps("p_in"), ps("p_qk"), ps("p_vo"), ps("p_pv")

        x_head, x_loaded = sem("x_head"), sem("x_loaded")
        token_loaded = [sem("token0"), sem("token1")]
        mv_ready, rstd_steps = sem("mv_ready"), sem("rstd_steps")
        one_set, x_summed, ln, xn_ready = sem("one_set"), sem("x_summed"), sem("ln"), sem("xn_ready")
        in_ready, in_copied, qk_ready, q_copied, k_copied = (
            sem("in_ready"), sem("in_copied"), sem("qk_ready"), sem("q_copied"), sem("k_copied"))
        pad_zero, q_placed = sem("pad_zero"), sem("q_placed")
        pvt_copied, turned_back = sem("pvt_copied"), sem("turned_back")
        v_ready, v_copied = sem("v_ready"), sem("v_copied")
        s_ready, max_ready, sub_ready, exp_ready = sem("s_ready"), sem("max_ready"), sem("sub_ready"), sem("exp_ready")
        pt_ready, pt_copied, pt_moved, pv_ready = sem("pt_ready"), sem("pt_copied"), sem("pt_moved"), sem("pv_ready")
        rsum_ready, att_ready, att_t_ready, att_t_copied = (
            sem("rsum_ready"), sem("att_ready"), sem("att_t_ready"), sem("att_t_copied"))
        o_ready, x_ready = sem("o_ready"), sem("x_ready")
        block = ctx.enter_context(nc.Block())

        @block.sync
        def _(sp):
            if cross:
                for a in range(0, N, 4):
                    sp.dma_start(k.x[:, a:a + 4, :], k.x1_dram.rearrange("(s n) d -> s n d", n=N)[:, a:a + 4, :]
                                 ).then_inc(x_loaded if a else x_head, 16)
                    if a == 0:
                        for slot in range(2):
                            sp.dma_start(token[:, slot, :], k.ctx_tok[slot]).then_inc(token_loaded[slot], 16)
            else:
                for t, name in ((k.wq, "pq"), (k.wl, "pl"), (k.wo, "po")):
                    sp.dma_start(t[:], w[name].rearrange("(c p) n -> p c n", p=P)).then_inc(k.loaded["wp"], 16)
                sp.dma_start(k.wc[:, 0, :], w["pc"][0:P, :]).then_inc(k.loaded["wp"], 16)
                sp.dma_start(k.wc[0:C - P, 1, :], w["pc"][P:C, :]).then_inc(k.loaded["wp"], 16)
                sp.dma_start(k.wr[:], w["wr"].rearrange("(c p) n -> p c n", p=P)).then_inc(k.loaded["ws"], 16)
                sp.dma_start(k.down[:], w["down"].rearrange("e (c p) n -> p e c n", p=P)).then_inc(k.loaded["ws"], 16)
                sp.dma_start(k.up[0:F1], w["up"].rearrange("e p n -> p e n")).then_inc(k.loaded["ws"], 16)
            sp.wait_ge(pad_zero, 1)

            def work(st):
                if st.has(1):
                    n = st.n(1)
                    hold(sp, q_copied, n + 1)
                    after(sp, s_ready, STRIPS * n)
                    for i in range(STRIPS):
                        rows = slice(32 * i, 32 * i + 32)
                        sp.dma_start(q_pad[rows, i], q_t[rows]).then_inc(q_placed, 16)
                if cross and st.has(0) and (not isinstance(st.pair, int) or st.pair > 0):
                    n, s = st.n(0), st.slot(0)
                    after(sp, in_ready, n - 1)
                    sp.dma_start(token[:, s, :], k.ctx_tok[bass.ds(n, 1)].rearrange("a s c -> (a s) c")).then_inc(
                        token_loaded[s], 16)

            pipeline(sp, N, 1, work)

        @block.gpsimd
        def _(pool):
            def gather(n, slot):
                nc.gpsimd.indirect_dma_start(
                    out=moe[:, slot, :], out_offset=None, in_=k.slots_out,
                    in_offset=bass.IndirectOffsetOnAxis(ap=k.slot_i[:, n:n + 1], axis=0)).then_inc(
                    token_loaded[slot], 16)

            if not cross:
                gather(0, 0)
            nc.gpsimd.memset(q_pad[:], 0.0).then_inc(pad_zero, 1)
            nc.gpsimd.memset(v1[:], 1.0).then_inc(one_set, 1)
            for n in range(N):
                if not cross and n + 1 < N:
                    after(pool, x_summed, n)
                    gather(n + 1, (n + 1) % 2)
                hold(pool, mv_ready, n + 1)
                inverse_root(k, pool, rstd[:], mv[:, 1:2], rstd_steps, n)
            if not cross:
                pool.wait_ge(rstd_steps, 2 * N)
                nc.gpsimd.memset(k.wc[C - P:P, 1, :], 0.0).then_inc(one_set, 1)
                pool.wait_ge(one_set, 2)
                nc.gpsimd.memset(k.up[F1:P], 0.0).then_inc(one_set, 1)
                pool.wait_ge(one_set, 3)

        @block.scalar
        def _(act):
            act.wait_ge(one_set, 1)

            def work(st):
                def exponential(i):
                    act.wait_ge(sub_ready, STRIPS * st.n(2) + i + 1)
                    nc.scalar.activation(prob[:, i, :], prob[:, i, :], ACT.Exp).then_inc(exp_ready, 1)

                if st.has(3):
                    n = st.n(3)
                    act.wait_ge(pv_ready, n + 1)
                    after(act, o_ready, n)
                    nc.scalar.copy(pv_t[:], p_pv[:]).then_inc(pvt_copied, 1)
                if st.has(2):
                    exponential(0)
                if st.has(1):
                    n = st.n(1)
                    act.wait_ge(in_ready, n + 1)
                    after(act, v_ready, n)
                    if cross:
                        nc.scalar.copy(in_t[:, 0:3, :], halves(p_in[:, 0:3 * P]))
                        nc.scalar.copy(in_t[0:C - P, 3, :], p_in[0:C - P, 3 * P:]).then_inc(in_copied, 1)
                    else:
                        nc.scalar.copy(in_t[:], halves(p_in[:, 0:D])).then_inc(in_copied, 1)
                if st.has(2):
                    exponential(1)
                    exponential(2)
                if st.has(1):
                    n, s = st.n(1), st.slot(1)
                    act.wait_ge(q_copied, n + 1)
                    after(act, s_ready, STRIPS * (n - 1))
                    nc.scalar.copy(k_t[:, s], halves(p_qk[:, D:2 * D])).then_inc(k_copied, 1)
                if st.has(1):
                    n, s = st.n(1), st.slot(1)
                    act.wait_ge(v_ready, n + 1)
                    after(act, pv_ready, n - 1)
                    nc.scalar.copy(v1[:, s, :, 0:HD], p_vo[:, 0:D].rearrange("p (h c) -> p h c", c=HD)).then_inc(
                        v_copied, 1)
                if st.has(2):
                    exponential(3)
                if st.has(2):
                    n = st.n(2)
                    after(act, pv_ready, n)
                    for i in (i for i in range(STRIPS) if i != MOVED):
                        act.wait_ge(pt_ready, STRIPS * n + i + 1)
                        nc.scalar.copy(prob_t[:, i, :], p_s[i][:]).then_inc(pt_copied, 1)
                if st.has(3):
                    n = st.n(3)
                    act.wait_ge(att_t_ready, n + 1)
                    nc.scalar.copy(att_t, halves(p_vo[:, 0:D])).then_inc(att_t_copied, 1)

            pipeline(act, N, 3, work)

        @block.vector
        def _(dve):
            if cross:
                dve.wait_ge(x_head, 16)

            def work(st):
                def shift(i):
                    n, sc = st.n(2), halves(p_s[i][:])
                    dve.wait_ge(s_ready, STRIPS * n + i + 1)
                    nc.vector.tensor_reduce(smax[:, :, i], sc, AX.X, ALU.max).then_inc(max_ready, 1)
                    dve.wait_ge(max_ready, STRIPS * n + i + 1)
                    after(dve, pt_ready, STRIPS * (n - 1) + i + 1)
                    nc.vector.tensor_tensor(halves(prob[:, i, :]), sc, smax[:, :, i].unsqueeze(2).to_broadcast(
                        [P, 4, P]), ALU.subtract).then_inc(sub_ready, 1)

                if st.has(2):
                    for i in range(STRIPS):
                        shift(i)
                if st.has(1):
                    n, s = st.n(1), st.slot(1)
                    dve.wait_ge(qk_ready, n + 1)
                    after(dve, q_placed, 16 * STRIPS * n)
                    for parity in range(2):
                        t = nc.vector.tensor_scalar(q_t[:, parity], halves(p_qk[:, 0:D]),
                                                    k.const("parity")[:, parity:parity + 1], None, ALU.mult)
                    t.then_inc(q_copied, 1)
                if st.has(0):
                    n, s = st.n(0), st.slot(0)
                    if not cross:
                        dve.wait_ge(token_loaded[s], 16 * (st.use(0) + 1))
                        nc.vector.tensor_tensor(row(k.x, n), moe[:, s, :], row(k.x, n), ALU.add).then_inc(x_summed, 1)
                        hold(dve, x_summed, n + 1)
                    if cross and st.starts(4):
                        dve.wait_ge(x_loaded, 16 * (N // 4 - 1))
                    nc.vector.bn_stats(stats[:], row(k.x, n)).then_inc(ln, 1)
                    after(dve, xn_ready, n)
                    hold(dve, ln, n + 1)
                    nc.vector.bn_aggr(mv[:], stats[:]).then_inc(mv_ready, 1)
                if st.has(3):
                    n = st.n(3)
                    pv = p_pv[:].rearrange("p (h c) -> p h c", c=32)
                    dve.wait_ge(turned_back, n + 1)
                    nc.vector.reciprocal(rsum[:], pv[:, :, HD]).then_inc(rsum_ready, 1)
                    dve.wait_ge(rsum_ready, n + 1)
                    nc.vector.tensor_tensor(att.rearrange("p (h c) -> p h c", c=HD), pv[:, :, 0:HD],
                                            rsum[:].unsqueeze(2).to_broadcast([P, H, HD]), ALU.mult).then_inc(
                        att_ready, 1)
                if st.has(2):
                    n = st.n(2)
                    dve.wait_ge(pt_ready, STRIPS * n + MOVED + 1)
                    after(dve, pv_ready, n)
                    nc.vector.tensor_copy(prob_t[:, MOVED, :], p_s[MOVED][:]).then_inc(pt_moved, 1)
                if st.has(0):
                    n, s = st.n(0), st.slot(0)
                    dve.wait_ge(rstd_steps, 2 * n + 2)
                    after(dve, in_ready, n - 1)
                    nc.vector.tensor_scalar(xn[:, s, :], row(k.x, n), mv[:, 0:1], rstd[:, 0:1], ALU.subtract,
                                            ALU.mult).then_inc(xn_ready, 1)
                if st.has(3):
                    n = st.n(3)
                    dve.wait_ge(o_ready, n + 1)
                    nc.vector.tensor_tensor(row(k.x, n), p_vo[:, D:2 * D], row(k.x, n), ALU.add).then_inc(x_ready, 1)

            pipeline(dve, N, 3, work)

        @block.tensor
        def _(pe):
            if cross:
                pe.wait_ge(k.loaded["wa0"], 16 * 6)
            else:
                pe.wait_ge(k.loaded["wa1"], 16 * 4)
            names = ("xq", "xk", "xv", "xo") if cross else ("aq", "ak", "av", "ao")
            kv_chunks = [(2, P), (3, C - P)] if cross else [(0, P), (1, P)]

            def project(o, name, at, wt, chunks):
                nc.tensor.matmul(o, k.bias_row(name, at, P), k.ones, start=True, stop=False)
                for i, (chunk, rows) in enumerate(chunks):
                    t = nc.tensor.matmul(o, wt[0:rows, i, at:at + P], in_t[0:rows, chunk, :], start=False,
                                         stop=i == KD - 1)
                return t

            def work(st):
                def score(i):
                    for j in range(4):
                        if j == 0 and not cross:
                            nc.tensor.matmul(halves(p_s[i][:]), k.const16("ident"), k.const16("window").unsqueeze(
                                1).to_broadcast([P, 4, P]), start=True, stop=False, skip_group_check=True)
                        half, parity = j // 2, j % 2
                        t = nc.tensor.matmul(p_s[i][:, j * P:(j + 1) * P], q_pad[:, i, parity, half, :],
                                             k_t[:, st.slot(2), half, :], start=cross, stop=True,
                                             skip_group_check=not cross)
                    t.then_inc(s_ready, 1)

                if st.has(2):
                    n = st.n(2)
                    pe.wait_ge(q_placed, 16 * STRIPS * (n + 1))
                    pe.wait_ge(k_copied, n + 1)
                    after(pe, pt_copied, 3 * n)
                    after(pe, pt_moved, n)
                    score(0)
                    score(1)
                if st.has(1):
                    n, s = st.n(1), st.slot(1)
                    pe.wait_ge(xn_ready, n + 1)
                    after(pe, in_copied, n)
                    for c in range(KD):
                        t = nc.tensor.transpose(p_in[:, c * P:(c + 1) * P], xn[:, s, c * P:(c + 1) * P],
                                                k.const("ident"))
                    if cross:
                        pe.wait_ge(token_loaded[s], 16 * (st.use(1) + 1))
                        nc.tensor.transpose(p_in[:, 2 * P:3 * P], token[:, s, 0:P], k.const("ident"))
                        t = nc.tensor.transpose(p_in[0:C - P, 3 * P:4 * P], token[:, s, P:C], k.const("ident"))
                    t.then_inc(in_ready, 1)
                if st.has(2):
                    score(2)
                    score(3)
                if st.has(1):
                    n, s = st.n(1), st.slot(1)
                    pe.wait_ge(in_copied, n + 1)
                    after(pe, q_copied, n)
                    after(pe, k_copied, n)
                    for c in range(KD):
                        project(p_qk[:, c * P:(c + 1) * P], names[0], c * P, wq, [(0, P), (1, P)])
                    for c in range(KD):
                        t = project(p_qk[:, D + c * P:D + (c + 1) * P], names[1], c * P, wk, kv_chunks)
                    t.then_inc(qk_ready, 1)
                if st.has(3):
                    n = st.n(3)
                    pe.wait_ge(pvt_copied, n + 1)
                    for c in range(4):
                        t = nc.tensor.transpose(p_pv[:, c * P:(c + 1) * P], pv_t[:, c * P:(c + 1) * P],
                                                k.const("ident"))
                    t.then_inc(turned_back, 1)
                if st.has(1):
                    n = st.n(1)
                    after(pe, x_ready, n - 2)
                    o = p_vo[:, 0:D]
                    nc.tensor.matmul(o, k.ones, k.bias_row(names[2]), start=True, stop=False)
                    for i, (chunk, rows) in enumerate(kv_chunks):
                        t = nc.tensor.matmul(o, in_t[0:rows, chunk, :], wv[0:rows, i, :], start=False,
                                             stop=i == KD - 1)
                    t.then_inc(v_ready, 1)
                if st.has(2):
                    n, s = st.n(2), st.slot(2)

                    def turn(i):
                        pe.wait_ge(exp_ready, STRIPS * n + i + 1)
                        for j in range(4):
                            t = nc.tensor.transpose(p_s[i][:, j * P:(j + 1) * P], prob[:, i, j * P:(j + 1) * P],
                                                    k.const("ident"))
                        t.then_inc(pt_ready, 1)

                    for i in range(STRIPS):
                        turn(i)
                if st.has(3):
                    n = st.n(3)
                    pe.wait_ge(att_ready, n + 1)
                    after(pe, v_copied, n + 3 if st.has(1) else N)
                    for c in range(KD):
                        t = nc.tensor.transpose(p_vo[:, c * P:(c + 1) * P], att[:, c * P:(c + 1) * P],
                                                k.const("ident"))
                    t.then_inc(att_t_ready, 1)
                if st.has(2):
                    n, s = st.n(2), st.slot(2)

                    def weigh(i):
                        if i == MOVED:
                            pe.wait_ge(pt_moved, n + 1)
                        else:
                            pe.wait_ge(pt_copied, 3 * n + i + (i < MOVED))
                        for j in range(4):
                            h = 8 * (j // 2) + 2 * i + j % 2
                            at = 32 * (h % 4)
                            t = nc.tensor.matmul(p_pv[at:at + 32, h // 4 * P:(h // 4 + 1) * P], v1[:, s, h, :],
                                                 prob_t[:, i, j * P:(j + 1) * P], start=True, stop=True)
                        return t

                    pe.wait_ge(v_copied, n + 1)
                    after(pe, att_ready, n)
                    for i in range(STRIPS):
                        t = weigh(i)
                    t.then_inc(pv_ready, 1)
                if st.has(3):
                    n = st.n(3)
                    pe.wait_ge(att_t_copied, n + 1)
                    o = p_vo[:, D:2 * D]
                    nc.tensor.matmul(o, k.ones, k.bias_row(names[3]), start=True, stop=False)
                    for i in range(KD):
                        t = nc.tensor.matmul(o, att_t[:, i, :], wo[:, i, :], start=False, stop=i == KD - 1)
                    t.then_inc(o_ready, 1)

            pipeline(pe, N, 3, work)


class Steps:

    def __init__(self, eng, sem):
        self.eng, self.sem, self.count = eng, sem, 0

    def then(self, instruction):
        instruction.then_inc(self.sem, 1)
        self.count += 1
        self.eng.wait_ge(self.sem, self.count)


def route(k):
    nc, w = k.nc, k.w
    with ExitStack() as ctx:
        def sb(name, shape, dt=F32):
            return ctx.enter_context(nc.sbuf_tensor("r_" + name, shape, dt))

        sem = ctx.enter_context(semaphores(nc, "r_"))

        wg = sb("wg", [P, KD, E])
        stats, mv, rstd = sb("stats", [P, 2, 6]), sb("mv", [P, 2, 2]), sb("rstd", [P, 2])
        xn, xn_all, xn_t = sb("xn", [P, 2, D]), sb("xn_all", [P, N, D]), sb("xn_t", [P, 2, D])
        logits, score = sb("logits", [P, N, E]), sb("score", [P, N, E])
        best = sb("best", [P, N])
        chosen, chosen16 = sb("chosen", [P, N, E]), sb("chosen16", [P, N + 1, E], BF16)
        rank = sb("rank", [P, N + 1, E])
        over = sb("over", [P, E, N])
        tiles_of, tri = sb("tiles_of", [P, E]), sb("tri", [P, E, E])
        first, last = sb("first", [P, E]), sb("last", [P, E])
        ends = sb("ends", [P, ROUTED + 1, E])
        tile_f = sb("tile_f", [P, ROUTED + 1])
        slot_f = sb("slot_f", [P, N])
        p_t = [ctx.enter_context(nc.psum_tensor(f"r_p_t{i}", [P, 512], F32)) for i in range(2)]
        p_lg = ctx.enter_context(nc.psum_tensor("r_p_lg", [P, 512], F32))
        p_rank = ctx.enter_context(nc.psum_tensor("r_p_rank", [P, 512], F32))

        w_loaded, ln, mv_ready, rstd_steps, xn_ready = (
            sem("w_loaded"), sem("ln"), sem("mv_ready"), sem("rstd_steps"), sem("xn_ready"))
        xn_kept, t_ready, t_copied, logits_ready = sem("xn_kept"), sem("t_ready"), sem("t_copied"), sem("logits_ready")
        steps, chosen_ready, rank_ready, slots_ready, sent = (
            sem("steps"), sem("chosen_ready"), sem("rank_ready"), sem("slots_ready"), sem("sent"))
        block = ctx.enter_context(nc.Block())

        @block.sync
        def _(sp):
            sp.dma_start(wg[:], w["gate"].rearrange("(c p) n -> p c n", p=P)).then_inc(w_loaded, 16)

        @block.gpsimd
        def _(pool):
            for n in range(N):
                s = n % 2
                pool.wait_ge(mv_ready, n + 1)
                inverse_root(k, pool, rstd[:, s:s + 1], mv[:, s, 1:2], rstd_steps, n)
            pool.wait_ge(slots_ready, 1)
            pool.wait_ge(xn_kept, N)
            pool.wait_ge(k.loaded["fill"], 16 * ROUTED)
            for n in range(N):
                nc.gpsimd.indirect_dma_start(
                    out=k.slots_in, out_offset=bass.IndirectOffsetOnAxis(ap=k.slot_i[:, n:n + 1], axis=0),
                    in_=xn_all[:, n, :], in_offset=None).then_inc(sent, 16)
            pool.wait_ge(sent, 16 * N)

        @block.scalar
        def _(act):
            def work(st):
                if st.has(2):
                    n, s = st.n(2), st.slot(2)
                    act.wait_ge(xn_ready, n + 1)
                    nc.scalar.copy(row(xn_all, n), xn[:, s, :]).then_inc(xn_kept, 1)
                    act.wait_ge(t_ready, n + 1)
                    after(act, logits_ready, n - 1)
                    nc.scalar.copy(xn_t[:, s, :], p_t[s][:, 0:D]).then_inc(t_copied, 1)

            pipeline(act, N, 2, work)

        @block.vector
        def _(dve):
            def work(st):
                if st.has(0):
                    n, s = st.n(0), st.slot(0)
                    nc.vector.bn_stats(stats[:, s, :], row(k.x, n)).then_inc(ln, 1)
                    after(dve, xn_ready, n - 1)
                    hold(dve, ln, n + 1)
                    nc.vector.bn_aggr(mv[:, s, :], stats[:, s, :]).then_inc(mv_ready, 1)
                if st.has(1):
                    n, s = st.n(1), st.slot(1)
                    dve.wait_ge(rstd_steps, 2 * n + 2)
                    after(dve, t_ready, n - 1)
                    after(dve, xn_kept, n - 1)
                    nc.vector.tensor_scalar(xn[:, s, :], row(k.x, n), mv[:, s, 0:1], rstd[:, s:s + 1], ALU.subtract,
                                            ALU.mult).then_inc(xn_ready, 1)

            pipeline(dve, N, 2, work)
            chain = Steps(dve, steps)
            by_tile = [P, N, E]
            dve.wait_ge(logits_ready, N)
            chain.then(nc.vector.tensor_copy(logits[:], p_lg[:, 0:N * E].rearrange("p (n e) -> p n e", e=E)))
            chain.then(nc.vector.tensor_reduce(best[:], logits[:], AX.X, ALU.max))
            chain.then(nc.vector.tensor_tensor(score[:], logits[:], best[:].unsqueeze(2).to_broadcast(by_tile),
                                               ALU.is_ge))
            backward = k.const("backward").unsqueeze(1).to_broadcast(by_tile)
            chain.then(nc.vector.tensor_tensor(score[:], score[:], backward, ALU.mult))
            chain.then(nc.vector.tensor_reduce(best[:], score[:], AX.X, ALU.max))
            chain.then(nc.vector.tensor_tensor(chosen[:], backward, best[:].unsqueeze(2).to_broadcast(by_tile),
                                               ALU.is_equal))
            chain.then(nc.vector.memset(chosen16[:], 0.0))
            nc.vector.tensor_copy(chosen16[:, 0:N, :], chosen[:]).then_inc(chosen_ready, 1)
            dve.wait_ge(rank_ready, 1)
            chain.then(nc.vector.tensor_copy(rank[:], p_rank[:, 0:(N + 1) * E].rearrange("p (n e) -> p n e", e=E)))
            chain.then(nc.vector.tensor_tensor(over[:], rank[:, N, :].unsqueeze(2).to_broadcast([P, E, N]),
                                               k.const("steps").unsqueeze(1).to_broadcast([P, E, N]), ALU.is_gt))
            chain.then(nc.vector.tensor_reduce(tiles_of[:], over[:], AX.X, ALU.add))
            chain.then(nc.vector.tensor_tensor(tri[:], k.const("before").rearrange("p (a b) -> p a b", b=E),
                                               tiles_of[:].unsqueeze(1).to_broadcast([P, E, E]), ALU.mult))
            chain.then(nc.vector.tensor_reduce(first[:], tri[:], AX.X, ALU.add))
            chain.then(nc.vector.tensor_tensor(last[:], first[:], tiles_of[:], ALU.add))
            chain.then(nc.vector.tensor_scalar(first[:], first[:], float(P), None, ALU.mult))
            chain.then(nc.vector.tensor_tensor(rank[:, 0:N, :], rank[:, 0:N, :],
                                               first[:].unsqueeze(1).to_broadcast(by_tile), ALU.add))
            chain.then(nc.vector.tensor_tensor(rank[:, 0:N, :], rank[:, 0:N, :], chosen[:], ALU.mult))
            chain.then(nc.vector.tensor_reduce(slot_f[:], rank[:, 0:N, :], AX.X, ALU.add))
            nc.vector.tensor_copy(k.slot_i[:], slot_f[:]).then_inc(slots_ready, 1)
            shape = [P, ROUTED + 1, E]
            chain.then(nc.vector.tensor_tensor(ends[:], k.const("tiles").unsqueeze(2).to_broadcast(shape),
                                               last[:].unsqueeze(1).to_broadcast(shape), ALU.is_ge))
            chain.then(nc.vector.tensor_reduce(tile_f[:], ends[:], AX.X, ALU.add))
            nc.vector.tensor_scalar(k.tile_expert[:], tile_f[:], float(E - 1), None, ALU.min)

        @block.tensor
        def _(pe):
            pe.wait_ge(w_loaded, 16)
            nc.tensor.matmul(p_lg[:, 0:N * E].rearrange("p (n e) -> p n e", e=E), k.ones,
                             k.bias_row("gate").unsqueeze(1).to_broadcast([P, N, E]), start=True, stop=False,
                             skip_group_check=True)

            def work(st):
                if st.has(2):
                    n, s = st.n(2), st.slot(2)
                    pe.wait_ge(xn_ready, n + 1)
                    after(pe, t_copied, n - 1)
                    for c in range(KD):
                        t = nc.tensor.transpose(p_t[s][:, c * P:(c + 1) * P], xn[:, s, c * P:(c + 1) * P],
                                                k.const("ident"))
                    t.then_inc(t_ready, 1)
                if st.has(3):
                    n, s = st.n(3), st.slot(3)
                    o = p_lg[:, bass.ds(n * E, E)]
                    pe.wait_ge(t_copied, n + 1)
                    pe.nop(nofuse=True)
                    xt = halves(xn_t[:, s, :])
                    for i in range(KD):
                        t = nc.tensor.matmul(o, xt[:, i, :], wg[:, i, :], start=False, stop=i == KD - 1,
                                             skip_group_check=True)
                    t.then_inc(logits_ready, 1)

            pipeline(pe, N, 3, work)
            pe.wait_ge(chosen_ready, 1)
            nc.tensor.matmul(p_rank[:, 0:(N + 1) * E], k.const16("upper"), chosen16[:].rearrange("p n e -> p (n e)"),
                             start=True, stop=False, skip_group_check=True)
            for n in range(N):
                later = N - n
                t = nc.tensor.matmul(p_rank[:, (n + 1) * E:(N + 1) * E].rearrange("p (n e) -> p n e", e=E),
                                     k.const16("ones"), chosen16[:, n:n + 1, :].to_broadcast([P, later, E]),
                                     start=False, stop=n == N - 1, skip_group_check=True)
            t.then_inc(rank_ready, 1)


def experts(k):
    nc, w = k.nc, k.w
    with ExitStack() as ctx:
        def sb(name, shape, dt=F32):
            return ctx.enter_context(nc.sbuf_tensor("e_" + name, shape, dt))

        sem = ctx.enter_context(semaphores(nc, "e_"))

        def ps(name, cols=512):
            return ctx.enter_context(nc.psum_tensor("e_" + name, [P, cols], F32))

        HC = F // P
        xs, xs_t = sb("xs", [P, 2, D]), sb("xs_t", [P, KD, P])
        w1_now = sb("w1_now", [P, 2, KD, F])
        hidden_t = sb("hidden_t", [P, HC, P])
        y = sb("y", [P, 2, D])
        p_in, p_h, p_y = ps("p_in"), ps("p_h", F), ps("p_y")
        loaded = [sem("loaded0"), sem("loaded1")]
        in_ready, in_copied, w1_ready, h_ready, relu_ready = (
            sem("in_ready"), sem("in_copied"), sem("w1_ready"), sem("h_ready"), sem("relu_ready"))
        y_ready, y_copied = sem("y_ready"), sem("y_copied")
        stored = [sem("stored0"), sem("stored1")]
        block = ctx.enter_context(nc.Block())

        @block.sync
        def _(sp):
            def work(st):
                if st.has(0):
                    n, s = st.n(0), st.slot(0)
                    after(sp, in_ready, n - 1)
                    sp.dma_start(xs[:, s, :], k.slots_in[bass.ds(n * P, P), :]).then_inc(loaded[s], 16)

            pipeline(sp, ROUTED, 1, work)
            for i in range(3):
                sp.dma_start(k.wa[:, i], w["qkv1"][:, i * D:(i + 1) * D].rearrange("(c p) n -> p c n", p=P)).then_inc(
                    k.loaded["wa1"], 16)
            sp.dma_start(k.wa[:, 3], w["out1"].rearrange("(c p) n -> p c n", p=P)).then_inc(k.loaded["wa1"], 16)

        @block.gpsimd
        def _(pool):
            def work(st):
                if st.has(1):
                    n, s = st.n(1), st.slot(1)
                    pool.wait_ge(y_copied, n + 1)
                    pool.nop(nofuse=True)
                    pool.dma_start(k.slots_out[bass.ds(n * P, P), :], y[:, s, :]).then_inc(stored[s], 16)

            pipeline(pool, ROUTED, 1, work)
            pool.wait_ge(stored[0], 16 * ((ROUTED + 1) // 2))
            pool.wait_ge(stored[1], 16 * (ROUTED // 2))

        @block.scalar
        def _(act):
            def work(st):
                if st.has(0):
                    n = st.n(0)
                    act.wait_ge(in_ready, n + 1)
                    after(act, h_ready, 2 * n)
                    nc.scalar.copy(xs_t[:], halves(p_in[:, 0:D])).then_inc(in_copied, 1)
                    for c in range(2):
                        act.wait_ge(h_ready, 2 * n + c + 1)
                        after(act, y_ready, n)
                        nc.scalar.activation(hidden_t[:, 4 * c:4 * c + 4, :], halves(p_h[:, c * 512:(c + 1) * 512]),
                                             ACT.Relu).then_inc(relu_ready, 1)

            pipeline(act, ROUTED, 1, work)

        @block.vector
        def _(dve):
            dve.wait_ge(k.loaded["ffn"], 16 * 2 * E)

            def work(st):
                if st.has(0):
                    n, s = st.n(0), st.slot(0)
                    e = dve.value_load(k.tile_expert[0:1, bass.ds(n, 1)], min_val=0, max_val=E - 1)
                    after(dve, h_ready, 2 * (n - 1))
                    dve.nop(nofuse=True)
                    nc.vector.tensor_copy(w1_now[:, s], k.w1[:, bass.ds(e, 1)].rearrange("p a c f -> p (a c) f")
                                          ).then_inc(w1_ready, 1)
                if st.has(2):
                    n, s = st.n(2), st.slot(2)
                    dve.wait_ge(y_ready, n + 1)
                    after(dve, stored[s], 16 * st.use(2))
                    nc.vector.tensor_copy(y[:, s, :], p_y[:, 0:D]).then_inc(y_copied, 1)

            pipeline(dve, ROUTED, 2, work)

        @block.tensor
        def _(pe):
            pe.wait_ge(k.loaded["ffn"], 16 * 2 * E)

            def expert_of(n):
                e = pe.value_load(k.tile_expert[0:1, bass.ds(n, 1)], min_val=0, max_val=E - 1)
                return e, k.const16("select")[:, bass.ds(e * P, P)]

            def work(st):
                if st.has(0):
                    n, s = st.n(0), st.slot(0)
                    pe.wait_ge(loaded[s], 16 * (st.use(0) + 1))
                    after(pe, in_copied, n)
                    for c in range(KD):
                        t = nc.tensor.transpose(p_in[:, c * P:(c + 1) * P], xs[:, s, c * P:(c + 1) * P],
                                                k.const("ident"))
                    t.then_inc(in_ready, 1)
                if st.has(1):
                    n = st.n(1)
                    e, select = expert_of(n)
                    after(pe, y_copied, n)
                    pe.nop(nofuse=True)
                    nc.tensor.matmul(p_y[:, 0:D], select, k.expert_bias[:, F:F + D], start=True, stop=False)
                    for j in range(HC):
                        if j in (0, HC // 2):
                            hold(pe, relu_ready, 2 * n + 1 + (j > 0))
                        t = nc.tensor.matmul(p_y[:, 0:D], hidden_t[:, j, :], k.w2[:, bass.ds(e, 1), j, :].rearrange(
                            "p a n -> p (a n)"), start=False, stop=j == HC - 1)
                    t.then_inc(y_ready, 1)
                if st.has(0):
                    n, s = st.n(0), st.slot(0)
                    e, select = expert_of(n)
                    pe.wait_ge(w1_ready, n + 1)
                    pe.wait_ge(in_copied, n + 1)
                    after(pe, relu_ready, 2 * n)
                    pe.nop(nofuse=True)
                    for j in range(HC):
                        o = p_h[:, j * P:(j + 1) * P]
                        nc.tensor.matmul(o, k.expert_bias[:, j * P:(j + 1) * P], select, start=True, stop=False)
                        for i in range(KD):
                            t = nc.tensor.matmul(o, w1_now[:, s, i, j * P:(j + 1) * P], xs_t[:, i, :], start=False,
                                                 stop=i == KD - 1)
                        if j % (HC // 2) == HC // 2 - 1:
                            t.then_inc(h_ready, 1)

            pipeline(pe, ROUTED, 1, work)


def perceiver(k):
    nc, w = k.nc, k.w
    with ExitStack() as ctx:
        def sb(name, shape, dt=F32):
            return ctx.enter_context(nc.sbuf_tensor("p_" + name, shape, dt))

        sem = ctx.enter_context(semaphores(nc, "p_"))

        def ps(name):
            return ctx.enter_context(nc.psum_tensor("p_" + name, [P, 512], F32))

        C1 = C - P
        wq, wl, wc, wo = k.wq, k.wl, k.wc, k.wo
        mask_u8, allowed = sb("mask_u8", [1, N * S], U8), sb("allowed", [P, N, S], BF16)
        token = sb("token", [P, 2, C])
        stats, mv = sb("stats", [P, 2, 6]), sb("mv", [P, 2, 2])
        rstd = sb("rstd", [P, 2])
        xn, cn = sb("xn", [P, D]), sb("cn", [P, C])
        in_t = sb("in_t", [P, 4, P])
        square = sb("square", [P, 3 * XH, XD])
        norm = sb("norm", [P, 3 * XH])
        qk = sb("qk", [P, 3 * XH, XD])
        v1 = sb("v1", [P, 2, 2, XH, P])
        q_t, k_t = sb("q_t", [P, 2, 2, P]), sb("k_t", [P, 2, 2, P])
        smax, prob, prob_t = sb("smax", [P, 2, 2]), sb("prob", [P, 2, 512]), sb("prob_t", [P, 2, 512])
        pv_t = sb("pv_t", [P, 512])
        rsum, att, att_t = sb("rsum", [P, XH]), sb("att", [P, D]), sb("att_t", [P, KD, P])
        p_in, p_q, p_l, p_c, p_k, p_pv = ps("p_in"), ps("p_q"), ps("p_l"), ps("p_c"), ps("p_k"), ps("p_pv")
        p_s = [ps("p_s0"), ps("p_s1")]

        mask_loaded, allowed_zero, allowed_ready, one_set = (
            sem("mask_loaded"), sem("allowed_zero"), sem("allowed_ready"), sem("one_set"))
        token_loaded = [sem("token0"), sem("token1")]
        ln, mv_ready, root_steps, xn_ready = sem("ln"), sem("mv_ready"), sem("root_steps"), sem("xn_ready")
        in_ready, in_copied, proj_ready, sq_ready, v_copied = (
            sem("in_ready"), sem("in_copied"), sem("proj_ready"), sem("sq_ready"), sem("v_copied"))
        pvt_copied, turned_back, pad_zero = sem("pvt_copied"), sem("turned_back"), sem("pad_zero")
        ss_ready, norm_steps, rnorm_ready, qk_ready = sem("ss_ready"), sem("norm_steps"), sem("rnorm_ready"), sem("qk_ready")
        qkt_ready, qkt_copied, s_ready, max_ready, sub_ready, exp_ready = (
            sem("qkt_ready"), sem("qkt_copied"), sem("s_ready"), sem("max_ready"), sem("sub_ready"), sem("exp_ready"))
        pt_ready, pt_copied, pv_ready, rsum_ready, att_ready = (
            sem("pt_ready"), sem("pt_copied"), sem("pv_ready"), sem("rsum_ready"), sem("att_ready"))
        att_t_ready, att_t_copied, o_ready, x_ready = (
            sem("att_t_ready"), sem("att_t_copied"), sem("o_ready"), sem("x_ready"))
        block = ctx.enter_context(nc.Block())

        @block.sync
        def _(sp):
            for slot in range(2):
                sp.dma_start(token[:, slot, :], k.ctx_tok[slot]).then_inc(token_loaded[slot], 16)
            sp.dma_start(mask_u8[:], k.mask.rearrange("(a n) s -> a (n s)", a=1)).then_inc(mask_loaded, 16)
            with sp.Fori(1, N // 2) as pair:
                for slot in range(2):
                    sp.wait_ge(xn_ready, 2 * pair + slot - 1)
                    sp.dma_start(token[:, slot, :], k.ctx_tok[bass.ds(2 * pair + slot, 1)].rearrange(
                        "a s c -> (a s) c")).then_inc(token_loaded[slot], 16)

        @block.gpsimd
        def _(pool):
            nc.gpsimd.memset(in_t[C1:P, 3, :], 0.0).then_inc(pad_zero, 1)
            pool.wait_ge(pad_zero, 1)

            def work(st):
                if st.starts(1):
                    nc.gpsimd.memset(v1[:], 1.0).then_inc(one_set, 1)
                    nc.gpsimd.memset(allowed[:], 0.0).then_inc(allowed_zero, 1)
                if st.has(0):
                    n = st.n(0)
                    hold(pool, mv_ready, n + 1)
                    twice_normalised(k, rstd[:, 0:1], mv[:, 0, 1:2]).then_inc(root_steps, 1)
                    hold(pool, root_steps, 3 * n + 1)
                    nc.gpsimd.tensor_scalar(rstd[:, 1:2], mv[:, 1, 1:2], EPS, 1.0, ALU.add, ALU.mult).then_inc(
                        root_steps, 1)
                    pool.wait_ge(root_steps, 3 * n + 2)
                    nc.gpsimd.tensor_tensor(rstd[:], rstd[:], k.const("power")[:, 0:2], ALU.pow).then_inc(root_steps, 1)
                if st.has(1):
                    n = st.n(1)
                    pool.wait_ge(ss_ready, n + 1)
                    nc.gpsimd.tensor_tensor(norm[:], norm[:], k.const("root"), ALU.pow).then_inc(norm_steps, 1)

            pipeline(pool, N, 4, work)

        @block.scalar
        def _(act):
            def work(st):
                def exponential(i):
                    act.wait_ge(sub_ready, 2 * st.n(3) + i + 1)
                    nc.scalar.activation(prob[:, i, :], prob[:, i, :], ACT.Exp, scale=XD ** -0.5).then_inc(
                        exp_ready, 1)

                def square_of(i, src):
                    nc.scalar.activation(square[:, i * XH:(i + 1) * XH, :],
                                         src[:, 0:D].rearrange("p (h c) -> p h c", c=XD), ACT.Square).then_inc(
                        sq_ready, 1)

                if st.has(2):
                    n, s = st.n(2), st.slot(2)
                    if st.starts(2):
                        act.wait_ge(one_set, 1)
                    after(act, pv_ready, n - 1)
                    for i, src in enumerate((p_c, p_l)):
                        t = nc.scalar.copy(v1[:, s, i, :, 0:XD], src[:, D:2 * D].rearrange("p (h c) -> p h c", c=XD))
                    t.then_inc(v_copied, 1)
                if st.has(4):
                    n = st.n(4)
                    act.wait_ge(pv_ready, n + 1)
                    after(act, turned_back, n)
                    nc.scalar.copy(pv_t[:], p_pv[:]).then_inc(pvt_copied, 1)
                if st.has(1):
                    n = st.n(1)
                    act.wait_ge(in_ready, n + 1)
                    after(act, proj_ready, 3 * n)
                    for i, (gain, shift, j, rows) in enumerate((("lg", "lb", 0, P), ("lg", "lb", 1, P),
                                                                ("xg", "xb", 0, P), ("xg", "xb", 1, C1))):
                        t = nc.scalar.activation(in_t[0:rows, i, :], p_in[0:rows, i * P:(i + 1) * P], ACT.Identity,
                                                 bias=k.col(shift, j, rows), scale=k.col(gain, j, rows))
                        if j == 1:
                            t.then_inc(in_copied, 1)
                if st.has(2):
                    n = st.n(2)
                    act.wait_ge(qkt_ready, n + 1)
                    after(act, s_ready, 2 * n)
                    for i, gain in enumerate(("qn0", "qn1")):
                        nc.scalar.activation(q_t[:, i], halves(p_q[:, D:2 * D]), ACT.Copy, scale=k.col(gain))
                    nc.scalar.activation(k_t[:].rearrange("p a b c -> p (a b) c"), halves(p_k[:]), ACT.Copy,
                                         scale=k.col("kn")).then_inc(qkt_copied, 1)
                if st.has(3):
                    exponential(0)
                    exponential(1)
                if st.has(1):
                    n = st.n(1)
                    act.wait_ge(proj_ready, 3 * n + 2)
                    after(act, ss_ready, n)
                    square_of(0, p_q)
                    square_of(1, p_l)
                    act.wait_ge(proj_ready, 3 * n + 3)
                    square_of(2, p_c)
                if st.has(4):
                    n = st.n(4)
                    act.wait_ge(att_t_ready, n + 1)
                    after(act, o_ready, n)
                    nc.scalar.copy(att_t[:], halves(p_k[:, 0:D])).then_inc(att_t_copied, 1)
                if st.has(3):
                    n = st.n(3)
                    for i in range(2):
                        act.wait_ge(pt_ready, 2 * n + i + 1)
                        after(act, pv_ready, n)
                        nc.scalar.copy(prob_t[:, i, :], p_s[i][:]).then_inc(pt_copied, 1)

            pipeline(act, N, 4, work)

        @block.vector
        def _(dve):
            def work(st):
                def shift(i):
                    n, sc = st.n(3), p_s[i][:].rearrange("p (a b) -> p a b", b=2 * P)
                    dve.wait_ge(s_ready, 2 * n + i + 1)
                    nc.vector.tensor_reduce(smax[:, i, :], sc, AX.X, ALU.max).then_inc(max_ready, 1)
                    dve.wait_ge(max_ready, 2 * n + i + 1)
                    after(dve, pt_ready, 2 * (n - 1) + i + 1)
                    nc.vector.tensor_tensor(prob[:, i, :].rearrange("p (a b) -> p a b", b=2 * P), sc,
                                            smax[:, i, :].unsqueeze(2).to_broadcast([P, 2, 2 * P]),
                                            ALU.subtract).then_inc(sub_ready, 1)

                if st.starts(2):
                    dve.wait_ge(mask_loaded, 16)
                    dve.wait_ge(allowed_zero, 1)
                    nc.vector.tensor_scalar(allowed[0:1].rearrange("p n s -> p (n s)"), mask_u8[:], -1.0, -FAR,
                                            ALU.add, ALU.mult).then_inc(allowed_ready, 1)
                if st.has(0):
                    n, s = st.n(0), st.slot(0)
                    nc.vector.bn_stats(stats[:, 0, :], row(k.x, n))
                    dve.wait_ge(token_loaded[s], 16 * (st.use(0) + 1))
                    nc.vector.bn_stats(stats[:, 1, :], token[:, s, :]).then_inc(ln, 1)
                    after(dve, xn_ready, n)
                    hold(dve, ln, n + 1)
                    nc.vector.bn_aggr(mv[:, 0, :], stats[:, 0, :])
                    nc.vector.bn_aggr(mv[:, 1, :], stats[:, 1, :]).then_inc(mv_ready, 1)
                if st.has(2):
                    n = st.n(2)
                    dve.wait_ge(norm_steps, n + 1)
                    nc.vector.tensor_scalar(norm[:], norm[:], XD ** -0.5, 1e-8, ALU.mult, ALU.max).then_inc(
                        rnorm_ready, 1)
                    dve.wait_ge(rnorm_ready, 2 * n + 1)
                    nc.vector.reciprocal(norm[:], norm[:]).then_inc(rnorm_ready, 1)
                    dve.wait_ge(rnorm_ready, 2 * n + 2)
                    dve.wait_ge(v_copied, n + 1)
                    after(dve, qkt_ready, n)
                    for i, src in enumerate((p_q, p_l, p_c)):
                        t = nc.vector.tensor_tensor(
                            qk[:, i * XH:(i + 1) * XH, :], src[:, 0:D].rearrange("p (h c) -> p h c", c=XD),
                            norm[:, i * XH:(i + 1) * XH].unsqueeze(2).to_broadcast([P, XH, XD]), ALU.mult)
                    t.then_inc(qk_ready, 1)
                if st.has(3):
                    shift(0)
                    shift(1)
                if st.has(4):
                    n = st.n(4)
                    pv = p_pv[:].rearrange("p (h c) -> p h c", c=P)
                    dve.wait_ge(turned_back, n + 1)
                    nc.vector.reciprocal(rsum[:], pv[:, :, XD]).then_inc(rsum_ready, 1)
                    dve.wait_ge(rsum_ready, n + 1)
                    after(dve, att_t_ready, n)
                    nc.vector.tensor_tensor(att[:].rearrange("p (h c) -> p h c", c=XD), pv[:, :, 0:XD],
                                            rsum[:].unsqueeze(2).to_broadcast([P, XH, XD]), ALU.mult).then_inc(
                        att_ready, 1)
                if st.has(0):
                    n, s = st.n(0), st.slot(0)
                    dve.wait_ge(root_steps, 3 * n + 3)
                    after(dve, in_ready, n)
                    nc.vector.tensor_scalar(xn[:], row(k.x, n), mv[:, 0, 0:1], rstd[:, 0:1], ALU.subtract, ALU.mult)
                    nc.vector.tensor_scalar(cn[:], token[:, s, :], mv[:, 1, 0:1], rstd[:, 1:2], ALU.subtract,
                                            ALU.mult).then_inc(xn_ready, 1)
                if st.has(5):
                    n = st.n(5)
                    hold(dve, x_ready, n + 1)
                    nc.vector.bn_stats(row(k.stats, n), row(k.x, n))
                if st.has(1):
                    n = st.n(1)
                    dve.wait_ge(sq_ready, 3 * n + 3)
                    nc.vector.tensor_reduce(norm[:], square[:], AX.X, ALU.add).then_inc(ss_ready, 1)
                if st.has(4):
                    n = st.n(4)
                    dve.wait_ge(o_ready, n + 1)
                    nc.vector.tensor_tensor(row(k.x, n), p_k[:, D:2 * D], row(k.x, n), ALU.add).then_inc(x_ready, 1)

            pipeline(dve, N, 5, work)

        @block.tensor
        def _(pe):
            pe.wait_ge(k.loaded["wp"], 16 * 5)
            pe.wait_ge(pad_zero, 1)
            ident = k.const("ident")

            def work(st):
                def project(o, chunks, weights):
                    for i in range(KD):
                        t = nc.tensor.matmul(o, in_t[:, chunks + i, :], weights[:, i, :], start=i == 0,
                                             stop=i == KD - 1)
                    t.then_inc(proj_ready, 1)

                if st.has(3):
                    n = st.n(3)
                    if st.starts(3):
                        pe.wait_ge(allowed_ready, 1)
                    pe.wait_ge(qkt_copied, n + 1)
                    after(pe, pt_copied, 2 * n)
                    pe.nop(nofuse=True)
                    for i in range(2):
                        sc = p_s[i][:].rearrange("p (m b) -> p m b", b=2 * P)
                        nc.tensor.matmul(sc[:, :, 0:P], k.const16("ones"), allowed[:, bass.ds(n, 1), :].to_broadcast(
                            [P, 2, P]), start=True, stop=False, skip_group_check=True)
                        for m in range(2):
                            t = nc.tensor.matmul(sc[:, m, :], q_t[:, i, m, :],
                                                 k_t[:, m].rearrange("p a b -> p (a b)"), start=False, stop=m == 1,
                                                 skip_group_check=True)
                        t.then_inc(s_ready, 1)
                if st.has(1):
                    n = st.n(1)
                    pe.wait_ge(xn_ready, n + 1)
                    after(pe, in_copied, 2 * n)
                    nc.tensor.transpose(p_in[:, 0:P], xn[:, 0:P], ident)
                    nc.tensor.transpose(p_in[:, P:2 * P], xn[:, P:D], ident)
                    nc.tensor.transpose(p_in[:, 2 * P:3 * P], cn[:, 0:P], ident)
                    nc.tensor.transpose(p_in[0:C1, 3 * P:4 * P], cn[:, P:C], ident).then_inc(in_ready, 1)
                if st.has(4):
                    n = st.n(4)
                    pe.wait_ge(pvt_copied, n + 1)
                    for c in range(4):
                        t = nc.tensor.transpose(p_pv[:, c * P:(c + 1) * P], pv_t[:, c * P:(c + 1) * P], ident)
                    t.then_inc(turned_back, 1)
                if st.has(2):
                    n = st.n(2)
                    pe.wait_ge(qk_ready, n + 1)
                    after(pe, qkt_copied, n)
                    after(pe, x_ready, n - 2)
                    flat = qk[:].rearrange("p h c -> p (h c)")
                    for m in range(2):
                        nc.tensor.transpose(p_q[:, D + m * P:D + (m + 1) * P], flat[:, m * P:(m + 1) * P], ident)
                        for i, src in enumerate((2, 1)):
                            t = nc.tensor.transpose(p_k[:, (2 * m + i) * P:(2 * m + i + 1) * P],
                                                    flat[:, src * D + m * P:src * D + (m + 1) * P], ident)
                    t.then_inc(qkt_ready, 1)
                if st.has(1):
                    n = st.n(1)
                    pe.wait_ge(in_copied, 2 * n + 1)
                    after(pe, qk_ready, n)
                    project(p_l[:], 0, wl)
                    after(pe, qkt_copied, n)
                    project(p_q[:, 0:D], 0, wq)
                    pe.wait_ge(in_copied, 2 * n + 2)
                    project(p_c[:], 2, wc)
                if st.has(4):
                    n = st.n(4)
                    pe.wait_ge(att_ready, n + 1)
                    if st.has(2):
                        pe.wait_ge(qkt_copied, n + 3)
                    for c in range(KD):
                        t = nc.tensor.transpose(p_k[:, c * P:(c + 1) * P], att[:, c * P:(c + 1) * P], ident)
                    t.then_inc(att_t_ready, 1)
                if st.has(3):
                    n = st.n(3)
                    for i in range(2):
                        pe.wait_ge(exp_ready, 2 * n + i + 1)
                        for j in range(4):
                            t = nc.tensor.transpose(p_s[i][:, j * P:(j + 1) * P], prob[:, i, j * P:(j + 1) * P],
                                                    ident)
                        t.then_inc(pt_ready, 1)
                if st.has(4):
                    n = st.n(4)
                    pe.wait_ge(att_t_copied, n + 1)
                    o = p_k[:, D:2 * D]
                    nc.tensor.matmul(o, k.ones, k.bias_row("po"), start=True, stop=False)
                    for i in range(KD):
                        t = nc.tensor.matmul(o, att_t[:, i, :], wo[:, i, :], start=False, stop=i == KD - 1)
                    t.then_inc(o_ready, 1)
                if st.has(3):
                    n, s = st.n(3), st.slot(3)
                    after(pe, att_ready, n)
                    for i in range(2):
                        pe.wait_ge(pt_copied, 2 * n + i + 1)
                        for m in range(2):
                            h = 2 * m + i
                            for c in range(2):
                                t = nc.tensor.matmul(p_pv[:, h * P:(h + 1) * P], v1[:, s, c, h, :],
                                                     prob_t[:, i, (2 * m + c) * P:(2 * m + c + 1) * P],
                                                     start=c == 0, stop=c == 1)
                    t.then_inc(pv_ready, 1)

            pipeline(pe, N, 4, work)


def sentence_experts(k):
    nc, w = k.nc, k.w
    with ExitStack() as ctx:
        def sb(name, shape, dt=F32):
            return ctx.enter_context(nc.sbuf_tensor("s_" + name, shape, dt))

        sem = ctx.enter_context(semaphores(nc, "s_"))

        def ps(name):
            return ctx.enter_context(nc.psum_tensor("s_" + name, [P, 512], F32))

        wr, down, up = k.wr, k.down, k.up
        bn_gain, bn_shift = sb("bn_gain", [P, KD]), sb("bn_shift", [P, KD])
        mv = sb("mv", [P, N, 2])
        rstd = sb("rstd", [P, N])
        z, z_t = sb("z", [P, 2, D]), sb("z_t", [P, N, KD, P])
        z_sum, z_bn = sb("z_sum", [P, KD, N]), sb("z_bn", [P, KD, P])
        best, score, shifted, total = sb("best", [P, 1]), sb("score", [P, E]), sb("shifted", [P, E]), sb("total", [P, 1])
        gate_expert, spread = sb("gate_expert", [P, 2]), sb("spread", [P, 2, P])
        gate, expert_i = sb("gate", [P, N]), sb("expert_i", [P, N], I32)
        hidden, hidden_t = sb("hidden", [P, 2, F1]), sb("hidden_t", [P, 2, P])
        z_now, result = sb("z_now", [P, 2, KD, P]), sb("result", [P, 2, D])
        p_in, p_h, p_y = [ps("p_in0"), ps("p_in1")], [ps("p_h0"), ps("p_h1")], [ps("p_y0"), ps("p_y1")]
        p_r, p_ht = ps("p_r"), ps("p_ht")
        bn_root, bn_steps, zero_set = sem("bn_root"), sem("bn_steps"), sem("zero_set")
        mv_ready, root_steps, z_ready = sem("mv_ready"), sem("root_steps"), sem("z_ready")
        in_ready, in_copied, bn_ready, logits_ready = sem("in_ready"), sem("in_copied"), sem("bn_ready"), sem("logits_ready")
        choice, exp_ready, chosen, spread_ready, expert_ready = (
            sem("choice"), sem("exp_ready"), sem("chosen"), sem("spread_ready"), sem("expert_ready"))
        h_ready, relu_ready, ht_ready, ht_copied, y_ready = (
            sem("h_ready"), sem("relu_ready"), sem("ht_ready"), sem("ht_copied"), sem("y_ready"))
        z_placed, out_ready, stored = sem("z_placed"), sem("out_ready"), [sem("stored0"), sem("stored1")]
        block = ctx.enter_context(nc.Block())

        @block.sync
        def _(sp):
            with sp.Fori(0, N // 2) as pair:
                for slot in range(2):
                    n = 2 * pair + slot
                    sp.wait_ge(out_ready, n + 1)
                    sp.dma_start(k.out[bass.ds(n, 1)].rearrange("a s d -> (a s) d"), result[:, slot, :]).then_inc(
                        stored[slot], 16)
            sp.wait_ge(stored[0], 16 * (N // 2))
            sp.wait_ge(stored[1], 16 * (N // 2))

        @block.gpsimd
        def _(pool):
            inverse_root(k, pool, bn_gain[:], k.cols[:, COLS["bnv"][0]:COLS["bnv"][0] + 2], bn_root, 0)
            pool.wait_ge(bn_root, 2)
            zeroed = Steps(pool, zero_set)
            zeroed.then(nc.gpsimd.memset(z_bn[:], 0.0))
            zeroed.then(nc.gpsimd.memset(hidden_t[F1:P], 0.0))
            pool.wait_ge(mv_ready, N)
            twice_normalised(k, rstd[:], mv[:, :, 1]).then_inc(root_steps, 1)
            pool.wait_ge(root_steps, 1)
            nc.gpsimd.tensor_tensor(rstd[:], rstd[:], k.const("power"), ALU.pow).then_inc(root_steps, 1)

        @block.scalar
        def _(act):
            def turned(st):
                if st.has(0):
                    n, s = st.n(0), st.slot(0)
                    act.wait_ge(in_ready, n + 1)
                    for i in range(KD):
                        t = nc.scalar.activation(z_t[:, bass.ds(n, 1), i, :].rearrange("p a d -> p (a d)"),
                                                 p_in[s][:, i * P:(i + 1) * P], ACT.Identity, bias=k.col("fb", i),
                                                 scale=k.col("fg", i), accum_out=z_sum[:, i, bass.ds(n, 1)])
                    t.then_inc(in_copied, 1)

            pipeline(act, N, 0, turned)
            act.wait_ge(choice, 2)
            nc.scalar.activation(shifted[:], shifted[:], ACT.Exp, accum_out=total[:]).then_inc(exp_ready, 1)
            act.wait_ge(zero_set, 2)

            def work(st):
                if st.has(1):
                    n, s = st.n(1), st.slot(1)
                    act.wait_ge(ht_ready, n + 1)
                    after(act, y_ready, n - 1)
                    nc.scalar.copy(hidden_t[0:F1, s, :], p_ht[0:F1, 0:P]).then_inc(ht_copied, 1)
                if st.has(0):
                    n, s = st.n(0), st.slot(0)
                    act.wait_ge(h_ready, n + 1)
                    after(act, ht_ready, n - 1)
                    nc.scalar.activation(hidden[:, s, :], p_h[s][:, 0:F1], ACT.Relu).then_inc(relu_ready, 1)

            pipeline(act, N, 2, work)

        @block.vector
        def _(dve):
            for n in range(N):
                nc.vector.bn_aggr(mv[:, n, :], k.stats[:, n, :]).then_inc(mv_ready, 1)
            link = Steps(dve, bn_steps)
            col = lambda name: k.cols[:, COLS[name][0]:COLS[name][0] + 2]
            dve.wait_ge(bn_root, 2)
            link.then(nc.vector.tensor_tensor(bn_gain[:], bn_gain[:], col("bng"), ALU.mult))
            link.then(nc.vector.tensor_tensor(bn_shift[:], bn_gain[:], col("bnm"), ALU.mult))
            link.then(nc.vector.tensor_tensor(bn_shift[:], col("bnb"), bn_shift[:], ALU.subtract))
            link.then(nc.vector.tensor_scalar(bn_gain[:], bn_gain[:], 1.0 / S, None, ALU.mult))
            dve.wait_ge(root_steps, 2)

            def normalised(st):
                if st.has(0):
                    n, s = st.n(0), st.slot(0)
                    after(dve, in_ready, n - 1)
                    nc.vector.tensor_scalar(z[:, s, :], row(k.x, n), mv[:, bass.ds(n, 1), 0], rstd[:, bass.ds(n, 1)],
                                            ALU.subtract, ALU.mult).then_inc(z_ready, 1)

            pipeline(dve, N, 0, normalised)
            dve.wait_ge(in_copied, N)
            dve.wait_ge(zero_set, 1)
            by_batch = [P, KD, N]
            link.then(nc.vector.tensor_tensor(z_sum[:], z_sum[:], bn_gain[:].unsqueeze(2).to_broadcast(by_batch),
                                              ALU.mult))
            nc.vector.tensor_tensor(z_bn[:, :, 0:N], z_sum[:], bn_shift[:].unsqueeze(2).to_broadcast(by_batch),
                                    ALU.add).then_inc(bn_ready, 1)
            dve.wait_ge(logits_ready, 1)
            nc.vector.tensor_reduce(best[:], p_r[:, 0:E], AX.X, ALU.max).then_inc(choice, 1)
            dve.wait_ge(choice, 1)
            nc.vector.tensor_scalar(shifted[:], p_r[:, 0:E], best[:, 0:1], None, ALU.subtract).then_inc(choice, 1)
            nc.vector.scalar_tensor_tensor(out=score[:], in0=p_r[:, 0:E], scalar=best[:, 0:1],
                                           in1=k.const("backward"), op0=ALU.is_ge, op1=ALU.mult).then_inc(choice, 1)
            dve.wait_ge(choice, 3)
            nc.vector.tensor_reduce(gate_expert[:, 1:2], score[:], AX.X, ALU.max).then_inc(choice, 1)
            dve.wait_ge(exp_ready, 1)
            nc.vector.reciprocal(gate_expert[:, 0:1], total[:]).then_inc(choice, 1)
            dve.wait_ge(choice, 5)
            nc.vector.tensor_copy(spread[:], gate_expert[:].unsqueeze(2).to_broadcast([P, 2, P])).then_inc(chosen, 1)
            dve.wait_ge(spread_ready, 1)
            nc.vector.tensor_copy(gate[:], p_r[:, 0:N]).then_inc(expert_ready, 1)
            nc.vector.tensor_scalar(expert_i[:], p_r[:, N:2 * N], -1.0, float(E), ALU.mult, ALU.add).then_inc(
                expert_ready, 1)
            dve.wait_ge(expert_ready, 2)

            def work(st):
                if st.has(0):
                    n, s = st.n(0), st.slot(0)
                    after(dve, h_ready, n - 1)
                    nc.vector.tensor_copy(z_now[:, s], z_t[:, bass.ds(n, 1)].rearrange("p a c d -> p (a c) d")
                                          ).then_inc(z_placed, 1)
                if st.has(3):
                    n, s = st.n(3), st.slot(3)
                    dve.wait_ge(y_ready, n + 1)
                    after(dve, stored[s], 16 * st.use(3))
                    nc.vector.scalar_tensor_tensor(out=result[:, s, :], in0=p_y[s][:, 0:D],
                                                   scalar=gate[:, bass.ds(n, 1)], in1=row(k.x, n), op0=ALU.mult,
                                                   op1=ALU.add).then_inc(out_ready, 1)

            pipeline(dve, N, 3, work)

        @block.tensor
        def _(pe):
            ident = k.const("ident")

            def turn(st):
                if st.has(0):
                    n, s = st.n(0), st.slot(0)
                    pe.wait_ge(z_ready, n + 1)
                    after(pe, in_copied, n - 1)
                    for c in range(KD):
                        t = nc.tensor.transpose(p_in[s][:, c * P:(c + 1) * P], z[:, s, c * P:(c + 1) * P], ident)
                    t.then_inc(in_ready, 1)

            pipeline(pe, N, 0, turn)
            pe.wait_ge(k.loaded["ws"], 48)
            nc.tensor.matmul(p_r[:, 0:E], k.ones, k.bias_row("route"), start=True, stop=False)
            pe.wait_ge(bn_ready, 1)
            for i in range(KD):
                t = nc.tensor.matmul(p_r[:, 0:E], z_bn[:, i, :], wr[:, i, :], start=False, stop=i == KD - 1)
            t.then_inc(logits_ready, 1)
            pe.wait_ge(chosen, 1)
            for i in range(2):
                t = nc.tensor.matmul(p_r[:, i * N:(i + 1) * N], spread[:, i, :], ident[:, 0:N], start=True, stop=True)
            t.then_inc(spread_ready, 1)
            pe.wait_ge(expert_ready, 2)
            pe.wait_ge(zero_set, 2)

            def expert_of(n):
                e = pe.value_load(expert_i[0:1, bass.ds(n, 1)], min_val=0, max_val=E - 1)
                return e, k.const16("select")[:, bass.ds(e * P, P)]

            def work(st):
                if st.has(0):
                    n, s = st.n(0), st.slot(0)
                    e, select = expert_of(n)
                    pe.wait_ge(z_placed, n + 1)
                    after(pe, relu_ready, n - 1)
                    pe.nop(nofuse=True)
                    nc.tensor.matmul(p_h[s][:, 0:F1], select, k.expert_bias[:, F + D:F + D + F1], start=True,
                                     stop=False)
                    for i in range(KD):
                        t = nc.tensor.matmul(p_h[s][:, 0:F1], z_now[:, s, i, :],
                                             down[:, bass.ds(e, 1), i, :].rearrange("p a n -> p (a n)"), start=False,
                                             stop=i == KD - 1)
                    t.then_inc(h_ready, 1)
                if st.has(2):
                    n, s = st.n(2), st.slot(2)
                    e, select = expert_of(n)
                    pe.wait_ge(ht_copied, n + 1)
                    after(pe, out_ready, n - 1)
                    pe.nop(nofuse=True)
                    nc.tensor.matmul(p_y[s][:, 0:D], select, k.expert_bias[:, F + D + F1:], start=True, stop=False)
                    nc.tensor.matmul(p_y[s][:, 0:D], hidden_t[:, s, :], up[:, bass.ds(e, 1), :].rearrange(
                        "p a n -> p (a n)"), start=False, stop=True).then_inc(y_ready, 1)
                if st.has(1):
                    n, s = st.n(1), st.slot(1)
                    after(pe, ht_copied, n)
                    hold(pe, relu_ready, n + 1)
                    nc.tensor.transpose(p_ht[0:F1, 0:P], hidden[:, s, :], ident).then_inc(ht_ready, 1)

            pipeline(pe, N, 2, work)


def lay_out(a):
    def c(x):
        return np.ascontiguousarray(x)

    l0, l1 = "L0_attn_", "L1_attn_"
    arrays = {
        "x_seq": c(np.transpose(a["x"], (1, 0, 2)).reshape(B * S, D)),
        "ctx": c(a["ctx_768"]),
        "mask": c(a["mask_BxS2_bk0"]),
        "w_q0": c(a[l0 + "Wq"].T),
        "w_kv0": c(np.concatenate([a[l0 + "Wk"], a[l0 + "Wv"]]).T),
        "w_v_gamma": c(a[l0 + "v_gamma"]), "w_v_beta": c(a[l0 + "v_beta"]),
        "w_xq": c(a["L0_xattn_Wq"]), "w_xk": c(a["L0_xattn_Wk"]), "w_xv": c(a["L0_xattn_Wv"]),
        "w_xo": c(a["L0_xattn_Wo"]),
        "w_gate": c(a["L0_ffn_gate_w"].T),
        "w_w1": c(np.transpose(a["L0_ffn_w1"], (0, 2, 1))), "w_w2": c(np.transpose(a["L0_ffn_w2"], (0, 2, 1))),
        "w_qkv1": c(a[l1 + "Wqkv"].T), "w_out1": c(a[l1 + "Wout"].T),
        "w_pq": c(a["L1_xattn_Wq"].T), "w_pc": c(a["L1_xattn_Wkv"].T), "w_pl": c(a["L1_xattn_Wlkv"].T),
        "w_po": c(a["L1_xattn_Wo"].T),
        "w_wr": c(a["L1_ffn_Wr"]), "w_down": c(a["L1_ffn_W_down"]), "w_up": c(a["L1_ffn_W_up"]),
    }
    bqkv = a[l1 + "bqkv"]
    rows = {"q0": a[l0 + "bq"], "k0": a[l0 + "bk"], "v0": a[l0 + "bv"], "xq": a["L0_xattn_bq"],
            "xk": a["L0_xattn_bk"], "xv": a["L0_xattn_bv"], "xo": a["L0_xattn_bo"], "gate": a["L0_ffn_gate_b"],
            "aq": bqkv[0:D], "ak": bqkv[D:2 * D], "av": bqkv[2 * D:], "ao": a[l1 + "bout"], "po": a["L1_xattn_bo"],
            "route": a["L1_ffn_br"]}
    bias = np.zeros(BIAS_N, np.float32)
    for name, (at, width) in BIAS_AT.items():
        bias[at:at + width] = rows[name]
    arrays["bias"] = bias.reshape(P, BIAS_G)
    arrays["expert_bias"] = c(np.concatenate([a["L0_ffn_b1"], a["L0_ffn_b2"], a["L1_ffn_b_down"],
                                              a["L1_ffn_b_up"]], 1))
    f, p = "L1_ffn_", "L1_xattn_"
    vectors = {"kg": a[l0 + "k_gamma"], "kb": a[l0 + "k_beta"], "xg": a[p + "ln_x_g"], "xb": a[p + "ln_x_b"],
               "lg": a[p + "ln_l_g"], "lb": a[p + "ln_l_b"],
               "qn0": np.concatenate([a[p + "qn_g"], np.zeros(XD, np.float32)]),
               "qn1": np.concatenate([np.zeros(XD, np.float32), a[p + "qn_g"]]),
               "kn": np.concatenate([a[p + "kn_g"]] * 2), "fg": a[f + "ln_g"], "fb": a[f + "ln_b"],
               "bng": a[f + "bn_g"], "bnb": a[f + "bn_b"], "bnm": a[f + "bn_mean"], "bnv": a[f + "bn_var"]}
    cols = np.zeros((COLS_N, P), np.float32)
    for name, (at, width) in COLS.items():
        v = vectors[name]
        cols[at:at + width].reshape(-1)[:v.size] = v
    arrays["cols"] = c(cols.T)
    return arrays


def kernel(**inputs):
    import concourse.bacc as bacc
    import ml_dtypes
    from concourse.bass_utils import run_bass_kernel_spmd

    arrays = lay_out({n: np.asarray(v) for n, v in inputs.items()})
    c32, c16 = constants()
    arrays["consts"], arrays["consts16"] = c32, c16.astype(ml_dtypes.bfloat16)
    nc = bacc.Bacc("TRN2", target_bir_lowering=False, num_devices=1)
    aps = {n: nc.dram_tensor("in_" + n, a.shape, mybir.dt.from_np(a.dtype), kind="ExternalInput").ap()
           for n, a in arrays.items()}
    out = nc.dram_tensor("out", (B, S, D), F32, kind="ExternalOutput").ap()
    w = {n[2:]: ap for n, ap in aps.items() if n.startswith("w_")}
    decoder(nc, aps["x_seq"], aps["ctx"], aps["mask"], w, aps["cols"], aps["bias"], aps["expert_bias"],
            aps["consts"], aps["consts16"], out)
    result = run_bass_kernel_spmd(nc, [{"in_" + n: a for n, a in arrays.items()}], core_ids=[0])
    return result.results[0]["out"]
```
